# Optimizing a Trainium2 kernel written in Bass

```python
import numpy as np
import jax
import jax.numpy as jnp

def _softmax(x, axis=-1):
    return jax.nn.softmax(x, axis=axis)

def _gelu(x):
    return jax.nn.gelu(x, approximate=True)

def _silu(x):
    return jax.nn.silu(x)

def _sigmoid(x):
    return jax.nn.sigmoid(x)

def _layernorm(x, axis=-1, eps=1e-05):
    m = jnp.mean(x, axis=axis, keepdims=True)
    v = jnp.var(x, axis=axis, keepdims=True)
    return (x - m) / jnp.sqrt(v + eps)

def _scatter_add(tgt, idx, src, axis=0):
    return tgt.at[idx].add(src)

def _segment_sum(src, seg, n):
    return jax.ops.segment_sum(src, seg, n)
kernel_name = 'mk_recurrent_d2_jaxref_r8_15afc6'

def setup_inputs(seed: int=0):
    np.random.seed(seed)
    _w = jnp.asarray

    def _L0_attn_setup():
        import jax, jax.numpy as jnp
        import numpy as np
        from jax import lax
        H = 64
        P = 64
        N = 128
        G = 8
        K = 4
        D_MODEL = 512
        I = H * P
        GN = G * N
        CONV_DIM = I + 2 * GN
        PROJ = I + CONV_DIM + H
        EPS = 1e-05
        GROUP_SIZE = I // G

        def _reference_tuple_inner(hidden_states, in_proj_w, conv_weight, conv_bias, dt_bias, A_log, D, norm_weight, out_proj_w):
            B, L, _ = hidden_states.shape
            proj = jnp.einsum('bld,pd->blp', hidden_states, in_proj_w)
            gate = proj[..., :I]
            hbc = proj[..., I:I + CONV_DIM]
            dt = proj[..., -H:]
            pad = jnp.pad(hbc, ((0, 0), (K - 1, 0), (0, 0)))
            conv = conv_bias
            for k in range(K):
                conv = conv + pad[:, k:k + L, :] * conv_weight[:, k]
            xBC = jax.nn.silu(conv)
            x = xBC[..., :I].reshape(B, L, H, P)
            Bm = xBC[..., I:I + GN].reshape(B, L, G, N)
            Cm = xBC[..., I + GN:].reshape(B, L, G, N)
            hpg = H // G
            B_h = jnp.repeat(Bm, hpg, axis=2)
            C_h = jnp.repeat(Cm, hpg, axis=2)
            dt_p = jax.nn.softplus(dt + dt_bias)
            A = -jnp.exp(A_log)
            dA = jnp.exp(dt_p * A)
            dtx = dt_p[..., None] * x

            def step(state, inp):
                dA_t, dtx_t, B_t, C_t = inp
                state = state * dA_t[..., None, None] + dtx_t[..., None] * B_t[:, :, None, :]
                y_t = jnp.einsum('bhpn,bhn->bhp', state, C_t)
                return (state, y_t)
            xs = (jnp.moveaxis(dA, 1, 0), jnp.moveaxis(dtx, 1, 0), jnp.moveaxis(B_h, 1, 0), jnp.moveaxis(C_h, 1, 0))
            state0 = jnp.zeros((B, H, P, N), jnp.float32)
            final_state, ys = lax.scan(step, state0, xs)
            y = jnp.moveaxis(ys, 0, 1) + x * D[None, None, :, None]
            y = y.reshape(B, L, I)
            yg = y.reshape(B, L, G, GROUP_SIZE)
            var = jnp.mean(yg * yg, axis=-1, keepdims=True)
            yn = (yg * lax.rsqrt(var + EPS)).reshape(B, L, I) * norm_weight
            yn = yn * jax.nn.silu(gate)
            out = jnp.einsum('bli,di->bld', yn, out_proj_w)
            conv_state_new = jnp.moveaxis(hbc[:, L - (K - 1):, :], 1, 2)
            return (out, conv_state_new, final_state)
        key = jax.random.key(seed)
        ks = jax.random.split(key, 6)
        B, L = (2, 256)
        s = 0.02
        return {'hidden_states': jax.random.normal(ks[0], (B, L, D_MODEL), jnp.float32), 'in_proj_w': jax.random.normal(ks[1], (PROJ, D_MODEL), jnp.float32) * s, 'conv_weight': jax.random.normal(ks[2], (CONV_DIM, K), jnp.float32) * s, 'conv_bias': jnp.zeros((CONV_DIM,), jnp.float32), 'dt_bias': jnp.ones((H,), jnp.float32), 'A_log': jnp.log(jnp.arange(1, H + 1, dtype=jnp.float32)), 'D': jnp.ones((H,), jnp.float32), 'norm_weight': jnp.ones((I,), jnp.float32), 'out_proj_w': jax.random.normal(ks[3], (D_MODEL, I), jnp.float32) * s}
    _L0_attn_in = _L0_attn_setup()

    def _L0_ffn_setup():
        import jax, jax.numpy as jnp
        import numpy as np
        HIDDEN = 512
        MOE_INTER = 128
        SHARED_INTER = 512
        NUM_EXPERTS = 16
        TOP_K = 2

        def _moe_forward(x, gate_w, w_gate_up, w_down, shared_w_gate_up, shared_w_down):
            orig_shape = x.shape
            x2 = x.reshape(-1, orig_shape[-1])
            gu_s = x2 @ shared_w_gate_up.T
            g_s, u_s = jnp.split(gu_s, 2, axis=-1)
            shared_out = jax.nn.silu(g_s) * u_s @ shared_w_down.T
            logits = x2 @ gate_w.T
            probs = jax.nn.softmax(logits, axis=-1)
            topk_vals, topk_idx = jax.lax.top_k(probs, TOP_K)
            topk_vals = topk_vals / jnp.sum(topk_vals, axis=-1, keepdims=True)
            combine = jnp.sum(jax.nn.one_hot(topk_idx, NUM_EXPERTS, dtype=x2.dtype) * topk_vals[..., None], axis=1)
            gu = jnp.einsum('th,eih->eti', x2, w_gate_up)
            g, u = jnp.split(gu, 2, axis=-1)
            act = jax.nn.silu(g) * u
            out_e = jnp.einsum('eti,ehi->eth', act, w_down)
            moe_out = jnp.einsum('eth,te->th', out_e, combine)
            return (moe_out + shared_out).reshape(orig_shape)
        key = jax.random.key(seed)
        ks = jax.random.split(key, 6)
        s = 0.02
        hidden_states = jax.random.normal(ks[0], (2, 256, HIDDEN), dtype=jnp.float32)
        gate_w = jax.random.normal(ks[1], (NUM_EXPERTS, HIDDEN), dtype=jnp.float32) * s
        w_gate_up = jax.random.normal(ks[2], (NUM_EXPERTS, 2 * MOE_INTER, HIDDEN), dtype=jnp.float32) * s
        w_down = jax.random.normal(ks[3], (NUM_EXPERTS, HIDDEN, MOE_INTER), dtype=jnp.float32) * s
        shared_w_gate_up = jax.random.normal(ks[4], (2 * SHARED_INTER, HIDDEN), dtype=jnp.float32) * s
        shared_w_down = jax.random.normal(ks[5], (HIDDEN, SHARED_INTER), dtype=jnp.float32) * s
        return {'hidden_states': hidden_states, 'gate_w': gate_w, 'w_gate_up': w_gate_up, 'w_down': w_down, 'shared_w_gate_up': shared_w_gate_up, 'shared_w_down': shared_w_down}
    _L0_ffn_in = _L0_ffn_setup()

    def _L1_attn_setup():
        import math
        import jax, jax.numpy as jnp
        import numpy as np

        def _rope_tables(T, h, dtype):
            pos = jnp.arange(T, dtype=jnp.float32)
            thetas = 1.0 / 10000.0 ** (jnp.arange(0, h, 2, dtype=jnp.float32) / h)
            pt = jnp.outer(pos, thetas)
            pt = jnp.concatenate([pt, pt], axis=-1)
            return (jnp.sin(pt).astype(dtype), jnp.cos(pt).astype(dtype))

        def _apply_rope(x, sin, cos):
            h = x.shape[-1]
            rot = jnp.concatenate([-x[..., h // 2:], x[..., :h // 2]], axis=-1)
            return x * cos + rot * sin
        key = jax.random.key(seed)
        ks = jax.random.split(key, 5)
        B, T, C = (2, 256, 512)
        s = 1.0 / math.sqrt(C)
        return {'x': jax.random.normal(ks[0], (B, T, C), dtype=jnp.float32), 'wq': jax.random.normal(ks[1], (C, C), dtype=jnp.float32) * s, 'wk': jax.random.normal(ks[2], (C, C), dtype=jnp.float32) * s, 'wv': jax.random.normal(ks[3], (C, C), dtype=jnp.float32) * s, 'wo': jax.random.normal(ks[4], (C, C), dtype=jnp.float32) * s}
    _L1_attn_in = _L1_attn_setup()

    def _L1_ffn_setup():
        import jax, jax.numpy as jnp
        import numpy as np
        BATCH, SEQ, D = (2, 256, 512)
        K, TOPK, RANK = (64, 16, 16)
        ALPHA = 32.0
        SCALING = ALPHA / RANK
        key = jax.random.key(seed)
        k1, k2, k3, k4 = jax.random.split(key, 4)
        x = jax.random.normal(k1, (BATCH, SEQ, D), dtype=jnp.float32)
        A = jax.random.normal(k2, (K, RANK, D), dtype=jnp.float32) * 0.02
        B = jax.random.normal(k3, (K, D, RANK), dtype=jnp.float32) * 0.02
        Wr = jax.random.normal(k4, (K, D), dtype=jnp.float32) * 0.02
        return {'x': x, 'A': A, 'B': B, 'Wr': Wr}
    _L1_ffn_in = _L1_ffn_setup()
    _d = {'L0_attn_hidden_states': _L0_attn_in['hidden_states'], 'L0_attn_in_proj_w': _L0_attn_in['in_proj_w'], 'L0_attn_conv_weight': _L0_attn_in['conv_weight'], 'L0_attn_conv_bias': _L0_attn_in['conv_bias'], 'L0_attn_dt_bias': _L0_attn_in['dt_bias'], 'L0_attn_A_log': _L0_attn_in['A_log'], 'L0_attn_D': _L0_attn_in['D'], 'L0_attn_norm_weight': _L0_attn_in['norm_weight'], 'L0_attn_out_proj_w': _L0_attn_in['out_proj_w'], 'L0_ffn_gate_w': _L0_ffn_in['gate_w'], 'L0_ffn_w_gate_up': _L0_ffn_in['w_gate_up'], 'L0_ffn_w_down': _L0_ffn_in['w_down'], 'L0_ffn_shared_w_gate_up': _L0_ffn_in['shared_w_gate_up'], 'L0_ffn_shared_w_down': _L0_ffn_in['shared_w_down'], 'L1_attn_wq': _L1_attn_in['wq'], 'L1_attn_wk': _L1_attn_in['wk'], 'L1_attn_wv': _L1_attn_in['wv'], 'L1_attn_wo': _L1_attn_in['wo'], 'L1_ffn_A': _L1_ffn_in['A'], 'L1_ffn_B': _L1_ffn_in['B'], 'L1_ffn_Wr': _L1_ffn_in['Wr']}
    _x0 = _d['L0_attn_hidden_states']
    _d['L0_attn_hidden_states'] = jax.random.normal(jax.random.fold_in(jax.random.key(seed), 1), (2, 512, 512), dtype=_x0.dtype)
    del _x0
    return _d

def reference(L0_attn_hidden_states, L0_attn_in_proj_w, L0_attn_conv_weight, L0_attn_conv_bias, L0_attn_dt_bias, L0_attn_A_log, L0_attn_D, L0_attn_norm_weight, L0_attn_out_proj_w, L0_ffn_gate_w, L0_ffn_w_gate_up, L0_ffn_w_down, L0_ffn_shared_w_gate_up, L0_ffn_shared_w_down, L1_attn_wq, L1_attn_wk, L1_attn_wv, L1_attn_wo, L1_ffn_A, L1_ffn_B, L1_ffn_Wr):

    def _L0_attn_ref(hidden_states, in_proj_w, conv_weight, conv_bias, dt_bias, A_log, D, norm_weight, out_proj_w):
        import jax, jax.numpy as jnp
        import numpy as np
        from jax import lax
        H = 64
        P = 64
        N = 128
        G = 8
        K = 4
        D_MODEL = 512
        I = H * P
        GN = G * N
        CONV_DIM = I + 2 * GN
        PROJ = I + CONV_DIM + H
        EPS = 1e-05
        GROUP_SIZE = I // G

        def _reference_tuple_inner(hidden_states, in_proj_w, conv_weight, conv_bias, dt_bias, A_log, D, norm_weight, out_proj_w):
            B, L, _ = hidden_states.shape
            proj = jnp.einsum('bld,pd->blp', hidden_states, in_proj_w)
            gate = proj[..., :I]
            hbc = proj[..., I:I + CONV_DIM]
            dt = proj[..., -H:]
            pad = jnp.pad(hbc, ((0, 0), (K - 1, 0), (0, 0)))
            conv = conv_bias
            for k in range(K):
                conv = conv + pad[:, k:k + L, :] * conv_weight[:, k]
            xBC = jax.nn.silu(conv)
            x = xBC[..., :I].reshape(B, L, H, P)
            Bm = xBC[..., I:I + GN].reshape(B, L, G, N)
            Cm = xBC[..., I + GN:].reshape(B, L, G, N)
            hpg = H // G
            B_h = jnp.repeat(Bm, hpg, axis=2)
            C_h = jnp.repeat(Cm, hpg, axis=2)
            dt_p = jax.nn.softplus(dt + dt_bias)
            A = -jnp.exp(A_log)
            dA = jnp.exp(dt_p * A)
            dtx = dt_p[..., None] * x

            def step(state, inp):
                dA_t, dtx_t, B_t, C_t = inp
                state = state * dA_t[..., None, None] + dtx_t[..., None] * B_t[:, :, None, :]
                y_t = jnp.einsum('bhpn,bhn->bhp', state, C_t)
                return (state, y_t)
            xs = (jnp.moveaxis(dA, 1, 0), jnp.moveaxis(dtx, 1, 0), jnp.moveaxis(B_h, 1, 0), jnp.moveaxis(C_h, 1, 0))
            state0 = jnp.zeros((B, H, P, N), jnp.float32)
            final_state, ys = lax.scan(step, state0, xs)
            y = jnp.moveaxis(ys, 0, 1) + x * D[None, None, :, None]
            y = y.reshape(B, L, I)
            yg = y.reshape(B, L, G, GROUP_SIZE)
            var = jnp.mean(yg * yg, axis=-1, keepdims=True)
            yn = (yg * lax.rsqrt(var + EPS)).reshape(B, L, I) * norm_weight
            yn = yn * jax.nn.silu(gate)
            out = jnp.einsum('bli,di->bld', yn, out_proj_w)
            conv_state_new = jnp.moveaxis(hbc[:, L - (K - 1):, :], 1, 2)
            return (out, conv_state_new, final_state)
        return _reference_tuple_inner(hidden_states, in_proj_w, conv_weight, conv_bias, dt_bias, A_log, D, norm_weight, out_proj_w)[0]

    def _L0_ffn_ref(hidden_states, gate_w, w_gate_up, w_down, shared_w_gate_up, shared_w_down):
        import jax, jax.numpy as jnp
        import numpy as np
        HIDDEN = 512
        MOE_INTER = 128
        SHARED_INTER = 512
        NUM_EXPERTS = 16
        TOP_K = 2

        def _moe_forward(x, gate_w, w_gate_up, w_down, shared_w_gate_up, shared_w_down):
            orig_shape = x.shape
            x2 = x.reshape(-1, orig_shape[-1])
            gu_s = x2 @ shared_w_gate_up.T
            g_s, u_s = jnp.split(gu_s, 2, axis=-1)
            shared_out = jax.nn.silu(g_s) * u_s @ shared_w_down.T
            logits = x2 @ gate_w.T
            probs = jax.nn.softmax(logits, axis=-1)
            topk_vals, topk_idx = jax.lax.top_k(probs, TOP_K)
            topk_vals = topk_vals / jnp.sum(topk_vals, axis=-1, keepdims=True)
            combine = jnp.sum(jax.nn.one_hot(topk_idx, NUM_EXPERTS, dtype=x2.dtype) * topk_vals[..., None], axis=1)
            gu = jnp.einsum('th,eih->eti', x2, w_gate_up)
            g, u = jnp.split(gu, 2, axis=-1)
            act = jax.nn.silu(g) * u
            out_e = jnp.einsum('eti,ehi->eth', act, w_down)
            moe_out = jnp.einsum('eth,te->th', out_e, combine)
            return (moe_out + shared_out).reshape(orig_shape)
        return _moe_forward(hidden_states, gate_w, w_gate_up, w_down, shared_w_gate_up, shared_w_down)

    def _L1_attn_ref(x, wq, wk, wv, wo):
        import math
        import jax, jax.numpy as jnp
        import numpy as np

        def _rope_tables(T, h, dtype):
            pos = jnp.arange(T, dtype=jnp.float32)
            thetas = 1.0 / 10000.0 ** (jnp.arange(0, h, 2, dtype=jnp.float32) / h)
            pt = jnp.outer(pos, thetas)
            pt = jnp.concatenate([pt, pt], axis=-1)
            return (jnp.sin(pt).astype(dtype), jnp.cos(pt).astype(dtype))

        def _apply_rope(x, sin, cos):
            h = x.shape[-1]
            rot = jnp.concatenate([-x[..., h // 2:], x[..., :h // 2]], axis=-1)
            return x * cos + rot * sin
        B, T, C = x.shape
        n_head = 32
        h = C // n_head

        def proj(w):
            y = jnp.einsum('btc,dc->btd', x, w)
            return y.reshape(B, T, n_head, h).transpose(0, 2, 1, 3)
        q, k, v = (proj(wq), proj(wk), proj(wv))
        sin, cos = _rope_tables(T, h, x.dtype)
        q = _apply_rope(q, sin, cos)
        k = _apply_rope(k, sin, cos)
        scores = jnp.einsum('bnth,bnsh->bnts', q, k) * (1.0 / math.sqrt(h))
        causal = jnp.tril(jnp.ones((T, T), dtype=bool))
        scores = jnp.where(causal, scores, -jnp.inf)
        attn = jax.nn.softmax(scores, axis=-1)
        out = jnp.einsum('bnts,bnsh->bnth', attn, v)
        out = out.transpose(0, 2, 1, 3).reshape(B, T, C)
        return jnp.einsum('btc,dc->btd', out, wo)

    def _L1_ffn_ref(x, A, B, Wr):
        import jax, jax.numpy as jnp
        import numpy as np
        BATCH, SEQ, D = (2, 256, 512)
        K, TOPK, RANK = (64, 16, 16)
        ALPHA = 32.0
        SCALING = ALPHA / RANK
        prefix = x.shape[:-1]
        xf = x.reshape(-1, x.shape[-1])
        N = xf.shape[0]
        scores = xf @ Wr.T
        top_vals, top_idx = jax.lax.top_k(scores, TOPK)
        gates = jax.nn.softmax(top_vals, axis=-1)
        G = jnp.zeros((N, K), xf.dtype).at[jnp.arange(N)[:, None], top_idx].set(gates)
        h = jnp.einsum('nd,krd->nkr', xf, A)
        out = jnp.einsum('nkr,kdr->nd', h * G[:, :, None], B)
        return (out * SCALING).reshape(*prefix, -1)
    x = L0_attn_hidden_states
    xn = _layernorm(x, axis=-1)
    s = _L0_attn_ref(xn, L0_attn_in_proj_w, L0_attn_conv_weight, L0_attn_conv_bias, L0_attn_dt_bias, L0_attn_A_log, L0_attn_D, L0_attn_norm_weight, L0_attn_out_proj_w)
    g = _silu(_L0_ffn_ref(xn, L0_ffn_gate_w, L0_ffn_w_gate_up, L0_ffn_w_down, L0_ffn_shared_w_gate_up, L0_ffn_shared_w_down))
    x = x + s * g
    xn = _layernorm(x, axis=-1)
    s = _L1_attn_ref(xn, L1_attn_wq, L1_attn_wk, L1_attn_wv, L1_attn_wo)
    g = _silu(_L1_ffn_ref(xn, L1_ffn_A, L1_ffn_B, L1_ffn_Wr))
    x = x + s * g
    return x

_drawn_inputs = setup_inputs


def setup_inputs(seed=0):
    import zlib

    import numpy as np

    out = dict(_drawn_inputs(seed))
    spreads = {'L0_attn_conv_bias': (0.0, 0.637),
     'L0_attn_dt_bias': (1.0, 0.6),
     'L0_attn_D': (1.0, 0.6),
     'L0_attn_norm_weight': (1.0, 0.6)}
    factors = {'L0_attn_in_proj_w': 6.246,
     'L0_attn_conv_weight': 8.0,
     'L0_attn_A_log': 8.0,
     'L0_attn_out_proj_w': 5.648,
     'L0_ffn_gate_w': 8.0,
     'L0_ffn_w_gate_up': 8.0,
     'L0_ffn_w_down': 8.0,
     'L0_ffn_shared_w_gate_up': 6.01,
     'L0_ffn_shared_w_down': 6.007,
     'L1_attn_wq': 8.0,
     'L1_attn_wk': 8.0,
     'L1_attn_wv': 8.0,
     'L1_attn_wo': 8.0,
     'L1_ffn_A': 8.0,
     'L1_ffn_B': 8.0,
     'L1_ffn_Wr': 8.0}
    for name, (base, spread) in spreads.items():
        noise = np.random.default_rng([zlib.crc32(name.encode()), seed]).standard_normal(out[name].shape)
        drawn = base * np.exp(spread * noise) if base else spread * noise
        out[name] = jnp.asarray(drawn.astype(out[name].dtype))
    for name, factor in factors.items():
        out[name] = (out[name] * factor).astype(out[name].dtype)
    return out
```

```python
from contextlib import ExitStack

import numpy as np

import concourse.bass as bass
from concourse import mybir
from concourse.alu_op_type import AluOpType as ALU

ACT = mybir.ActivationFunctionType
F32 = mybir.dt.float32
BF16 = mybir.dt.bfloat16
U32 = mybir.dt.uint32
AX = mybir.AxisListType

P = 128
NB, L, DM = 2, 512, 512
T = NB * L
TT = T // P
KD = DM // P
EPS = 1e-5

G, H, PH, NS, KC = 8, 64, 64, 128, 4
HG = H // G
CG = HG * PH
MG = CG // P
MC = MG + 2
CH = L // P
HT = H + 16

NE, EB, EC = 20, 4, 5

HN, HD, HU = 32, 16, 8
TH = L // P
PTW = sum(L - P * j for j in range(TH))
BLOCKS = [(0, 0), (1, 0), (2, 0), (0, 1), (1, 1), (0, 2)]
KB = HD * len(BLOCKS)
KR = KB + 3
NEG = -3.0e38


def phase_semaphores(nc, ctx, tag):
    taken = []

    def sem(name):
        taken.append(nc.alloc_semaphore(f"{tag}_{name}"))
        return taken[-1]

    def end():
        nc.clear_and_free_semaphores(taken)
        nc.all_engine_barrier()

    ctx.callback(end)
    return sem


def layernorm_phase(nc, x_dram, xnT, ident, x_res, tag, combine=None):
    with ExitStack() as ctx:
        sb = lambda n, s, d=F32: ctx.enter_context(nc.sbuf_tensor(f"{tag}_{n}", s, d))
        sem = phase_semaphores(nc, ctx, tag)
        xt = x_res if x_res is not None else sb("x", [P, TT, DM])
        xn = sb("xn", [P, 2, DM])
        gate = sb("gate", [P, 2, DM])
        prod = sb("prod", [P, 2, DM])
        stats = sb("stats", [P, TT, 6])
        mv = sb("mv", [P, TT, 2])
        ve = sb("ve", [P, TT])
        half = sb("half", [P, TT])
        rstd = sb("rstd", [P, TT])
        ps = ctx.enter_context(nc.psum_tensor(f"{tag}_ps", [P, 2, 512], F32))
        loaded = [sem(f"loaded{i}") for i in range(TT)]
        half_set, gate_done, prod_done, x_done = sem("half_set"), sem("gate_done"), sem("prod_done"), sem("x_done")
        stats_done, mv_done, ve_done, rstd_done = sem("stats_done"), sem("mv_done"), sem("ve_done"), sem("rstd_done")
        xn_done, tr_done, out_done = sem("xn_done"), sem("tr_done"), sem("out_done")
        block = ctx.enter_context(nc.Block())
        xv = x_dram.rearrange("(n p) d -> n p d", p=P)

        @block.sync
        def _(sp):
            for i in range(TT):
                sp.dma_start(xt[:, i, :], xv[i]).then_inc(loaded[i], 16)

        @block.gpsimd
        def _(pool):
            pool.wait_ge(half_set, 1)
            pool.wait_ge(ve_done, TT)
            pool.tensor_tensor(rstd[:], ve[:], half[:], ALU.pow).then_inc(rstd_done, 1)

        @block.scalar
        def _(act):
            if combine is not None:
                _, s, f, fscale = combine
                for i in range(TT):
                    if i >= 2:
                        act.wait_ge(prod_done, i - 1)
                    act.activation(gate[:, i % 2, :], f[:, i, :], ACT.Silu, scale=fscale).then_inc(gate_done, 1)
            for i in range(TT):
                act.wait_ge(tr_done, i + 1)
                act.activation(xnT[:, :, i * P:(i + 1) * P],
                               ps[:, i % 2, :].rearrange("p (k t) -> p k t", k=KD), ACT.Copy).then_inc(out_done, 1)

        @block.vector
        def _(dve):
            dve.memset(half[:], -0.5).then_inc(half_set, 1)
            for i in range(TT):
                dve.wait_ge(loaded[i], 16)
                if combine is not None:
                    _, s, f, _ = combine
                    dve.wait_ge(gate_done, i + 1)
                    if i >= 2:
                        dve.wait_ge(x_done, i - 1)
                    dve.tensor_tensor(prod[:, i % 2, :], s[:, i, :], gate[:, i % 2, :], ALU.mult).then_inc(prod_done, 1)
                    dve.wait_ge(prod_done, i + 1)
                    dve.tensor_tensor(xt[:, i, :], xt[:, i, :], prod[:, i % 2, :], ALU.add).then_inc(x_done, 1)
                    dve.wait_ge(x_done, i + 1)
                dve.bn_stats(stats[:, i, :], xt[:, i, :]).then_inc(stats_done, 1)
                dve.wait_ge(stats_done, i + 1)
                dve.bn_aggr(mv[:, i, :], stats[:, i, :]).then_inc(mv_done, 1)
                dve.wait_ge(mv_done, i + 1)
                dve.tensor_scalar(ve[:, i:i + 1], mv[:, i, 1:2], EPS, None, ALU.add).then_inc(ve_done, 1)
            dve.wait_ge(rstd_done, 1)
            for i in range(TT):
                if i >= 2:
                    dve.wait_ge(tr_done, i - 1)
                dve.tensor_scalar(xn[:, i % 2, :], xt[:, i, :], mv[:, i, 0:1], rstd[:, i:i + 1],
                                  ALU.subtract, ALU.mult).then_inc(xn_done, 1)

        @block.tensor
        def _(pe):
            for i in range(TT):
                pe.wait_ge(xn_done, i + 1)
                if i >= 2:
                    pe.wait_ge(out_done, i - 1)
                for k in range(KD):
                    last = pe.transpose(ps[:, i % 2, k * P:(k + 1) * P], xn[:, i % 2, k * P:(k + 1) * P], ident[:])
                last.then_inc(tr_done, 1)


def small_phase(nc, w_small, small_bias, a_log, iota16, xnT, ident, dtT, daz_dram, din_dram, comb_dram):
    with ExitStack() as ctx:
        sb = lambda n, s, d=F32: ctx.enter_context(nc.sbuf_tensor(f"sm_{n}", s, d))
        sem = phase_semaphores(nc, ctx, "sm")
        w = sb("w", [P, KD, HT])
        bias = sb("bias", [H, 1])
        alog = sb("alog", [H, 1])
        ea = sb("ea", [H, 1])
        nea = sb("nea", [H, 1])
        io = sb("io", [P, 16])
        z = sb("z", [HT, T])
        v = sb("v", [H, T])
        ab = sb("ab", [H, T])
        e = sb("e", [H, T])
        u = sb("u", [H, T])
        lnu = sb("lnu", [H, T])
        d = sb("d", [H, T])
        r = sb("r", [H, T])
        mx = sb("mx", [H, T])
        dA = sb("dA", [H, T])
        first = sb("first", [H, T])
        din = sb("din", [H, T])
        lg = sb("lg", [P, TT, 16])
        top = sb("top", [P, TT, 8])
        idx = sb("idx", [P, TT, 8], U32)
        idf = sb("idf", [P, TT, 8])
        gap = sb("gap", [P, TT, 1])
        eg = sb("eg", [P, TT, 1])
        den = sb("den", [P, TT, 1])
        wt = sb("wt", [P, TT, 2])
        oh = sb("oh", [P, TT, 2, 16])
        comb = sb("comb", [P, TT, 16])
        combT = sb("combT", [16, T])
        ones = sb("ones", [4, T])
        ps = ctx.enter_context(nc.psum_tensor("sm_ps", [P, 2, 512], F32))
        pt = ctx.enter_context(nc.psum_tensor("sm_pt", [P, 2, 512], F32))
        pc = ctx.enter_context(nc.psum_tensor("sm_pc", [P, 2, 512], F32))
        ld, pe_z, a_z, tr, ct, stored = (sem(n) for n in ("ld", "pe_z", "a_z", "tr", "ct", "stored"))
        scan_done, ct_done, ones_set = sem("scan_done"), sem("ct_done"), sem("ones_set")
        ea_done, nea_done, e_done, ln_done, dA_done, eg_done, ab_done = (sem(n) for n in (
            "ea_done", "nea_done", "e_done", "ln_done", "dA_done", "eg_done", "ab_done"))
        v_done, chain, dt_done, dtT_done, lg_done, comb_done, gap_done, z_free = (sem(n) for n in (
            "v_done", "chain", "dt_done", "dtT_done", "lg_done", "comb_done", "gap_done", "z_free"))
        block = ctx.enter_context(nc.Block())

        @block.sync
        def _(sp):
            for dst, src in ((w[:], w_small), (bias[:], small_bias), (alog[:], a_log), (io[:], iota16)):
                sp.dma_start(dst, src).then_inc(ld, 16)
            sp.wait_ge(scan_done, 1)
            sp.dma_start(daz_dram.rearrange("c h t -> h c t"), dA[:].rearrange("h (c t) -> h c t", t=P)).then_inc(stored, 16)
            sp.dma_start(din_dram.rearrange("c h t -> h c t"), din[:].rearrange("h (c t) -> h c t", t=P)).then_inc(stored, 16)
            sp.wait_ge(ct_done, TT)
            sp.dma_start(comb_dram[0:16, :], combT[:]).then_inc(stored, 16)
            sp.wait_ge(ones_set, 1)
            sp.dma_start(comb_dram[16:20, :], ones[:]).then_inc(stored, 16)
            sp.wait_ge(stored, 64)

        @block.tensor
        def _(pe):
            pe.wait_ge(ld, 64)
            for b in range(NB):
                for k in range(KD):
                    last = pe.matmul(ps[0:HT, b, :], w[:, k, :], xnT[:, k, b * L:(b + 1) * L], start=(k == 0), stop=(k == KD - 1))
                last.then_inc(pe_z, 1)
            pe.wait_ge(dt_done, 1)
            pe.wait_ge(a_z, NB)
            for i in range(TT):
                if i >= 2:
                    pe.wait_ge(lg_done, i - 1)
                pe.transpose(pt[:, i % 2, 0:HT], z[:, i * P:(i + 1) * P], ident[0:HT, 0:HT]).then_inc(tr, 1)
            for i in range(TT):
                pe.wait_ge(comb_done, i + 1)
                if i >= 2:
                    pe.wait_ge(ct_done, i - 1)
                pe.transpose(pc[0:16, i % 2, 0:P], comb[:, i, :], ident[:]).then_inc(ct, 1)

        @block.scalar
        def _(act):
            act.wait_ge(ld, 64)
            act.activation(ea[:], alog[:], ACT.Exp).then_inc(ea_done, 1)
            act.wait_ge(ea_done, 1)
            act.activation(nea[:], ea[:], ACT.Copy, scale=-1.0).then_inc(nea_done, 1)
            for b in range(NB):
                act.wait_ge(pe_z, b + 1)
                act.activation(z[H:HT, b * L:(b + 1) * L], ps[H:HT, b, :], ACT.Copy).then_inc(a_z, 1)
            act.wait_ge(v_done, 2)
            act.activation(ab[:], v[:], ACT.Abs).then_inc(ab_done, 1)
            act.wait_ge(ab_done, 1)
            act.activation(e[:], ab[:], ACT.Exp, scale=-1.0).then_inc(e_done, 1)
            act.wait_ge(chain, 1)
            act.activation(lnu[:], u[:], ACT.Ln).then_inc(ln_done, 1)
            act.wait_ge(dt_done, 1)
            act.wait_ge(nea_done, 1)
            act.activation(dA[:], z[0:H, :], ACT.Exp, scale=nea[:]).then_inc(dA_done, 1)
            act.wait_ge(gap_done, 1)
            act.activation(eg[:], gap[:], ACT.Exp).then_inc(eg_done, 1)

        @block.vector
        def _(dve):
            dve.memset(ones[:], 1.0).then_inc(ones_set, 1)
            dve.memset(first[:], 0.0).then_inc(z_free, 1)
            dve.wait_ge(ld, 64)
            for b in range(NB):
                dve.wait_ge(a_z, b + 1)
                dve.tensor_scalar(v[:, b * L:(b + 1) * L], ps[0:H, b, :], bias[:], None, ALU.add).then_inc(v_done, 1)
            dve.wait_ge(e_done, 1)
            dve.tensor_scalar(u[:], e[:], 1.0, None, ALU.add).then_inc(chain, 1)
            dve.wait_ge(chain, 1)
            dve.scalar_tensor_tensor(d[:], u[:], -1.0, e[:], ALU.add, ALU.subtract).then_inc(chain, 1)
            dve.reciprocal(r[:], u[:]).then_inc(chain, 1)
            dve.wait_ge(chain, 3)
            dve.tensor_tensor(d[:], d[:], r[:], ALU.mult).then_inc(chain, 1)
            dve.wait_ge(ln_done, 1)
            dve.wait_ge(v_done, 2)
            dve.scalar_tensor_tensor(mx[:], v[:], 0.0, lnu[:], ALU.max, ALU.add).then_inc(chain, 1)
            dve.wait_ge(chain, 5)
            dve.tensor_tensor(z[0:H, :], mx[:], d[:], ALU.subtract).then_inc(dt_done, 1)
            dve.wait_ge(dA_done, 1)
            dve.wait_ge(z_free, 1)
            dAc = dA[:].rearrange("h (c t) -> h c t", t=P)
            fc = first[:].rearrange("h (c t) -> h c t", t=P)
            dve.tensor_copy(fc[:, :, 0:1], dAc[:, :, 0:1]).then_inc(chain, 1)
            dve.wait_ge(chain, 6)
            dve.memset(dAc[:, :, 0:1], 0.0).then_inc(chain, 1)
            dve.wait_ge(chain, 7)
            dve.tensor_tensor_scan(din[:], dA[:], first[:], 0.0, ALU.mult, ALU.add).then_inc(scan_done, 1)
            for i in range(TT):
                dve.wait_ge(tr, i + 1)
                dve.tensor_copy(dtT[:, i, :], pt[:, i % 2, 0:H]).then_inc(dtT_done, 1)
                dve.tensor_copy(lg[:, i, :], pt[:, i % 2, H:HT]).then_inc(lg_done, 1)
            for i in range(TT):
                dve.wait_ge(lg_done, i + 1)
                dve.max(top[:, i, :], lg[:, i, :]).then_inc(chain, 1)
                dve.wait_ge(chain, 8 + 2 * i)
                dve.max_index(idx[:, i, :], top[:, i, :], lg[:, i, :]).then_inc(chain, 1)
            n = 7 + 2 * TT
            dve.wait_ge(chain, n)
            dve.tensor_copy(idf[:], idx[:]).then_inc(chain, 1)
            dve.tensor_tensor(gap[:], top[:, :, 1:2], top[:, :, 0:1], ALU.subtract).then_inc(gap_done, 1)
            dve.wait_ge(eg_done, 1)
            dve.tensor_scalar(den[:], eg[:], 1.0, None, ALU.add).then_inc(chain, 1)
            dve.wait_ge(chain, n + 2)
            dve.reciprocal(wt[:, :, 0:1], den[:]).then_inc(chain, 1)
            dve.wait_ge(chain, n + 3)
            dve.tensor_tensor(wt[:, :, 1:2], eg[:], wt[:, :, 0:1], ALU.mult).then_inc(chain, 1)
            dve.wait_ge(chain, n + 4)
            for i in range(TT):
                for j in range(2):
                    dve.tensor_scalar(oh[:, i, j, :], io[:], idf[:, i, j:j + 1], wt[:, i, j:j + 1],
                                      ALU.is_equal, ALU.mult).then_inc(chain, 1)
                dve.wait_ge(chain, n + 6 + 2 * i)
                dve.tensor_tensor(comb[:, i, :], oh[:, i, 0, :], oh[:, i, 1, :], ALU.add).then_inc(comb_done, 1)
            for i in range(TT):
                dve.wait_ge(ct, i + 1)
                dve.tensor_copy(combT[:, i * P:(i + 1) * P], pc[0:16, i % 2, 0:P]).then_inc(ct_done, 1)


def ssm_phase(nc, w_x, w_bc, w_gate, w_out, conv_par, d_par, n_par, ident8, xnT, ident, dtT, daz_dram, din_dram, s_acc):
    with ExitStack() as ctx:
        sb = lambda n, s, d=F32: ctx.enter_context(nc.sbuf_tensor(f"ss_{n}", s, d))
        sem = phase_semaphores(nc, ctx, "ss")
        wx = sb("wx", [P, KD, CG])
        wbc = sb("wbc", [P, KD, 2 * P])
        wg = sb("wg", [P, KD, CG])
        wo = sb("wo", [P, MG, DM])
        cpar = sb("cpar", [P, MC, KC + 1])
        dpar = sb("dpar", [P, MG])
        npar = sb("npar", [P, MG])
        id8 = sb("id8", [P, HG * P])
        daz = sb("daz", [P, 2, HG * P])
        din = sb("din", [P, 2, HG, P])
        cv = sb("cv", [P, 2, L])
        xc = sb("xc", [P, MG, L])
        Bc = sb("Bc", [P, L])
        Cc = sb("Cc", [P, 2, L])
        xD = sb("xD", [P, MG, L])
        Bt = sb("Bt", [P, CH, NS])
        xdt = sb("xdt", [P, CH, CG])
        Lm = sb("Lm", [P, 2, HG * P])
        M = sb("M", [P, CH, HG, P])
        CD = sb("CD", [P, 2, HG, P])
        Xw = sb("Xw", [P, 2, CG])
        S = sb("S", [P, 2, CG])
        St = sb("St", [P, CG])
        y = sb("y", [P, MG, L])
        ysq = sb("ysq", [P, MG, L])
        sg = sb("sg", [P, MG, L])
        z = sb("z", [P, MG, L])
        ones = sb("ones", [P, 1])
        half = sb("half", [P, CH])
        var = sb("var", [P, CH])
        rstd = sb("rstd", [P, CH])
        pp = ctx.enter_context(nc.psum_tensor("ss_pp", [P, 2, 512], F32))
        pt = ctx.enter_context(nc.psum_tensor("ss_pt", [P, 2, 512], F32))
        pc = ctx.enter_context(nc.psum_tensor("ss_pc", [P, CH, P], F32))
        py = ctx.enter_context(nc.psum_tensor("ss_py", [P, 2, MG, P], F32))
        pss = ctx.enter_context(nc.psum_tensor("ss_ps", [P, 512], F32))

        ld_x, ld_bc, ld_g, ld_o, ld_cp, ld_d, ld_n, ld_id = (sem(n) for n in (
            "ld_x", "ld_bc", "ld_g", "ld_o", "ld_cp", "ld_d", "ld_n", "ld_id"))
        ld_daz = [sem("ld_daz0"), sem("ld_daz1")]
        ld_din = [sem("ld_din0"), sem("ld_din1")]
        proj, gatep, tr, cb, ds, yp, ssq, outp = (sem(n) for n in (
            "proj", "gatep", "tr", "cb", "ds", "yp", "ssq", "outp"))
        acc, xc_d, xD_d, bt_d, sg_d = (sem(n) for n in ("acc", "xc_d", "xD_d", "bt_d", "sg_d"))
        tap, xdt_d, scan, m_d, s_d, y_d, z_d, o_d, var_d, cst = (sem(n) for n in (
            "tap", "xdt_d", "scan", "m_d", "s_d", "y_d", "z_d", "o_d", "var_d", "cst"))
        xw_d, cd_d, st_d, sq_d, r_d = (sem(n) for n in ("xw_d", "cd_d", "st_d", "sq_d", "r_d"))
        block = ctx.enter_context(nc.Block())
        TAPS = KC - 1
        row = lambda dram, i: dram[bass.ds(i, 1)].rearrange("a p n -> p (a n)")

        def groups(eng, pair):
            pair(0, False)
            with eng.Fori(1, G - 1) as g:
                pair(g, False)
            pair(G - 1, True)

        @block.sync
        def _(sp):
            def load_early(g):
                sp.wait_ge(tap, MC * TAPS * 2 * g)
                sp.dma_start(cpar[:].rearrange("p m k -> p (m k)"), row(conv_par, g)).then_inc(ld_cp, 16)
                sp.dma_start(wx[:].rearrange("p k n -> p (k n)"), row(w_x, g)).then_inc(ld_x, 16)
                sp.dma_start(wbc[:].rearrange("p k n -> p (k n)"), row(w_bc, g)).then_inc(ld_bc, 16)

            def load_mid(g):
                sp.wait_ge(sg_d, MG * 2 * g)
                sp.dma_start(wg[:].rearrange("p k n -> p (k n)"), row(w_gate, g)).then_inc(ld_g, 16)
                sp.dma_start(dpar[:], row(d_par, g)).then_inc(ld_d, 16)

            def load_late(g):
                sp.wait_ge(outp, CH * 2 * g)
                sp.dma_start(wo[:].rearrange("p k n -> p (k n)"), row(w_out, g)).then_inc(ld_o, 16)
                sp.dma_start(npar[:], row(n_par, g)).then_inc(ld_n, 16)

            def load_daz(g, b, j):
                if not (isinstance(g, int) and g == 0 and b == 0 and j < 2):
                    sp.wait_ge(scan, CH * (2 * g + b) + j - 1)
                src = daz_dram[CH * b + j, bass.ds(HG * g, HG), :].rearrange("h t -> (h t)").partition_broadcast(P)
                sp.dma_start(daz[:, j % 2, :], src).then_inc(ld_daz[j % 2], 16)

            def load_din(g, b, j):
                s = 2 * g + b
                if j == 2:
                    sp.wait_ge(cd_d, (CH - 1) * s)
                else:
                    sp.wait_ge(st_d, 2 * s + (j == 3))
                src = din_dram[CH * b + j, bass.ds(HG * g, HG), :].rearrange("h t -> (h t)").partition_broadcast(P)
                sp.dma_start(din[:, (b + j - 1) % 2].rearrange("p h t -> p (h t)"), src).then_inc(ld_din[(b + j - 1) % 2], 16)

            load_early(0)
            sp.dma_start(id8[:], ident8).then_inc(ld_id, 16)
            load_mid(0)

            def pair(g, last, first=False):
                for b in range(NB):
                    if not (first and b == 0):
                        load_daz(g, b, 0)
                        load_daz(g, b, 1)
                    load_din(g, b, 1)
                    load_din(g, b, 2)
                    load_daz(g, b, 2)
                    load_daz(g, b, 3)
                    if b == 0:
                        load_late(g)
                    load_din(g, b, 3)
                    if not last:
                        load_early(g + 1) if b == 0 else load_mid(g + 1)

            load_daz(0, 0, 0)
            load_daz(0, 0, 1)
            pair(0, False, first=True)
            with sp.Fori(1, G - 1) as g:
                pair(g, False)
            pair(G - 1, True)

        @block.tensor
        def _(pe):
            def project(g, b, m):
                s = 2 * g + b
                if m == 0:
                    pe.wait_ge(ld_x, 16 * (g + 1))
                if m == MG:
                    pe.wait_ge(ld_bc, 16 * (g + 1))
                if m < MC - 1:
                    pe.wait_ge(tap, TAPS * (MC * s + m))
                w = wx[:, :, m * P:(m + 1) * P] if m < MG else wbc[:, :, (m - MG) * P:(m - MG + 1) * P]
                for k in range(KD):
                    last = pe.matmul(pp[:, m == MC - 1, :], w[:, k, :], xnT[:, k, b * L:(b + 1) * L],
                                     start=(k == 0), stop=(k == KD - 1))
                last.then_inc(proj, 1)

            def gate(g, b, m):
                s = 2 * g + b
                if m == 0:
                    pe.wait_ge(ld_g, 16 * (g + 1))
                    pe.wait_ge(o_d, CH * s)
                pe.wait_ge(sg_d, MG * s + m)
                if m == 0:
                    pe.wait_ge(tap, TAPS * MC * (s + 1))
                for k in range(KD):
                    last = pe.matmul(pp[:, 1, :], wg[:, k, m * P:(m + 1) * P], xnT[:, k, b * L:(b + 1) * L],
                                     start=(k == 0), stop=(k == KD - 1))
                last.then_inc(gatep, 1)

            for m in range(MC):
                project(0, 0, m)

            def step(g, b, nxt):
                s = 2 * g + b
                for j in range(CH):
                    if j == 0:
                        pe.wait_ge(xc_d, MC * (s + 1))
                        pe.wait_ge(bt_d, s)
                    elif j == 1:
                        pe.wait_ge(var_d, s)
                    else:
                        pe.wait_ge(xdt_d, CH * s + j - 1)
                    for m in range(MG):
                        last = pe.transpose(pt[:, j % 2, m * P:(m + 1) * P], xc[:, m, j * P:(j + 1) * P], ident[:])
                    last.then_inc(tr, 1)
                pe.wait_ge(xdt_d, CH * s + 3)
                for j in range(CH):
                    last = pe.transpose(pt[:, 0, j * P:(j + 1) * P], Bc[:, j * P:(j + 1) * P], ident[:])
                last.then_inc(tr, 1)
                pe.wait_ge(m_d, CH * s)
                for j in range(CH):
                    last = pe.matmul(pc[:, j, :], Bc[:, j * P:(j + 1) * P], Cc[:, b, j * P:(j + 1) * P], start=True, stop=True)
                last.then_inc(cb, 1)
                for m in range(MC):
                    if nxt is not None:
                        if m == 0:
                            pe.wait_ge(o_d, CH * s)
                        if m == MC - 1:
                            pe.wait_ge(sg_d, MG * (s + 1))
                        project(*nxt, m)
                    if m < MG:
                        gate(g, b, m)
                for j in range(CH):
                    if j < CH - 1:
                        pe.wait_ge(xw_d, (CH - 1) * s + j + 1)
                        if j == 0:
                            pe.wait_ge(bt_d, s + 1)
                        pe.wait_ge(s_d, (CH - 1) * s + j)
                        pe.matmul(pss[:], Bt[:, j, :], Xw[:, (b + j) % 2, :], start=True, stop=True).then_inc(ds, 1)
                    pe.wait_ge(m_d, CH * s + j + 1)
                    pe.wait_ge(y_d, CH * s + j - 1 if j >= 2 else CH * s)
                    if j:
                        pe.wait_ge(cd_d, (CH - 1) * s + j)
                        pe.wait_ge(s_d, (CH - 1) * s + j)
                    for m in range(MG):
                        for hh in range(2):
                            h = 2 * m + hh
                            dst = py[hh * PH:(hh + 1) * PH, j % 2, m, :]
                            last = pe.matmul(dst, xdt[:, j, h * PH:(h + 1) * PH], M[:, j, h, :], start=True, stop=(j == 0))
                            if j:
                                last = pe.matmul(dst, S[:, (j - 1) % 2, h * PH:(h + 1) * PH], CD[:, (b + j - 1) % 2, h, :],
                                                 start=False, stop=True)
                    last.then_inc(yp, 1)
                pe.wait_ge(sq_d, 3 * (s + 1))
                for j in range(CH):
                    last = pe.matmul(pt[:, 1, j:j + 1], ysq[:, 0, j * P:(j + 1) * P], ones[:], start=True, stop=True)
                last.then_inc(ssq, 1)
                for j in range(CH):
                    if j == 0:
                        pe.wait_ge(ld_o, 16 * (g + 1))
                        pe.wait_ge(z_d, MG * (s + 1))
                        if nxt is not None:
                            pe.wait_ge(tap, TAPS * (MC * (s + 1) + MC - 1))
                        else:
                            pe.wait_ge(o_d, CH * s)
                    elif j == 1:
                        if nxt is not None:
                            pe.wait_ge(tap, TAPS * MC * (s + 2))
                        else:
                            pe.wait_ge(sg_d, MG * (s + 1))
                    else:
                        pe.wait_ge(o_d, CH * s + j - 1)
                    for m in range(MG):
                        last = pe.matmul(pp[:, j % 2, :], z[:, m, j * P:(j + 1) * P], wo[:, m, :], start=(m == 0), stop=(m == MG - 1))
                    last.then_inc(outp, 1)

            def pair(g, last):
                step(g, 0, (g, 1))
                step(g, 1, None if last else (g + 1, 0))

            groups(pe, pair)

        @block.scalar
        def _(act):
            def conv_start(g, b, m):
                s = 2 * g + b
                act.wait_ge(proj, MC * s + m + 1)
                if m == 0:
                    act.wait_ge(ld_cp, 16 * (g + 1))
                act.wait_ge(xc_d, MC * s + max(m - 1, 0))
                act.activation(cv[:, m % 2, :], pp[:, m == MC - 1, :], ACT.Identity, scale=cpar[:, m, KC - 1:KC],
                               bias=cpar[:, m, KC:KC + 1]).then_inc(acc, 1)

            def conv_silu(g, b, m, first=False):
                s = 2 * g + b
                act.wait_ge(tap, TAPS * (MC * s + m + 1))
                if m < MG:
                    dst = xc[:, m, :]
                    if not first:
                        act.wait_ge(tr, (CH + 1) * (s - 1) + CH)
                        act.wait_ge(xD_d, MG * s)
                elif m == MG:
                    dst = Bc[:]
                    if not first:
                        act.wait_ge(cb, s)
                else:
                    dst = Cc[:, b, :]
                    if not first:
                        act.wait_ge(cd_d, (CH - 1) * (s - 1))
                act.activation(dst, cv[:, m % 2, :], ACT.Silu).then_inc(xc_d, 1)

            for m in range(MC):
                conv_start(0, 0, m)
                if m:
                    conv_silu(0, 0, m - 1, True)
            conv_silu(0, 0, MC - 1, True)

            def step(g, b, nxt):
                s = 2 * g + b
                act.wait_ge(ld_d, 16 * (g + 1))
                act.wait_ge(y_d, CH * s)
                act.wait_ge(xc_d, MC * s + MG)
                for m in range(MG):
                    act.activation(xD[:, m, :], xc[:, m, :], ACT.Copy, scale=dpar[:, m:m + 1]).then_inc(xD_d, 1)
                act.wait_ge(tr, (CH + 1) * (s + 1))
                act.wait_ge(ds, (CH - 1) * s)
                act.activation(Bt[:].rearrange("p c n -> p (c n)"), pt[:, 0, :], ACT.Copy).then_inc(bt_d, 1)
                for m in range(MC + 1):
                    if nxt is not None and m < MC:
                        conv_start(*nxt, m)
                    if m < MG:
                        act.wait_ge(gatep, MG * s + m + 1)
                        if m == 0:
                            act.wait_ge(z_d, MG * s)
                        act.activation(sg[:, m, :], pp[:, 1, :], ACT.Silu).then_inc(sg_d, 1)
                    if nxt is not None and m:
                        conv_silu(*nxt, m - 1)

            def pair(g, last):
                step(g, 0, (g, 1))
                step(g, 1, None if last else (g + 1, 0))

            groups(act, pair)

        @block.vector
        def _(dve):
            dve.memset(ones[:], 1.0).then_inc(cst, 1)
            dve.memset(half[:], -0.5).then_inc(cst, 1)
            dve.memset(s_acc[:], 0.0).then_inc(cst, 1)

            def taps(g, b, m):
                s = 2 * g + b
                dve.wait_ge(acc, MC * s + m + 1)
                for i in range(1, KC):
                    n = TAPS * (MC * s + m) + i - 1
                    if i > 1:
                        dve.wait_ge(tap, n)
                    dve.scalar_tensor_tensor(cv[:, m % 2, i:], pp[:, m == MC - 1, :L - i], cpar[:, m, KC - 1 - i:KC - i],
                                             cv[:, m % 2, i:], ALU.mult, ALU.add).then_inc(tap, 1)

            for m in range(MC):
                taps(0, 0, m)
            dve.wait_ge(cst, 3)
            dve.wait_ge(ld_id, 16)

            def step(g, b, nxt):
                s = 2 * g + b
                for j in range(CH):
                    dve.wait_ge(tr, (CH + 1) * s + j + 1)
                    if j == 0:
                        dve.wait_ge(yp, CH * s)
                        dve.wait_ge(xw_d, (CH - 1) * s)
                    dtb = dtT[:, CH * b + j, bass.ds(HG * g, HG)].unsqueeze(2).to_broadcast([P, HG, PH])
                    dve.tensor_tensor(xdt[:, j, :].rearrange("p (h c) -> p h c", h=HG),
                                      pt[:, j % 2, :].rearrange("p (h c) -> p h c", h=HG), dtb, ALU.mult).then_inc(xdt_d, 1)
                for j in range(MC):
                    if j < CH:
                        dve.wait_ge(ld_daz[j % 2], 16 * (2 * s + j // 2 + 1))
                        dve.wait_ge(m_d, CH * s + max(j - 1, 0))
                        dve.wait_ge(xw_d, (CH - 1) * s + max(j - 1, 0))
                        dve.tensor_tensor_scan(Lm[:, j % 2, :], daz[:, j % 2, :], id8[:], 0.0, ALU.mult, ALU.add).then_inc(scan, 1)
                        dve.wait_ge(scan, CH * s + j + 1)
                        if j == 0:
                            dve.wait_ge(cb, s + 1)
                        dve.tensor_tensor(M[:, j], Lm[:, j % 2, :].rearrange("p (h t) -> p h t", h=HG),
                                          pc[:, j, :].unsqueeze(1).to_broadcast([P, HG, P]), ALU.mult).then_inc(m_d, 1)
                    if nxt is not None:
                        taps(*nxt, j)
                for j in range(CH):
                    if j < CH - 1:
                        dve.wait_ge(ds, (CH - 1) * s + j + 1)
                        if j == 0:
                            dve.wait_ge(st_d, 2 * s)
                            dve.tensor_copy(S[:, 0, :], pss[:]).then_inc(s_d, 1)
                        else:
                            if j == 2:
                                dve.wait_ge(yp, CH * s + 2)
                            dve.wait_ge(st_d, 2 * s + j)
                            dve.tensor_tensor(S[:, j % 2, :], pss[:], St[:], ALU.add).then_inc(s_d, 1)
                    dve.wait_ge(yp, CH * s + j + 1)
                    if j == 0:
                        dve.wait_ge(sq_d, 3 * s)
                        dve.wait_ge(z_d, MG * s)
                        dve.wait_ge(xD_d, MG * (s + 1))
                    dve.tensor_tensor(y[:, :, j * P:(j + 1) * P], py[:, j % 2], xD[:, :, j * P:(j + 1) * P], ALU.add).then_inc(y_d, 1)
                dve.wait_ge(y_d, CH * (s + 1))
                dve.wait_ge(sg_d, MG * (s + 1))
                dve.wait_ge(ld_n, 16 * (g + 1))
                dve.wait_ge(outp, CH * s)
                for m in range(MG):
                    dve.scalar_tensor_tensor(z[:, m, :], y[:, m, :], npar[:, m:m + 1], sg[:, m, :], ALU.mult, ALU.mult).then_inc(z_d, 1)
                dve.wait_ge(ssq, s + 1)
                dve.wait_ge(r_d, s)
                dve.tensor_scalar(var[:], pt[:, 1, 0:CH], 1.0 / CG, EPS, ALU.mult, ALU.add).then_inc(var_d, 1)
                dve.wait_ge(r_d, s + 1)
                dve.wait_ge(o_d, CH * s)
                for j in range(CH):
                    dve.wait_ge(outp, CH * s + j + 1)
                    i = CH * b + j
                    dve.scalar_tensor_tensor(s_acc[:, i, :], pp[:, j % 2, :], rstd[:, j:j + 1], s_acc[:, i, :],
                                             ALU.mult, ALU.add).then_inc(o_d, 1)

            def pair(g, last):
                step(g, 0, (g, 1))
                step(g, 1, None if last else (g + 1, 0))

            groups(dve, pair)

        @block.gpsimd
        def _(pool):
            pool.wait_ge(cst, 3)

            def step(g, b):
                s = 2 * g + b

                def scale_c(j):
                    q = (b + j - 1) % 2
                    n = 3 * g + ([1, 1, 2, 2, 3, 3][3 * b + j - 1])
                    pool.wait_ge(ld_din[q], 16 * n)
                    if j == 1:
                        pool.wait_ge(xc_d, MC * (s + 1))
                    pool.wait_ge(yp, CH * s + (2 if j == 3 else 0))
                    pool.tensor_tensor(CD[:, q], din[:, q], Cc[:, b, j * P:(j + 1) * P].unsqueeze(1).to_broadcast([P, HG, P]),
                                       ALU.mult).then_inc(cd_d, 1)

                for j in range(CH - 1):
                    pool.wait_ge(scan, CH * s + j + 1)
                    if j == 0:
                        pool.wait_ge(xdt_d, CH * (s + 1))
                    pool.wait_ge(ds, (CH - 1) * s + (1 if j == 2 else 0))
                    last = Lm[:, j % 2, :].rearrange("p (h t) -> p h t", h=HG)[:, :, P - 1:P].to_broadcast([P, HG, PH])
                    pool.tensor_tensor(Xw[:, (b + j) % 2, :].rearrange("p (h c) -> p h c", h=HG),
                                       xdt[:, j, :].rearrange("p (h c) -> p h c", h=HG), last, ALU.mult).then_inc(xw_d, 1)
                    if j < 2:
                        scale_c(j + 1)
                for j in (1, 2):
                    q = (b + j - 1) % 2
                    pool.wait_ge(s_d, (CH - 1) * s + j)
                    last = din[:, q, :, P - 1:P].to_broadcast([P, HG, PH])
                    pool.tensor_tensor(St[:].rearrange("p (h c) -> p h c", h=HG),
                                       S[:, (j - 1) % 2, :].rearrange("p (h c) -> p h c", h=HG), last, ALU.mult).then_inc(st_d, 1)
                scale_c(3)
                pool.wait_ge(y_d, CH * (s + 1))
                pool.wait_ge(ssq, s)
                pool.tensor_tensor(ysq[:], y[:], y[:], ALU.mult).then_inc(sq_d, 1)
                pool.wait_ge(sq_d, 3 * s + 1)
                pool.tensor_tensor(ysq[:, 0:2, :], ysq[:, 0:2, :], ysq[:, 2:4, :], ALU.add).then_inc(sq_d, 1)
                pool.wait_ge(sq_d, 3 * s + 2)
                pool.tensor_tensor(ysq[:, 0, :], ysq[:, 0, :], ysq[:, 1, :], ALU.add).then_inc(sq_d, 1)
                pool.wait_ge(var_d, s + 1)
                pool.wait_ge(o_d, CH * s)
                pool.tensor_tensor(rstd[:], var[:], half[:], ALU.pow).then_inc(r_d, 1)

            def pair(g, last):
                step(g, 0)
                step(g, 1)

            groups(pool, pair)


def moe_phase(nc, w_gu, w_dn, comb_dram, xnT, f_acc):
    with ExitStack() as ctx:
        sb = lambda n, s, d=F32: ctx.enter_context(nc.sbuf_tensor(f"mo_{n}", s, d))
        sem = phase_semaphores(nc, ctx, "mo")
        wgu = [sb(f"wgu{i}", [P, KD, EB, 2 * P]) for i in range(2)]
        wdn = [sb(f"wdn{i}", [P, EB, DM]) for i in range(2)]
        comb = [sb(f"comb{i}", [P, EB, T]) for i in range(2)]
        sgl = sb("sgl", [P, 2, L])
        sgc = sb("sgc", [P, 2, L])
        act_t = sb("act", [P, EB, T])
        pg = ctx.enter_context(nc.psum_tensor("mo_pg", [P, 2, 512], F32))
        pu = ctx.enter_context(nc.psum_tensor("mo_pu", [P, 2, 512], F32))
        pd = ctx.enter_context(nc.psum_tensor("mo_pd", [P, 2, 512], F32))
        ld_gu = [sem(f"ld_gu{i}") for i in range(2)]
        ld_dn = [sem(f"ld_dn{i}") for i in range(2)]
        ld_cb = [sem(f"ld_cb{i}") for i in range(2)]
        gp, up, dn, sl_d, sc_d, act_d, f_d, cst = (sem(n) for n in ("gp", "up", "dn", "sl_d", "sc_d", "act_d", "f_d", "cst"))
        block = ctx.enter_context(nc.Block())
        UN = EB * NB

        def load_count(c, q):
            return 8 * (c - q) + 16

        def chunks(eng, one):
            one(0, 0)
            with eng.Fori(0, EC // 2) as i:
                one(2 * i + 1, 1)
                one(2 * i + 2, 0)

        @block.sync
        def _(sp):
            for c in range(EC):
                q, free = c % 2, UN * max(c - 1, 0)
                sp.wait_ge(up, free)
                sp.dma_start(wgu[q][:].rearrange("p k e n -> p (k e n)"), w_gu[c]).then_inc(ld_gu[q], 16)
                sp.wait_ge(sc_d, free)
                sp.dma_start(comb[q][:].rearrange("p e t -> p (e t)"),
                             comb_dram[EB * c:EB * (c + 1), :].rearrange("e t -> (e t)").partition_broadcast(P)).then_inc(ld_cb[q], 16)
                sp.wait_ge(dn, TT * max(c - 1, 0))
                sp.dma_start(wdn[q][:].rearrange("p e n -> p (e n)"), w_dn[c]).then_inc(ld_dn[q], 16)

        @block.tensor
        def _(pe):
            def one(c, q):
                for b in range(NB):
                    for e in range(EB):
                        u = b * EB + e
                        n = UN * c + u
                        if u == 0:
                            pe.wait_ge(ld_gu[q], load_count(c, q))
                        pe.wait_ge(sl_d, UN * c + max(u - 1, 0))
                        for k in range(KD):
                            last = pe.matmul(pg[:, u % 2, :], wgu[q][:, k, e, 0:P], xnT[:, k, b * L:(b + 1) * L],
                                             start=(k == 0), stop=(k == KD - 1))
                        last.then_inc(gp, 1)
                        pe.wait_ge(act_d, UN * c + max(u - 1, 0))
                        for k in range(KD):
                            last = pe.matmul(pu[:, u % 2, :], wgu[q][:, k, e, P:2 * P], xnT[:, k, b * L:(b + 1) * L],
                                             start=(k == 0), stop=(k == KD - 1))
                        last.then_inc(up, 1)
                pe.wait_ge(ld_dn[q], load_count(c, q))
                for i in range(TT):
                    if i % (TT // NB) == 0:
                        pe.wait_ge(act_d, UN * c + EB * (i // (TT // NB) + 1))
                    pe.wait_ge(f_d, TT * c + max(i - 1, 0))
                    for e in range(EB):
                        last = pe.matmul(pd[:, i % 2, :], act_t[:, e, i * P:(i + 1) * P], wdn[q][:, e, :],
                                         start=(e == 0), stop=(e == EB - 1))
                    last.then_inc(dn, 1)
            chunks(pe, one)

        @block.scalar
        def _(act):
            def one(c, q):
                for u in range(UN):
                    act.wait_ge(gp, UN * c + u + 1)
                    act.wait_ge(sc_d, UN * c + max(u - 1, 0))
                    act.activation(sgl[:, u % 2, :], pg[:, u % 2, :], ACT.Silu).then_inc(sl_d, 1)
            chunks(act, one)

        @block.gpsimd
        def _(pool):
            def one(c, q):
                for u in range(UN):
                    b, e = u // EB, u % EB
                    if u == 0:
                        pool.wait_ge(ld_cb[q], load_count(c, q))
                    pool.wait_ge(sl_d, UN * c + u + 1)
                    pool.wait_ge(act_d, UN * c + max(u - 1, 0))
                    pool.tensor_tensor(sgc[:, u % 2, :], sgl[:, u % 2, :], comb[q][:, e, b * L:(b + 1) * L], ALU.mult).then_inc(sc_d, 1)
            chunks(pool, one)

        @block.vector
        def _(dve):
            dve.memset(f_acc[:], 0.0).then_inc(cst, 1)

            def one(c, q):
                for u in range(UN):
                    b, e = u // EB, u % EB
                    if u == 0:
                        dve.wait_ge(dn, TT * c)
                    dve.wait_ge(up, UN * c + u + 1)
                    dve.wait_ge(sc_d, UN * c + u + 1)
                    dve.tensor_tensor(act_t[:, e, b * L:(b + 1) * L], pu[:, u % 2, :], sgc[:, u % 2, :], ALU.mult).then_inc(act_d, 1)
                dve.wait_ge(cst, 1)
                dve.wait_ge(f_d, TT * c)
                for i in range(TT):
                    dve.wait_ge(dn, TT * c + i + 1)
                    dve.tensor_tensor(f_acc[:, i, :], pd[:, i % 2, :], f_acc[:, i, :], ALU.add).then_inc(f_d, 1)
            chunks(dve, one)


def qkv_phase(nc, w_q, w_k, w_v, rot_dram, cos_dram, sin_dram, xnT, V1, q_parts, k_parts):
    with ExitStack() as ctx:
        sb = lambda n, s, d=F32: ctx.enter_context(nc.sbuf_tensor(f"qk_{n}", s, d))
        sem = phase_semaphores(nc, ctx, "qk")
        w = [sb(n, [P, KD, DM]) for n in ("wq", "wk", "wv")]
        rot = sb("rot", [P, P])
        cos = sb("cos", [P, L])
        sin = sb("sin", [P, L])
        raw = sb("raw", [P, 2, L])
        t1 = sb("t1", [P, 2, L])
        t2 = sb("t2", [P, 2, L])
        qr = sb("qr", [P, 2, L])
        r1 = sb("r1", [P, 2, L])
        parts = sb("parts", [P, 2, 3, L], BF16)
        pq = ctx.enter_context(nc.psum_tensor("qk_pq", [P, 2, 512], F32))
        pr = ctx.enter_context(nc.psum_tensor("qk_pr", [P, 2, 512], F32))
        ld = [sem(f"ld{i}") for i in range(3)]
        ldc, proj, rotd, raw_d, t1_d, t2_d, qr_d, p1_d, r1_d, p2_d, p3_d, vp, v_d, vz, out_s = (sem(n) for n in (
            "ldc", "proj", "rotd", "raw_d", "t1_d", "t2_d", "qr_d", "p1_d", "r1_d", "p2_d", "p3_d", "vp", "v_d", "vz", "out_s"))
        st = [sem("st0"), sem("st1")]
        block = ctx.enter_context(nc.Block())
        items = [(b, i, m) for b in range(NB) for i in range(2) for m in range(KD)]
        N = len(items)

        @block.sync
        def _(sp):
            for i, (dst, src) in enumerate(zip(w, (w_q, w_k, w_v))):
                sp.dma_start(dst[:].rearrange("p k n -> p (k n)"), src).then_inc(ld[i], 16)
                if i == 0:
                    for dst, src in ((rot[:], rot_dram), (cos[:], cos_dram), (sin[:], sin_dram)):
                        sp.dma_start(dst, src).then_inc(ldc, 16)
            for n, (b, i, m) in enumerate(items):
                sp.wait_ge(p3_d, n + 1)
                sp.wait_ge(p1_d, n + 1)
                sp.wait_ge(p2_d, n + 1)
                dst = (q_parts, k_parts)[i][b, :, m * P:(m + 1) * P, :].rearrange("a p t -> p a t")
                sp.dma_start(dst, parts[:, n % 2]).then_inc(st[n % 2], 16)
            for i in range(2):
                sp.wait_ge(st[i], 16 * N // 2)

        @block.tensor
        def _(pe):
            def rotate(n):
                pe.wait_ge(raw_d, n + 1)
                if n >= 2:
                    pe.wait_ge(t1_d, n - 1)
                if n == 0:
                    pe.wait_ge(ldc, 48)
                pe.matmul(pr[:, n % 2, :], rot[:], raw[:, n % 2, :], start=True, stop=True).then_inc(rotd, 1)

            for n, (b, i, m) in enumerate(items):
                pe.wait_ge(ld[i], 16)
                if n >= 2:
                    pe.wait_ge(raw_d, n - 1)
                for k in range(KD):
                    last = pe.matmul(pq[:, n % 2, :], w[i][:, k, m * P:(m + 1) * P], xnT[:, k, b * L:(b + 1) * L],
                                     start=(k == 0), stop=(k == KD - 1))
                last.then_inc(proj, 1)
                if n:
                    rotate(n - 1)
            rotate(N - 1)
            pe.wait_ge(ld[2], 16)
            for i in range(TT):
                if i < 2:
                    pe.wait_ge(raw_d, N)
                else:
                    pe.wait_ge(v_d, i - 1)
                for k in range(KD):
                    last = pe.matmul(pq[:, i % 2, :], xnT[:, k, i * P:(i + 1) * P], w[2][:, k, :], start=(k == 0), stop=(k == KD - 1))
                last.then_inc(vp, 1)

        @block.scalar
        def _(act):
            def split(n):
                act.wait_ge(qr_d, n + 1)
                if n >= 2:
                    act.wait_ge(st[n % 2], 16 * (n // 2))
                act.activation(parts[:, n % 2, 0, :], qr[:, n % 2, :], ACT.Copy).then_inc(p1_d, 1)
                act.wait_ge(r1_d, n + 1)
                act.activation(parts[:, n % 2, 1, :], r1[:, n % 2, :], ACT.Copy).then_inc(p2_d, 1)

            for n in range(N):
                act.wait_ge(proj, n + 1)
                if n >= 2:
                    act.wait_ge(rotd, n - 1)
                    act.wait_ge(t2_d, n - 1)
                act.activation(raw[:, n % 2, :], pq[:, n % 2, :], ACT.Copy).then_inc(raw_d, 1)
                if n:
                    split(n - 1)
            split(N - 1)
            act.wait_ge(vz, 2)
            for i in range(TT):
                act.wait_ge(vp, i + 1)
                act.activation(V1[:, i, :, 0:HD], pq[:, i % 2, :].rearrange("p (h d) -> p h d", d=HD), ACT.Copy).then_inc(v_d, 1)

        @block.gpsimd
        def _(pool):
            pool.wait_ge(ldc, 48)
            for n in range(N):
                pool.wait_ge(raw_d, n + 1)
                if n >= 2:
                    pool.wait_ge(qr_d, n - 1)
                pool.tensor_tensor(t2[:, n % 2, :], raw[:, n % 2, :], cos[:], ALU.mult).then_inc(t2_d, 1)

        @block.vector
        def _(dve):
            dve.memset(V1[:], 0.0).then_inc(vz, 1)
            dve.wait_ge(vz, 1)
            dve.memset(V1[:, :, :, HD:HD + 1], 1.0).then_inc(vz, 1)
            for n in range(N):
                dve.wait_ge(rotd, n + 1)
                if n == 0:
                    dve.wait_ge(ldc, 48)
                if n >= 2:
                    dve.wait_ge(qr_d, n - 1)
                dve.tensor_tensor(t1[:, n % 2, :], pr[:, n % 2, :], sin[:], ALU.mult).then_inc(t1_d, 1)
                dve.wait_ge(t1_d, n + 1)
                dve.wait_ge(t2_d, n + 1)
                if n >= 2:
                    dve.wait_ge(p1_d, n - 1)
                    dve.wait_ge(r1_d, n - 1)
                dve.tensor_tensor(qr[:, n % 2, :], t1[:, n % 2, :], t2[:, n % 2, :], ALU.add).then_inc(qr_d, 1)
                dve.wait_ge(p1_d, n + 1)
                if n >= 2:
                    dve.wait_ge(p3_d, n - 1)
                    dve.wait_ge(p2_d, n - 1)
                dve.tensor_tensor(r1[:, n % 2, :], qr[:, n % 2, :], parts[:, n % 2, 0, :], ALU.subtract).then_inc(r1_d, 1)
                dve.wait_ge(p2_d, n + 1)
                dve.tensor_tensor(parts[:, n % 2, 2, :], r1[:, n % 2, :], parts[:, n % 2, 1, :], ALU.subtract).then_inc(p3_d, 1)


def attention_phase(nc, q_parts, k_parts, V1, w_o, mask_dram, maskT_dram, sel_dram, ident, s_acc):
    with ExitStack() as ctx:
        sb = lambda n, s, d=F32: ctx.enter_context(nc.sbuf_tensor(f"at_{n}", s, d))
        sem = phase_semaphores(nc, ctx, "at")
        QS = [sb(f"QS{i}", [KR, HU, L], BF16) for i in range(2)]
        KS = [sb(f"KS{i}", [KR, HU, L], BF16) for i in range(2)]
        wo = sb("wo", [P, HN // 4, DM])
        mask = sb("mask", [P, L])
        maskf = sb("maskf", [P, P])
        maskT = sb("maskT", [P, P], BF16)
        identb = sb("identb", [P, P], BF16)
        sel = sb("sel", [P, P])
        junk = sb("junk", [P, 2, L], BF16)
        mx = sb("mx", [P, TH, HU])
        nm = sb("nm", [HU, L])
        nr = sb("nr", [HU, L])
        nparts = sb("nparts", [HU, 3, L], BF16)
        PT = sb("PT", [P, 4, PTW])
        oT = sb("oT", [P, 2, L])
        rb = sb("rb", [P, 2, L])
        on = sb("on", [P, HN // 4, L])
        p1 = ctx.enter_context(nc.psum_tensor("at_p1", [P, 2, 512], F32))
        p2 = ctx.enter_context(nc.psum_tensor("at_p2", [P, 3, 512], F32))
        po = ctx.enter_context(nc.psum_tensor("at_po", [P, 512], F32))
        pb = ctx.enter_context(nc.psum_tensor("at_pb", [P, 512], F32))
        pf = ctx.enter_context(nc.psum_tensor("at_pf", [P, 512], F32))
        ldc = sem("ldc")
        ldq = [sem("ldq0"), sem("ldq1")]
        ld1 = [sem("ld1_0"), sem("ld1_1")]
        ldm = [sem("ldm0"), sem("ldm1")]
        s1, mx_d, mt, nm_d, nr_d, np1_d, np2_d, np3_d, s2, ex_d, pv, oT_d, bc, rb_d, on_d, fo, f_d, ones_d = (sem(n) for n in (
            "s1", "mx_d", "mt", "nm_d", "nr_d", "np1_d", "np2_d", "np3_d", "s2", "ex_d", "pv", "oT_d", "bc", "rb_d",
            "on_d", "fo", "f_d", "ones_d"))
        block = ctx.enter_context(nc.Block())
        NU = NB * HN // HU
        UB = NU // NB
        off = [sum(L - P * i for i in range(j)) for j in range(TH)]

        @block.sync
        def _(sp):
            for dst, src in ((mask[:], mask_dram), (maskf[:], maskT_dram), (sel[:], sel_dram),
                             (wo[:].rearrange("p q n -> p (q n)"), w_o)):
                sp.dma_start(dst, src).then_inc(ldc, 16)
            def load(u):
                b, m, q = u // UB, u % UB, u % 2
                if u >= 2:
                    sp.wait_ge(s2, TH * HU * (u - 1))
                for n, (a, c) in enumerate(BLOCKS):
                    for dst, src, part in ((QS[q], q_parts, a), (KS[q], k_parts, c)):
                        sp.dma_start(dst[n * HD:(n + 1) * HD, :, :],
                                     src[b, part, m * P:(m + 1) * P, :].rearrange("(h d) t -> d h t", d=HD)).then_inc(ldq[q], 16)

            load(0)
            load(1)
            for u in range(NU):
                sp.wait_ge(np1_d, u + 1)
                sp.wait_ge(np2_d, u + 1)
                sp.wait_ge(np3_d, u + 1)
                for i in range(3):
                    sp.dma_start(QS[u % 2][KB + i:KB + i + 1, :, :], nparts[:, i, :]).then_inc(ldm[u % 2], 16)
                if u >= 1 and u + 1 < NU:
                    load(u + 1)

        @block.tensor
        def _(pe):
            pe.wait_ge(ldc, 64)
            pe.wait_ge(ones_d, 4)

            def maxima(u):
                q = u % 2
                pe.wait_ge(ldq[q], 16 * 12 * (u // 2 + 1))
                for h in range(HU):
                    for i in range(TH):
                        n = (u * HU + h) * TH + i
                        if n >= 2:
                            pe.wait_ge(mx_d, n - 1)
                        if h == 0 and i < 2 and u:
                            pe.wait_ge(nm_d, u)
                        pe.matmul(p1[:, n % 2, 0:(i + 1) * P], QS[q][0:KB, h, i * P:(i + 1) * P], KS[q][0:KB, h, 0:(i + 1) * P],
                                  start=True, stop=True).then_inc(s1, 1)
                pe.wait_ge(mx_d, TH * HU * (u + 1))
                for i in range(TH):
                    last = pe.transpose(p1[0:HU, 0, i * P:(i + 1) * P], mx[:, i, :], ident[:])
                last.then_inc(mt, 1)

            def weigh(u):
                q, b = u % 2, u // UB
                pe.wait_ge(ldm[q], 48 * (u // 2 + 1))
                for quad in range(HU // 4):
                    nq = u * (HU // 4) + quad
                    for c in range(4):
                        h = quad * 4 + c
                        for j in range(TH):
                            n = (u * HU + h) * TH + j
                            if n >= 3:
                                pe.wait_ge(ex_d, n - 2)
                            w = L - j * P
                            pe.matmul(p2[:, n % 3, 0:w], KS[q][:, h, j * P:(j + 1) * P], QS[q][:, h, j * P:L], start=True, stop=False)
                            pe.matmul(p2[:, n % 3, 0:P], identb[:], maskT[:], start=False, stop=True).then_inc(s2, 1)
                    pe.wait_ge(ex_d, 4 * TH * (nq + 1))
                    if nq:
                        pe.wait_ge(oT_d, nq)
                    for j in range(TH):
                        for c in range(4):
                            h = (u % UB) * HU + quad * 4 + c
                            last = pe.matmul(po[32 * c:32 * c + 32, j * P:L], V1[:, b * TH + j, h, :], PT[:, c, off[j]:off[j] + L - j * P],
                                             start=(j == 0), stop=(j == TH - 1), skip_group_check=True)
                    last.then_inc(pv, 1)
                    pe.wait_ge(oT_d, nq + 1)
                    if nq:
                        pe.wait_ge(rb_d, nq)
                    pe.matmul(pb[:], sel[:], oT[:, nq % 2, :], start=True, stop=True).then_inc(bc, 1)

            def output(b):
                pe.wait_ge(on_d, (HN // 4) * (b + 1))
                for i in range(TH):
                    n = b * TH + i
                    if n:
                        pe.wait_ge(f_d, n)
                    for qd in range(HN // 4):
                        last = pe.matmul(pf[:], on[:, qd, i * P:(i + 1) * P], wo[:, qd, :], start=(qd == 0), stop=(qd == HN // 4 - 1))
                    last.then_inc(fo, 1)

            maxima(0)
            for u in range(NU):
                if u + 1 < NU:
                    maxima(u + 1)
                weigh(u)
                if u % UB == UB - 1:
                    output(u // UB)

        @block.scalar
        def _(act):
            def weigh(u):
                for quad in range(HU // 4):
                    nq = u * (HU // 4) + quad
                    for c in range(4):
                        h = quad * 4 + c
                        for j in range(TH):
                            n = (u * HU + h) * TH + j
                            act.wait_ge(s2, n + 1)
                            if nq:
                                act.wait_ge(pv, nq)
                            w = L - j * P
                            act.activation(PT[:, c, off[j]:off[j] + w], p2[:, n % 3, 0:w], ACT.Exp, scale=HD ** -0.5).then_inc(ex_d, 1)
                    act.wait_ge(pv, nq + 1)
                    if nq >= 2:
                        act.wait_ge(bc, nq - 1)
                        act.wait_ge(on_d, nq - 1)
                    act.activation(oT[:, nq % 2, :], po[:], ACT.Copy).then_inc(oT_d, 1)

            def output(b):
                for i in range(TH):
                    n = b * TH + i
                    act.wait_ge(fo, n + 1)
                    act.activation(s_acc[:, n, :], pf[:], ACT.Copy).then_inc(f_d, 1)

            for u in range(NU):
                weigh(u)
                if u % UB == UB - 1:
                    output(u // UB)

        @block.gpsimd
        def _(pool):
            pass

        @block.vector
        def _(dve):
            for i in range(2):
                dve.memset(KS[i][KB:KR, :, :], 1.0).then_inc(ones_d, 1)
            dve.wait_ge(ldc, 64)
            dve.tensor_copy(maskT[:], maskf[:]).then_inc(ones_d, 1)
            dve.tensor_copy(identb[:], ident[:]).then_inc(ones_d, 1)

            def maxima(u):
                for h in range(HU):
                    for i in range(TH):
                        n = (u * HU + h) * TH + i
                        dve.wait_ge(s1, n + 1)
                        if n >= 2:
                            dve.wait_ge(mx_d, n - 1)
                        if h == 0 and u:
                            dve.wait_ge(mt, u)
                        w = (i + 1) * P
                        dve.tensor_tensor_reduce(junk[:, n % 2, 0:w], p1[:, n % 2, 0:w], mask[:, L - w:L], 1.0, NEG,
                                                 ALU.add, ALU.max, mx[:, i, h:h + 1]).then_inc(mx_d, 1)
                dve.wait_ge(mt, u + 1)
                if u:
                    dve.wait_ge(np3_d, u)
                    dve.wait_ge(ldm[(u - 1) % 2], 48 * ((u - 1) // 2 + 1))
                dve.tensor_scalar(nm[:], p1[0:HU, 0, :], -1.0, None, ALU.mult).then_inc(nm_d, 1)
                dve.wait_ge(nm_d, u + 1)
                dve.tensor_copy(nparts[:, 0, :], nm[:]).then_inc(np1_d, 1)
                dve.wait_ge(np1_d, u + 1)
                dve.tensor_tensor(nr[:], nm[:], nparts[:, 0, :], ALU.subtract).then_inc(nr_d, 1)
                dve.wait_ge(nr_d, u + 1)
                dve.tensor_copy(nparts[:, 1, :], nr[:]).then_inc(np2_d, 1)
                dve.wait_ge(np2_d, u + 1)
                dve.tensor_tensor(nparts[:, 2, :], nr[:], nparts[:, 1, :], ALU.subtract).then_inc(np3_d, 1)

            def normalise(nq):
                dve.wait_ge(bc, nq + 1)
                if nq >= 2:
                    dve.wait_ge(on_d, nq - 1)
                dve.reciprocal(rb[:, nq % 2, :], pb[:]).then_inc(rb_d, 1)
                dve.wait_ge(rb_d, nq + 1)
                if nq >= HN // 4 and nq % (HN // 4) == 0:
                    dve.wait_ge(fo, TH * (nq // (HN // 4)))
                dve.tensor_tensor(on[:, nq % (HN // 4), :], oT[:, nq % 2, :], rb[:, nq % 2, :], ALU.mult).then_inc(on_d, 1)

            maxima(0)
            for u in range(NU):
                if u + 1 < NU:
                    maxima(u + 1)
                for quad in range(HU // 4):
                    normalise(u * (HU // 4) + quad)


def adapter_phase(nc, w_r, w_a, w_b, xnT, ident, g_dram, s_acc, x_res, out):
    NA, TOP, RK = 64, 16, 16
    with ExitStack() as ctx:
        sb = lambda n, s, d=F32: ctx.enter_context(nc.sbuf_tensor(f"ad_{n}", s, d))
        sem = phase_semaphores(nc, ctx, "ad")
        KT = NA * RK // P
        wr = sb("wr", [P, KD, NA])
        wa = sb("wa", [P, KD, NA * RK])
        wb = sb("wb", [P, KT, DM])
        lgT = sb("lgT", [NA, T])
        lg = sb("lg", [P, TT, NA])
        v8 = sb("v8", [P, TT, 2, 8])
        rest = sb("rest", [P, TT, 2, NA])
        sh = sb("sh", [P, TT, NA])
        ex = sb("ex", [P, TT, NA])
        tk = sb("tk", [P, TT, NA])
        sm = sb("sm", [P, TT, 1])
        gT = sb("gT", [NA, T])
        gb = sb("gb", [P, 2, T])
        hs = sb("hs", [P, KT, T])
        ga = sb("ga", [P, 2, DM])
        pr = sb("pr", [P, 2, DM])
        res = sb("res", [P, 2, DM])
        pl = ctx.enter_context(nc.psum_tensor("ad_pl", [P, 2, 512], F32))
        ph = ctx.enter_context(nc.psum_tensor("ad_ph", [P, 2, 512], F32))
        pf = ctx.enter_context(nc.psum_tensor("ad_pf", [P, 2, 512], F32))
        ld_r, ld_a, ld_b, links = sem("ld_r"), sem("ld_a"), sem("ld_b"), sem("links")
        ld_g = [sem("ld_g0"), sem("ld_g1")]
        st = [sem("st0"), sem("st1")]
        lp, lT_d, tr, lg_d, ch, ex_d, sh_d, gt, gT_d, g_st, hp, hs_d, fp, ga_d, pr_d, re_d = (sem(n) for n in (
            "lp", "lT_d", "tr", "lg_d", "ch", "ex_d", "sh_d", "gt", "gT_d", "g_st", "hp", "hs_d", "fp", "ga_d", "pr_d", "re_d"))
        block = ctx.enter_context(nc.Block())

        @block.sync
        def _(sp):
            sp.dma_start(wr[:].rearrange("p k n -> p (k n)"), w_r).then_inc(ld_r, 16)
            sp.dma_start(wa[:].rearrange("p k n -> p (k n)"), w_a).then_inc(ld_a, 16)
            sp.dma_start(wb[:].rearrange("p k n -> p (k n)"), w_b).then_inc(ld_b, 16)
            sp.wait_ge(gT_d, TT)
            sp.dma_start(g_dram, gT[:]).then_inc(g_st, 16)
            sp.wait_ge(g_st, 16)
            for i in range(KT):
                if i >= 2:
                    sp.wait_ge(hs_d, NB * (i - 1))
                for a in range(NA // KT):
                    r = i * (NA // KT) + a
                    sp.dma_start(gb[a * RK:(a + 1) * RK, i % 2, :], g_dram[r].partition_broadcast(RK)).then_inc(ld_g[i % 2], 16)
            for i in range(TT):
                sp.wait_ge(re_d, i + 1)
                sp.dma_start(out[i * P:(i + 1) * P, :], res[:, i % 2, :]).then_inc(st[i % 2], 16)
            for i in range(2):
                sp.wait_ge(st[i], 16 * TT // 2)

        @block.tensor
        def _(pe):
            pe.wait_ge(ld_r, 16)
            for b in range(NB):
                for k in range(KD):
                    last = pe.matmul(pl[0:NA, b, :], wr[:, k, :], xnT[:, k, b * L:(b + 1) * L], start=(k == 0), stop=(k == KD - 1))
                last.then_inc(lp, 1)
            for i in range(TT):
                pe.wait_ge(lT_d, NB)
                if i >= 2:
                    pe.wait_ge(lg_d, i - 1)
                pe.transpose(pl[:, i % 2, 0:NA], lgT[:, i * P:(i + 1) * P], ident[0:NA, 0:NA]).then_inc(tr, 1)
            for i in range(TT):
                pe.wait_ge(ch, 1)
                if i < 2:
                    pe.wait_ge(lg_d, TT)
                else:
                    pe.wait_ge(gT_d, i - 1)
                pe.transpose(pl[0:NA, i % 2, 0:P], tk[:, i, :], ident[:]).then_inc(gt, 1)
            pe.wait_ge(ld_a, 16)
            for i in range(KT):
                for b in range(NB):
                    n = i * NB + b
                    if n >= 2:
                        pe.wait_ge(hs_d, n - 1)
                    for k in range(KD):
                        last = pe.matmul(ph[:, n % 2, :], wa[:, k, i * P:(i + 1) * P], xnT[:, k, b * L:(b + 1) * L],
                                         start=(k == 0), stop=(k == KD - 1))
                    last.then_inc(hp, 1)
            pe.wait_ge(ld_b, 16)
            pe.wait_ge(hs_d, KT * NB)
            for i in range(TT):
                if i >= 2:
                    pe.wait_ge(ga_d, i - 1)
                for k in range(KT):
                    last = pe.matmul(pf[:, i % 2, :], hs[:, k, i * P:(i + 1) * P], wb[:, k, :], start=(k == 0), stop=(k == KT - 1))
                last.then_inc(fp, 1)

        @block.scalar
        def _(act):
            for b in range(NB):
                act.wait_ge(lp, b + 1)
                act.activation(lgT[:, b * L:(b + 1) * L], pl[0:NA, b, :], ACT.Copy).then_inc(lT_d, 1)
            act.wait_ge(sh_d, TT)
            act.activation(ex[:], sh[:], ACT.Exp).then_inc(ex_d, 1)
            for i in range(TT):
                act.wait_ge(fp, i + 1)
                if i >= 2:
                    act.wait_ge(pr_d, i - 1)
                act.activation(ga[:, i % 2, :], pf[:, i % 2, :], ACT.Silu, scale=2.0).then_inc(ga_d, 1)

        @block.gpsimd
        def _(pool):
            pass

        @block.vector
        def _(dve):
            chain, count = links, [0]

            def link(ins):
                count[0] += 1
                ins.then_inc(chain, 1)
                dve.wait_ge(chain, count[0])

            for i in range(TT):
                dve.wait_ge(tr, i + 1)
                dve.tensor_copy(lg[:, i, :], pl[:, i % 2, 0:NA]).then_inc(lg_d, 1)
            for i in range(TT):
                dve.wait_ge(lg_d, i + 1)
                link(dve.max(v8[:, i, 0, :], lg[:, i, :]))
                dve.tensor_scalar(sh[:, i, :], lg[:, i, :], v8[:, i, 0, 0:1], None, ALU.subtract).then_inc(sh_d, 1)
                link(dve.match_replace(rest[:, i, 0, :], v8[:, i, 0, :], lg[:, i, :], NEG))
                link(dve.max(v8[:, i, 1, :], rest[:, i, 0, :]))
                link(dve.match_replace(rest[:, i, 1, :], v8[:, i, 1, :], rest[:, i, 0, :], NEG))
            link(dve.tensor_tensor(tk[:], lg[:], rest[:, :, 1, :], ALU.not_equal))
            dve.wait_ge(ex_d, 1)
            link(dve.tensor_tensor(tk[:], tk[:], ex[:], ALU.mult))
            link(dve.tensor_reduce(sm[:], tk[:], AX.X, ALU.add))
            link(dve.reciprocal(sm[:], sm[:]))
            dve.tensor_tensor(tk[:], tk[:], sm[:].to_broadcast([P, TT, NA]), ALU.mult).then_inc(ch, 1)
            for i in range(TT):
                dve.wait_ge(gt, i + 1)
                dve.tensor_copy(gT[:, i * P:(i + 1) * P], pl[0:NA, i % 2, 0:P]).then_inc(gT_d, 1)
            for i in range(KT):
                dve.wait_ge(ld_g[i % 2], 16 * (NA // KT) * (i // 2 + 1))
                for b in range(NB):
                    dve.wait_ge(hp, i * NB + b + 1)
                    dve.tensor_tensor(hs[:, i, b * L:(b + 1) * L], ph[:, b, :], gb[:, i % 2, b * L:(b + 1) * L], ALU.mult).then_inc(hs_d, 1)
            for i in range(TT):
                dve.wait_ge(ga_d, i + 1)
                if i >= 2:
                    dve.wait_ge(re_d, i - 1)
                dve.tensor_tensor(pr[:, i % 2, :], s_acc[:, i, :], ga[:, i % 2, :], ALU.mult).then_inc(pr_d, 1)
                dve.wait_ge(pr_d, i + 1)
                if i >= 2:
                    dve.wait_ge(st[i % 2], 16 * (i // 2))
                dve.tensor_tensor(res[:, i % 2, :], pr[:, i % 2, :], x_res[:, i, :], ALU.add).then_inc(re_d, 1)


def build_program(nc, x, w_small, small_bias, a_log, iota16, ident_dram, ident8, w_x, w_bc, w_gate, w_out,
                  conv_par, d_par, n_par, w_gu, w_dn, w_q, w_k, w_v, w_o, rot, cos, sin, mask, maskT, sel,
                  w_r, w_a, w_b, out):
    scratch = lambda n, s, d=F32: nc.dram_tensor(n, s, d, kind="Internal").ap()
    daz_dram = scratch("daz_dram", (TT, H, P))
    din_dram = scratch("din_dram", (TT, H, P))
    comb_dram = scratch("comb_dram", (NE, T))
    q_parts = scratch("q_parts", (NB, 3, DM, L), BF16)
    k_parts = scratch("k_parts", (NB, 3, DM, L), BF16)
    g_dram = scratch("g_dram", (64, T))
    with ExitStack() as ctx:
        sb = lambda n, s, d=F32: ctx.enter_context(nc.sbuf_tensor(n, s, d))
        ident = sb("ident", [P, P])
        xnT = sb("xnT", [P, KD, T])
        s_acc = sb("s_acc", [P, TT, DM])
        with nc.semaphore("ld0") as ld0, nc.Block() as block:
            @block.sync
            def _(sp):
                sp.dma_start(ident[:], ident_dram).then_inc(ld0, 16)
                sp.wait_ge(ld0, 16)
        layernorm_phase(nc, x, xnT, ident, None, "n0")
        with nc.sbuf_tensor("dtT", [P, TT, H], F32) as dtT:
            small_phase(nc, w_small, small_bias, a_log, iota16, xnT, ident, dtT, daz_dram, din_dram, comb_dram)
            ssm_phase(nc, w_x, w_bc, w_gate, w_out, conv_par, d_par, n_par, ident8, xnT, ident, dtT, daz_dram, din_dram, s_acc)
        x1 = sb("x1", [P, TT, DM])
        with nc.sbuf_tensor("f_acc", [P, TT, DM], F32) as f_acc:
            moe_phase(nc, w_gu, w_dn, comb_dram, xnT, f_acc)
            layernorm_phase(nc, x, xnT, ident, x1, "n1", combine=(x, s_acc, f_acc, 1.0))
        with nc.sbuf_tensor("V1", [P, TT, HN, 2 * HD], F32) as V1:
            qkv_phase(nc, w_q, w_k, w_v, rot, cos, sin, xnT, V1, q_parts, k_parts)
            attention_phase(nc, q_parts, k_parts, V1, w_o, mask, maskT, sel, ident, s_acc)
        adapter_phase(nc, w_r, w_a, w_b, xnT, ident, g_dram, s_acc, x1, out)


def layouts(d):
    a = {k: np.asarray(v) for k, v in d.items()}
    W = a["L0_attn_in_proj_w"]
    I, GN = H * PH, G * NS

    def kmajor(rows):
        return rows.reshape(-1, KD, P).transpose(2, 1, 0)

    def per_group(lo, n):
        return W[lo:lo + G * n].reshape(G, n, KD, P).transpose(0, 3, 2, 1)

    conv = np.concatenate([a["L0_attn_conv_weight"], a["L0_attn_conv_bias"][:, None]], 1)
    cx = conv[:I].reshape(G, MG, P, KC + 1)
    cB = conv[I:I + GN].reshape(G, 1, P, KC + 1)
    cC = conv[I + GN:].reshape(G, 1, P, KC + 1)
    shared = a["L0_ffn_shared_w_gate_up"].reshape(2, 4, P, DM).transpose(1, 0, 2, 3).reshape(4, 2 * P, DM)
    gu = np.concatenate([a["L0_ffn_w_gate_up"], shared], 0)
    shared_dn = a["L0_ffn_shared_w_down"].reshape(DM, 4, P).transpose(1, 2, 0)
    dn = np.concatenate([a["L0_ffn_w_down"].transpose(0, 2, 1), shared_dn], 0)
    theta = (1.0 / np.float32(10000.0) ** (np.arange(0, HD, 2, dtype=np.float32) / np.float32(HD))).astype(np.float32)
    angle = np.outer(np.arange(L, dtype=np.float32), theta).astype(np.float32)
    angle = np.tile(np.concatenate([angle, angle], 1).T, (P // HD, 1))
    R = np.zeros((P, P), np.float32)
    for p in range(P):
        base, i = p - p % HD, p % HD
        if i < HD // 2:
            R[base + i + HD // 2, p] = -1.0
        else:
            R[base + i - HD // 2, p] = 1.0
    mask = np.zeros((P, L), np.float32)
    mask[:, L - P:] = np.where(np.arange(P)[None, :] > np.arange(P)[:, None], np.float32(-1e30), np.float32(0))
    maskT = np.where(np.arange(P)[:, None] > np.arange(P)[None, :], np.float32(-1e30), np.float32(0))
    sel = np.zeros((P, P), np.float32)
    for p in range(P):
        sel[p - p % 32 + HD, p] = 1.0
    wo = np.zeros((P, HN // 4, DM), np.float32)
    wo.reshape(4, 32, HN // 4, DM)[:, :HD] = a["L1_attn_wo"].reshape(DM, HN // 4, 4, HD).transpose(2, 3, 1, 0)
    arr = {
        "x": a["L0_attn_hidden_states"].reshape(T, DM),
        "w_small": kmajor(np.concatenate([W[-H:], a["L0_ffn_gate_w"]], 0)),
        "small_bias": a["L0_attn_dt_bias"][:, None],
        "a_log": a["L0_attn_A_log"][:, None],
        "iota16": np.tile(np.arange(16, dtype=np.float32), (P, 1)),
        "ident_dram": np.eye(P, dtype=np.float32),
        "ident8": np.tile(np.eye(P, dtype=np.float32), (1, HG)),
        "w_x": per_group(I, CG).reshape(G, P, -1),
        "w_bc": np.concatenate([per_group(2 * I, NS), per_group(2 * I + GN, NS)], 3).reshape(G, P, -1),
        "w_gate": per_group(0, CG).reshape(G, P, -1),
        "w_out": a["L0_attn_out_proj_w"].reshape(DM, G, MG, P).transpose(1, 3, 2, 0).reshape(G, P, -1),
        "conv_par": np.concatenate([cx, cB, cC], 1).transpose(0, 2, 1, 3).reshape(G, P, -1),
        "d_par": np.repeat(a["L0_attn_D"], PH).reshape(G, MG, P).transpose(0, 2, 1),
        "n_par": a["L0_attn_norm_weight"].reshape(G, MG, P).transpose(0, 2, 1),
        "w_gu": gu.reshape(EC, EB, 2 * P, KD, P).transpose(0, 4, 3, 1, 2).reshape(EC, P, -1),
        "w_dn": dn.reshape(EC, EB, P, DM).transpose(0, 2, 1, 3).reshape(EC, P, -1),
        "w_q": kmajor(a["L1_attn_wq"]).reshape(P, -1),
        "w_k": kmajor(a["L1_attn_wk"]).reshape(P, -1),
        "w_v": kmajor(a["L1_attn_wv"]).reshape(P, -1),
        "w_o": wo.reshape(P, -1),
        "rot": R,
        "cos": np.cos(angle).astype(np.float32),
        "sin": np.sin(angle).astype(np.float32),
        "mask": mask,
        "maskT": maskT,
        "sel": sel,
        "w_r": kmajor(a["L1_ffn_Wr"]).reshape(P, -1),
        "w_a": kmajor(a["L1_ffn_A"].reshape(-1, DM)).reshape(P, -1),
        "w_b": a["L1_ffn_B"].transpose(0, 2, 1).reshape(8, P, DM).transpose(1, 0, 2).reshape(P, -1),
    }
    return {k: np.ascontiguousarray(v) for k, v in arr.items()}


def kernel(**inputs):
    import concourse.bacc as bacc
    from concourse.bass_utils import run_bass_kernel_spmd

    nc = bacc.Bacc("TRN2", target_bir_lowering=False, num_devices=1)
    arrays = layouts(inputs)
    args = [nc.dram_tensor(k, v.shape, mybir.dt.from_np(v.dtype), kind="ExternalInput").ap() for k, v in arrays.items()]
    args.append(nc.dram_tensor("out", (T, DM), F32, kind="ExternalOutput").ap())
    build_program(nc, *args)
    r = run_bass_kernel_spmd(nc, [arrays], core_ids=[0])
    return r.results[0]["out"].reshape(NB, L, DM)
```

```python
from contextlib import ExitStack

import numpy as np

import concourse.bass as bass
from concourse import mybir
from concourse.alu_op_type import AluOpType as ALU

ACT = mybir.ActivationFunctionType
F32 = mybir.dt.float32
F32R = mybir.dt.float32r
BF16 = mybir.dt.bfloat16
U32 = mybir.dt.uint32
AX = mybir.AxisListType

P = 128
NB, L, DM = 2, 512, 512
T = NB * L
TT = T // P
KD = DM // P
EPS = 1e-5

G, H, PH, NS, KC = 8, 64, 64, 128, 4
HG = H // G
CG = HG * PH
MG = CG // P
MC = MG + 2
CH = L // P
HT = H + 16

NPI = MG + MC + MG

NE, EB, EC = 20, 4, 5

HN, HD, HU = 32, 16, 4
TH = L // P
PTW = sum(L - P * j for j in range(TH))
BLOCKS = [(0, 0), (1, 0), (2, 0), (0, 1), (1, 1), (0, 2)]
KB = HD * len(BLOCKS)
KR = KB + 3
NEG = -3.0e38


def phase_semaphores(nc, ctx, tag):
    taken = []

    def sem(name):
        taken.append(nc.alloc_semaphore(f"{tag}_{name}"))
        return taken[-1]

    def end():
        nc.clear_and_free_semaphores(taken)
        nc.all_engine_barrier()

    ctx.callback(end)
    return sem


def matmul3(pe, out, lhs, rhs, start, stop):
    pe.matmul(out, lhs[0], rhs[0], start=start, stop=False)
    pe.matmul(out, lhs[0], rhs[1], start=False, stop=False)
    return pe.matmul(out, lhs[1], rhs[0], start=False, stop=stop)


def both(parts, *index):
    return tuple(p[index] for p in parts)


def layernorm_phase(nc, x_dram, xT, ident, x_res, tag, combine=None):
    with ExitStack() as ctx:
        sb = lambda n, s, d=F32: ctx.enter_context(nc.sbuf_tensor(f"{tag}_{n}", s, d))
        sem = phase_semaphores(nc, ctx, tag)
        xt = x_res if x_res is not None else sb("x", [P, TT, DM])
        xn = sb("xn", [P, 2, DM])
        gate = sb("gate", [P, 2, DM])
        prod = sb("prod", [P, 2, DM])
        stats = sb("stats", [P, TT, 6])
        mv = sb("mv", [P, TT, 2])
        ve = sb("ve", [P, TT])
        half = sb("half", [P, TT])
        rstd = sb("rstd", [P, TT])
        ps = ctx.enter_context(nc.psum_tensor(f"{tag}_ps", [P, 2, 512], F32))
        loaded = [sem(f"loaded{i}") for i in range(TT)]
        half_set, gate_done, prod_done, x_done = sem("half_set"), sem("gate_done"), sem("prod_done"), sem("x_done")
        stats_done, mv_done, ve_done, rstd_done = sem("stats_done"), sem("mv_done"), sem("ve_done"), sem("rstd_done")
        xn_done, tr_done, hi_done, out_done = sem("xn_done"), sem("tr_done"), sem("hi_done"), sem("out_done")
        block = ctx.enter_context(nc.Block())
        xv = x_dram.rearrange("(n p) d -> n p d", p=P)

        @block.sync
        def _(sp):
            for i in range(TT):
                sp.dma_start(xt[:, i, :], xv[i]).then_inc(loaded[i], 16)

        @block.gpsimd
        def _(pool):
            pool.wait_ge(half_set, 1)
            pool.wait_ge(ve_done, TT)
            pool.tensor_tensor(rstd[:], ve[:], half[:], ALU.pow).then_inc(rstd_done, 1)

        @block.scalar
        def _(act):
            if combine is not None:
                _, s, f, fscale = combine
                for i in range(TT):
                    if i >= 2:
                        act.wait_ge(prod_done, i - 1)
                    act.activation(gate[:, i % 2, :], f[:, i, :], ACT.Silu, scale=fscale).then_inc(gate_done, 1)
            for i in range(TT):
                act.wait_ge(tr_done, i + 1)
                act.activation(xT[0][:, :, i * P:(i + 1) * P],
                               ps[:, i % 2, :].rearrange("p (k t) -> p k t", k=KD), ACT.Copy).then_inc(hi_done, 1)

        @block.vector
        def _(dve):
            dve.memset(half[:], -0.5).then_inc(half_set, 1)
            for i in range(TT):
                dve.wait_ge(loaded[i], 16)
                if combine is not None:
                    _, s, f, _ = combine
                    dve.wait_ge(gate_done, i + 1)
                    if i >= 2:
                        dve.wait_ge(x_done, i - 1)
                    dve.tensor_tensor(prod[:, i % 2, :], s[:, i, :], gate[:, i % 2, :], ALU.mult).then_inc(prod_done, 1)
                    dve.wait_ge(prod_done, i + 1)
                    dve.tensor_tensor(xt[:, i, :], xt[:, i, :], prod[:, i % 2, :], ALU.add).then_inc(x_done, 1)
                    dve.wait_ge(x_done, i + 1)
                dve.bn_stats(stats[:, i, :], xt[:, i, :]).then_inc(stats_done, 1)
                dve.wait_ge(stats_done, i + 1)
                dve.bn_aggr(mv[:, i, :], stats[:, i, :]).then_inc(mv_done, 1)
                dve.wait_ge(mv_done, i + 1)
                dve.tensor_scalar(ve[:, i:i + 1], mv[:, i, 1:2], EPS, None, ALU.add).then_inc(ve_done, 1)
            dve.wait_ge(rstd_done, 1)

            def low_part(i):
                dve.wait_ge(hi_done, i + 1)
                part = (slice(None), slice(None), slice(i * P, (i + 1) * P))
                dve.tensor_tensor(xT[1][part], ps[:, i % 2, :].rearrange("p (k t) -> p k t", k=KD),
                                  xT[0][part].bitcast(F32), ALU.subtract).then_inc(out_done, 1)

            for i in range(TT):
                if i >= 2:
                    dve.wait_ge(tr_done, i - 1)
                dve.tensor_scalar(xn[:, i % 2, :], xt[:, i, :], mv[:, i, 0:1], rstd[:, i:i + 1],
                                  ALU.subtract, ALU.mult).then_inc(xn_done, 1)
                if i:
                    low_part(i - 1)
            low_part(TT - 1)

        @block.tensor
        def _(pe):
            for i in range(TT):
                pe.wait_ge(xn_done, i + 1)
                if i >= 2:
                    pe.wait_ge(out_done, i - 1)
                for k in range(KD):
                    last = pe.transpose(ps[:, i % 2, k * P:(k + 1) * P], xn[:, i % 2, k * P:(k + 1) * P], ident[:])
                last.then_inc(tr_done, 1)


def small_phase(nc, w_small, small_bias, a_log, iota16, xT, ident, dtT, daz_dram, din_dram, comb_dram):
    with ExitStack() as ctx:
        sb = lambda n, s, d=F32: ctx.enter_context(nc.sbuf_tensor(f"sm_{n}", s, d))
        sem = phase_semaphores(nc, ctx, "sm")
        w = sb("w", [P, KD, HT])
        w2 = [sb(f"w{i}", [P, KD, HT], F32R) for i in range(2)]
        bias = sb("bias", [H, 1])
        alog = sb("alog", [H, 1])
        ea = sb("ea", [H, 1])
        nea = sb("nea", [H, 1])
        io = sb("io", [P, 16])
        z = sb("z", [HT, T])
        v = sb("v", [H, T])
        ab = sb("ab", [H, T])
        e = sb("e", [H, T])
        u = sb("u", [H, T])
        lnu = sb("lnu", [H, T])
        d = sb("d", [H, T])
        r = sb("r", [H, T])
        mx = sb("mx", [H, T])
        dA = sb("dA", [H, T])
        first = sb("first", [H, T])
        din = sb("din", [H, T])
        lg = sb("lg", [P, TT, 16])
        top = sb("top", [P, TT, 8])
        idx = sb("idx", [P, TT, 8], U32)
        idf = sb("idf", [P, TT, 8])
        gap = sb("gap", [P, TT, 1])
        eg = sb("eg", [P, TT, 1])
        den = sb("den", [P, TT, 1])
        wt = sb("wt", [P, TT, 2])
        oh = sb("oh", [P, TT, 2, 16])
        comb = sb("comb", [P, TT, 16])
        combT = sb("combT", [16, T])
        ones = sb("ones", [4, T])
        ps = ctx.enter_context(nc.psum_tensor("sm_ps", [P, 2, 512], F32))
        pt = ctx.enter_context(nc.psum_tensor("sm_pt", [P, 2, 512], F32))
        pc = ctx.enter_context(nc.psum_tensor("sm_pc", [P, 2, 512], F32))
        w2_done = sem("w2_done")
        ld, pe_z, a_z, tr, ct, stored = (sem(n) for n in ("ld", "pe_z", "a_z", "tr", "ct", "stored"))
        scan_done, ct_done, ones_set = sem("scan_done"), sem("ct_done"), sem("ones_set")
        ea_done, nea_done, e_done, ln_done, dA_done, eg_done, ab_done = (sem(n) for n in (
            "ea_done", "nea_done", "e_done", "ln_done", "dA_done", "eg_done", "ab_done"))
        v_done, chain, dt_done, dtT_done, lg_done, comb_done, gap_done, z_free = (sem(n) for n in (
            "v_done", "chain", "dt_done", "dtT_done", "lg_done", "comb_done", "gap_done", "z_free"))
        block = ctx.enter_context(nc.Block())

        @block.sync
        def _(sp):
            for dst, src in ((w[:], w_small), (bias[:], small_bias), (alog[:], a_log), (io[:], iota16)):
                sp.dma_start(dst, src).then_inc(ld, 16)
            sp.wait_ge(scan_done, 1)
            sp.dma_start(daz_dram.rearrange("c h t -> h c t"), dA[:].rearrange("h (c t) -> h c t", t=P)).then_inc(stored, 16)
            sp.dma_start(din_dram.rearrange("c h t -> h c t"), din[:].rearrange("h (c t) -> h c t", t=P)).then_inc(stored, 16)
            sp.wait_ge(ct_done, TT)
            sp.dma_start(comb_dram[0:16, :], combT[:]).then_inc(stored, 16)
            sp.wait_ge(ones_set, 1)
            sp.dma_start(comb_dram[16:20, :], ones[:]).then_inc(stored, 16)
            sp.wait_ge(stored, 64)

        @block.tensor
        def _(pe):
            pe.wait_ge(w2_done, 2)
            for b in range(NB):
                for k in range(KD):
                    last = matmul3(pe, ps[0:HT, b, :], both(w2, slice(None), k),
                                   both(xT, slice(None), k, slice(b * L, (b + 1) * L)), k == 0, k == KD - 1)
                last.then_inc(pe_z, 1)
            pe.wait_ge(dt_done, 1)
            pe.wait_ge(a_z, NB)
            for i in range(TT):
                if i >= 2:
                    pe.wait_ge(lg_done, i - 1)
                pe.transpose(pt[:, i % 2, 0:HT], z[:, i * P:(i + 1) * P], ident[0:HT, 0:HT]).then_inc(tr, 1)
            for i in range(TT):
                pe.wait_ge(comb_done, i + 1)
                if i >= 2:
                    pe.wait_ge(ct_done, i - 1)
                pe.transpose(pc[0:16, i % 2, 0:P], comb[:, i, :], ident[:]).then_inc(ct, 1)

        @block.scalar
        def _(act):
            act.wait_ge(ld, 64)
            act.activation(ea[:], alog[:], ACT.Exp).then_inc(ea_done, 1)
            act.wait_ge(ea_done, 1)
            act.activation(nea[:], ea[:], ACT.Copy, scale=-1.0).then_inc(nea_done, 1)
            for b in range(NB):
                act.wait_ge(pe_z, b + 1)
                act.activation(z[H:HT, b * L:(b + 1) * L], ps[H:HT, b, :], ACT.Copy).then_inc(a_z, 1)
            act.wait_ge(v_done, 2)
            act.activation(ab[:], v[:], ACT.Abs).then_inc(ab_done, 1)
            act.wait_ge(ab_done, 1)
            act.activation(e[:], ab[:], ACT.Exp, scale=-1.0).then_inc(e_done, 1)
            act.wait_ge(chain, 1)
            act.activation(lnu[:], u[:], ACT.Ln).then_inc(ln_done, 1)
            act.wait_ge(dt_done, 1)
            act.wait_ge(nea_done, 1)
            act.activation(dA[:], z[0:H, :], ACT.Exp, scale=nea[:]).then_inc(dA_done, 1)
            act.wait_ge(gap_done, 1)
            act.activation(eg[:], gap[:], ACT.Exp).then_inc(eg_done, 1)

        @block.vector
        def _(dve):
            dve.memset(ones[:], 1.0).then_inc(ones_set, 1)
            dve.memset(first[:], 0.0).then_inc(z_free, 1)
            dve.wait_ge(ld, 64)
            dve.tensor_copy(w2[0][:], w[:]).then_inc(w2_done, 1)
            dve.wait_ge(w2_done, 1)
            dve.tensor_tensor(w2[1][:], w[:], w2[0][:].bitcast(F32), ALU.subtract).then_inc(w2_done, 1)
            for b in range(NB):
                dve.wait_ge(a_z, b + 1)
                dve.tensor_scalar(v[:, b * L:(b + 1) * L], ps[0:H, b, :], bias[:], None, ALU.add).then_inc(v_done, 1)
            dve.wait_ge(e_done, 1)
            dve.tensor_scalar(u[:], e[:], 1.0, None, ALU.add).then_inc(chain, 1)
            dve.wait_ge(chain, 1)
            dve.scalar_tensor_tensor(d[:], u[:], -1.0, e[:], ALU.add, ALU.subtract).then_inc(chain, 1)
            dve.reciprocal(r[:], u[:]).then_inc(chain, 1)
            dve.wait_ge(chain, 3)
            dve.tensor_tensor(d[:], d[:], r[:], ALU.mult).then_inc(chain, 1)
            dve.wait_ge(ln_done, 1)
            dve.wait_ge(v_done, 2)
            dve.scalar_tensor_tensor(mx[:], v[:], 0.0, lnu[:], ALU.max, ALU.add).then_inc(chain, 1)
            dve.wait_ge(chain, 5)
            dve.tensor_tensor(z[0:H, :], mx[:], d[:], ALU.subtract).then_inc(dt_done, 1)
            dve.wait_ge(dA_done, 1)
            dve.wait_ge(z_free, 1)
            dAc = dA[:].rearrange("h (c t) -> h c t", t=P)
            fc = first[:].rearrange("h (c t) -> h c t", t=P)
            dve.tensor_copy(fc[:, :, 0:1], dAc[:, :, 0:1]).then_inc(chain, 1)
            dve.wait_ge(chain, 6)
            dve.memset(dAc[:, :, 0:1], 0.0).then_inc(chain, 1)
            dve.wait_ge(chain, 7)
            dve.tensor_tensor_scan(din[:], dA[:], first[:], 0.0, ALU.mult, ALU.add).then_inc(scan_done, 1)
            for i in range(TT):
                dve.wait_ge(tr, i + 1)
                dve.tensor_copy(dtT[:, i, :], pt[:, i % 2, 0:H]).then_inc(dtT_done, 1)
                dve.tensor_copy(lg[:, i, :], pt[:, i % 2, H:HT]).then_inc(lg_done, 1)
            for i in range(TT):
                dve.wait_ge(lg_done, i + 1)
                dve.max(top[:, i, :], lg[:, i, :]).then_inc(chain, 1)
                dve.wait_ge(chain, 8 + 2 * i)
                dve.max_index(idx[:, i, :], top[:, i, :], lg[:, i, :]).then_inc(chain, 1)
            n = 7 + 2 * TT
            dve.wait_ge(chain, n)
            dve.tensor_copy(idf[:], idx[:]).then_inc(chain, 1)
            dve.tensor_tensor(gap[:], top[:, :, 1:2], top[:, :, 0:1], ALU.subtract).then_inc(gap_done, 1)
            dve.wait_ge(eg_done, 1)
            dve.tensor_scalar(den[:], eg[:], 1.0, None, ALU.add).then_inc(chain, 1)
            dve.wait_ge(chain, n + 2)
            dve.reciprocal(wt[:, :, 0:1], den[:]).then_inc(chain, 1)
            dve.wait_ge(chain, n + 3)
            dve.tensor_tensor(wt[:, :, 1:2], eg[:], wt[:, :, 0:1], ALU.mult).then_inc(chain, 1)
            dve.wait_ge(chain, n + 4)
            for i in range(TT):
                for j in range(2):
                    dve.tensor_scalar(oh[:, i, j, :], io[:], idf[:, i, j:j + 1], wt[:, i, j:j + 1],
                                      ALU.is_equal, ALU.mult).then_inc(chain, 1)
                dve.wait_ge(chain, n + 6 + 2 * i)
                dve.tensor_tensor(comb[:, i, :], oh[:, i, 0, :], oh[:, i, 1, :], ALU.add).then_inc(comb_done, 1)
            for i in range(TT):
                dve.wait_ge(ct, i + 1)
                dve.tensor_copy(combT[:, i * P:(i + 1) * P], pc[0:16, i % 2, 0:P]).then_inc(ct_done, 1)


def ssm_phase(nc, w_pieces, conv_par, d_par, n_par, xT, ident, dtT, daz_dram, din_dram, s_acc):
    with ExitStack() as ctx:
        sb = lambda n, s, d=F32: ctx.enter_context(nc.sbuf_tensor(f"ss_{n}", s, d))
        sem = phase_semaphores(nc, ctx, "ss")
        two = lambda n, s: [sb(f"{n}{i}", s, F32R) for i in range(2)]
        stage = sb("stage", [P, 2, DM])
        wx = two("wx", [P, MC, KD, P])
        wg = two("wg", [P, MG, KD, P])
        wo = two("wo", [P, MG, DM])
        cpar = sb("cpar", [P, MC, KC + 1])
        dpar = sb("dpar", [P, MG])
        npar = sb("npar", [P, MG])
        id8 = sb("id8", [P, HG, P], BF16)
        daz = sb("daz", [P, 2, HG * P])
        din = sb("din", [P, 2, HG, P])
        cv = sb("cv", [P, 2, L])
        xc = sb("xc", [P, MG, L])
        Bc = sb("Bc", [P, L])
        Cc = sb("Cc", [P, 2, L])
        xD = sb("xD", [P, MG, L])
        Bt = sb("Bt", [P, CH, NS])
        xdt = sb("xdt", [P, CH, CG])
        Lm = sb("Lm", [P, 2, HG * P])
        M = sb("M", [P, 2, HG, P])
        CD = sb("CD", [P, 2, HG, P])
        Xw = sb("Xw", [P, 2, CG])
        S = sb("S", [P, 2, CG])
        St = sb("St", [P, CG])
        y = sb("y", [P, 2, MG, P])
        ysq = sb("ysq", [P, MG, P])
        sg = sb("sg", [P, MG, L])
        zf = sb("zf", [P, MG, P])
        z = two("z", [P, 2, MG, P])
        ones = sb("ones", [P, 1])
        half = sb("half", [P, 1])
        var = sb("var", [P, CH])
        rstd = sb("rstd", [P, CH])
        pp = ctx.enter_context(nc.psum_tensor("ss_pp", [P, 2, 512], F32))
        pt = ctx.enter_context(nc.psum_tensor("ss_pt", [P, 2, 512], F32))
        pc = ctx.enter_context(nc.psum_tensor("ss_pc", [P, CH, P], F32))
        py = ctx.enter_context(nc.psum_tensor("ss_py", [P, 2, MG, P], F32))
        pss = ctx.enter_context(nc.psum_tensor("ss_ps", [P, 512], F32))

        ld_cp, ld_d, ld_n = (sem(n) for n in ("ld_cp", "ld_d", "ld_n"))
        ld_w = [sem("ld_w0"), sem("ld_w1")]
        ld_daz = [sem("ld_daz0"), sem("ld_daz1")]
        ld_din = [sem("ld_din0"), sem("ld_din1")]
        proj, gatep, tr, cb, ds, yp, ssq, outp = (sem(n) for n in (
            "proj", "gatep", "tr", "cb", "ds", "yp", "ssq", "outp"))
        acc, xc_d, xD_d, bt_d, sg_d, zh_d, hi_d = (sem(n) for n in (
            "acc", "xc_d", "xD_d", "bt_d", "sg_d", "zh_d", "hi_d"))
        tap, xdt_d, scan, m_d, s_d, y_d, zf_d, zl_d, o_d, var_d, cst, loo_d = (sem(n) for n in (
            "tap", "xdt_d", "scan", "m_d", "s_d", "y_d", "zf_d", "zl_d", "o_d", "var_d", "cst", "loo_d"))
        xw_d, cd_d, st_d, sq_d, r_d, lo_d = (sem(n) for n in ("xw_d", "cd_d", "st_d", "sq_d", "r_d", "lo_d"))
        block = ctx.enter_context(nc.Block())
        TAPS = KC - 1
        row = lambda dram, i: dram[bass.ds(i, 1)].rearrange("a p n -> p (a n)")
        O, X, GT = 0, MG, MG + MC
        LOW = MC + MG

        def order(g, k):
            return NPI * (g + (k < X)) + k - X

        def low_count(g, k):
            return LOW * g + k - X + 1

        def groups(eng, pair):
            pair(0, False)
            with eng.Fori(1, G - 1) as g:
                pair(g, False)
            pair(G - 1, True)

        def steps(eng, step):
            def pair(g, last):
                step(g, 0, (g, 1), last)
                step(g, 1, None if last else (g + 1, 0), last)
            groups(eng, pair)

        @block.sync
        def _(sp):
            def load_piece(g, k):
                if k < X:
                    sp.wait_ge(*((lo_d, low_count(g, k + NPI - 2)) if k < 2 else (loo_d, MG * g + k - 1)))
                elif k < X + 2:
                    if not isinstance(g, int) or g:
                        sp.wait_ge(loo_d, MG * (g - 1) + k - 1)
                else:
                    sp.wait_ge(lo_d, low_count(g, k - 2))
                sp.dma_start(stage[:, k % 2, :], row(w_pieces, NPI * g + k)).then_inc(ld_w[k % 2], 16)

            def load_conv(g):
                sp.wait_ge(tap, MC * TAPS * 2 * g)
                sp.dma_start(cpar[:].rearrange("p m k -> p (m k)"), row(conv_par, g)).then_inc(ld_cp, 16)

            def load_d(g):
                sp.wait_ge(xD_d, MG * 2 * g)
                sp.dma_start(dpar[:], row(d_par, g)).then_inc(ld_d, 16)

            def load_n(g):
                sp.wait_ge(loo_d, MG * g)
                sp.dma_start(npar[:], row(n_par, g)).then_inc(ld_n, 16)

            def load_daz(g, b, j):
                if not (isinstance(g, int) and g == 0 and b == 0 and j < 2):
                    sp.wait_ge(scan, CH * (2 * g + b) + j - 1)
                src = daz_dram[CH * b + j, bass.ds(HG * g, HG), :].rearrange("h t -> (h t)").partition_broadcast(P)
                sp.dma_start(daz[:, j % 2, :], src).then_inc(ld_daz[j % 2], 16)

            def load_din(g, b, j):
                s = 2 * g + b
                if j == 2:
                    sp.wait_ge(cd_d, (CH - 1) * s)
                else:
                    sp.wait_ge(st_d, 2 * s + (j == 3))
                src = din_dram[CH * b + j, bass.ds(HG * g, HG), :].rearrange("h t -> (h t)").partition_broadcast(P)
                sp.dma_start(din[:, (b + j - 1) % 2].rearrange("p h t -> p (h t)"), src).then_inc(ld_din[(b + j - 1) % 2], 16)

            load_conv(0)
            for k in range(X, NPI):
                load_piece(0, k)
                if k == X + 1:
                    load_d(0)
                    load_n(0)
                    load_daz(0, 0, 0)
                    load_daz(0, 0, 1)
                    load_din(0, 0, 1)
                    load_din(0, 0, 2)

            def pair(g, last, first=False):
                if not first:
                    load_d(g)
                    load_n(g)
                load_piece(g, O)
                load_piece(g, O + 1)
                load_daz(g, 0, 2)
                load_piece(g, O + 2)
                load_piece(g, O + 3)
                load_daz(g, 0, 3)
                if not last:
                    load_piece(g + 1, X)
                    load_piece(g + 1, X + 1)
                load_din(g, 0, 3)
                load_daz(g, 1, 0)
                if not last:
                    load_piece(g + 1, X + 2)
                    load_piece(g + 1, X + 3)
                load_daz(g, 1, 1)
                load_din(g, 1, 1)
                load_din(g, 1, 2)
                if not last:
                    load_piece(g + 1, X + 4)
                    load_piece(g + 1, X + 5)
                    load_conv(g + 1)
                load_daz(g, 1, 2)
                if not last:
                    load_piece(g + 1, GT)
                    load_piece(g + 1, GT + 1)
                load_daz(g, 1, 3)
                load_din(g, 1, 3)
                if not last:
                    load_daz(g + 1, 0, 0)
                    load_piece(g + 1, GT + 2)
                    load_piece(g + 1, GT + 3)
                    load_daz(g + 1, 0, 1)
                    load_din(g + 1, 0, 1)
                    load_din(g + 1, 0, 2)

            pair(0, False, first=True)
            with sp.Fori(1, G - 1) as g:
                pair(g, False)
            pair(G - 1, True)

        @block.tensor
        def _(pe):
            def project(g, b, m):
                if b == 0:
                    pe.wait_ge(lo_d, low_count(g, X + m))
                for k in range(KD):
                    last = matmul3(pe, pp[:, m % 2, :], both(wx, slice(None), m, k),
                                   both(xT, slice(None), k, slice(b * L, (b + 1) * L)), k == 0, k == KD - 1)
                last.then_inc(proj, 1)

            def gate(g, b, m):
                s = 2 * g + b
                if b == 0:
                    pe.wait_ge(lo_d, low_count(g, GT + m))
                if m < 2:
                    pe.wait_ge(tap, TAPS * (MC * s + m + MC - 1))
                else:
                    pe.wait_ge(sg_d, MG * s + m - 1)
                for k in range(KD):
                    last = matmul3(pe, pp[:, m % 2, :], both(wg, slice(None), m, k),
                                   both(xT, slice(None), k, slice(b * L, (b + 1) * L)), k == 0, k == KD - 1)
                last.then_inc(gatep, 1)

            def turn_x(g, b, j):
                s = 2 * g + b
                if j == 0:
                    pe.wait_ge(xc_d, MC * s + MG)
                if j < 2:
                    if not (isinstance(s, int) and s == 0):
                        pe.wait_ge(o_d, CH * s + j - 1)
                else:
                    pe.wait_ge(xdt_d, CH * s + j - 1)
                for m in range(MG):
                    last = pe.transpose(pt[:, j % 2, m * P:(m + 1) * P], xc[:, m, j * P:(j + 1) * P], ident[:])
                last.then_inc(tr, 1)

            for m in range(MC):
                if m >= 2:
                    pe.wait_ge(tap, TAPS * (m - 1))
                project(0, 0, m)
            turn_x(0, 0, 0)
            gate(0, 0, 0)

            def step(g, b, nxt, last_group):
                s = 2 * g + b

                def chunk(j):
                    if j < CH - 1:
                        pe.wait_ge(xw_d, (CH - 1) * s + j + 1)
                        if j == 0:
                            pe.wait_ge(bt_d, s + 1)
                        pe.wait_ge(s_d, (CH - 1) * s + j)
                        pe.matmul(pss[:], Bt[:, j, :], Xw[:, (b + j) % 2, :], start=True, stop=True).then_inc(ds, 1)
                    pe.wait_ge(m_d, CH * s + j + 1)
                    pe.wait_ge(var_d, CH * s + max(j - 1, 0))
                    if j:
                        pe.wait_ge(cd_d, (CH - 1) * s + j)
                        pe.wait_ge(s_d, (CH - 1) * s + j)
                    for m in range(MG):
                        for hh in range(2):
                            h = 2 * m + hh
                            dst = py[hh * PH:(hh + 1) * PH, j % 2, m, :]
                            last = pe.matmul(dst, xdt[:, j, h * PH:(h + 1) * PH], M[:, j % 2, h, :], start=True, stop=(j == 0))
                            if j:
                                last = pe.matmul(dst, S[:, (j - 1) % 2, h * PH:(h + 1) * PH], CD[:, (b + j - 1) % 2, h, :],
                                                 start=False, stop=True)
                    last.then_inc(yp, 1)

                def output(j):
                    pe.wait_ge(sq_d, 3 * (CH * s + j + 1))
                    pe.matmul(py[:, j % 2, 0, 0:1], ysq[:, 0, :], ones[:], start=True, stop=True).then_inc(ssq, 1)
                    if j == 0 and b == 0:
                        pe.wait_ge(loo_d, MG * (g + 1))
                    if j == 0:
                        pe.wait_ge(bt_d, s + 1)
                    elif j == 1:
                        pe.wait_ge(xdt_d, CH * (s + 1))
                    else:
                        pe.wait_ge(o_d, CH * s + j - 1)
                    pe.wait_ge(zl_d, CH * s + j + 1)
                    for m in range(MG):
                        last = matmul3(pe, pt[:, j % 2, :], both(z, slice(None), j % 2, m), both(wo, slice(None), m), m == 0, m == MG - 1)
                    last.then_inc(outp, 1)

                def next_tile(m):
                    if nxt is not None:
                        if m < 2:
                            pe.wait_ge(sg_d, MG * s + m + 3)
                        else:
                            pe.wait_ge(tap, TAPS * (MC * (s + 1) + m - 1))
                        project(*nxt, m)

                gate(g, b, 1)
                turn_x(g, b, 1)
                turn_x(g, b, 2)
                gate(g, b, 2)
                turn_x(g, b, 3)
                pe.wait_ge(xc_d, MC * (s + 1))
                pe.wait_ge(xdt_d, CH * s + 3)
                for j in range(CH):
                    last = pe.transpose(pt[:, 0, j * P:(j + 1) * P], Bc[:, j * P:(j + 1) * P], ident[:])
                last.then_inc(tr, 1)
                pe.wait_ge(m_d, CH * s)
                for j in range(CH):
                    last = pe.matmul(pc[:, j, :], Bc[:, j * P:(j + 1) * P], Cc[:, b, j * P:(j + 1) * P], start=True, stop=True)
                last.then_inc(cb, 1)
                gate(g, b, 3)
                chunk(0)
                next_tile(0)
                next_tile(1)
                chunk(1)
                output(0)
                next_tile(2)
                chunk(2)
                output(1)
                next_tile(3)
                next_tile(4)
                chunk(3)
                output(2)
                next_tile(5)
                if nxt is not None:
                    turn_x(*nxt, 0)
                    gate(*nxt, 0)
                output(3)

            steps(pe, step)

        @block.scalar
        def _(act):
            def conv_start(g, b, m):
                s = 2 * g + b
                act.wait_ge(proj, MC * s + m + 1)
                if m == 0:
                    act.wait_ge(ld_cp, 16 * (g + 1))
                act.wait_ge(xc_d, MC * s + max(m - 1, 0))
                act.activation(cv[:, m % 2, :], pp[:, m % 2, :], ACT.Identity, scale=cpar[:, m, KC - 1:KC],
                               bias=cpar[:, m, KC:KC + 1]).then_inc(acc, 1)

            def conv_silu(g, b, m, first=False):
                s = 2 * g + b
                act.wait_ge(tap, TAPS * (MC * s + m + 1))
                if m < MG:
                    dst = xc[:, m, :]
                    if not first:
                        act.wait_ge(tr, (CH + 1) * (s - 1) + CH)
                        act.wait_ge(xD_d, MG * s)
                elif m == MG:
                    dst = Bc[:]
                    if not first:
                        act.wait_ge(cb, s)
                else:
                    dst = Cc[:, b, :]
                    if not first:
                        act.wait_ge(cd_d, (CH - 1) * (s - 1))
                act.activation(dst, cv[:, m % 2, :], ACT.Silu).then_inc(xc_d, 1)

            def high(g, k, first=False):
                act.wait_ge(ld_w[k % 2], 16 * (NPI // 2 * (g + (k < X)) + (k - X) // 2 + 1))
                if k < X:
                    if k == 0:
                        act.wait_ge(outp, CH * 2 * g)
                        act.wait_ge(ld_n, 16 * (g + 1))
                    act.activation(wo[0][:, k, :], stage[:, k % 2, :], ACT.Copy, scale=npar[:, k:k + 1]).then_inc(hi_d, 1)
                    return
                if k < GT:
                    dst = wx[0][:, k - X].rearrange("p k n -> p (k n)")
                    if not first:
                        act.wait_ge(proj, MC * (2 * g - 1) + k - X + 1)
                else:
                    dst = wg[0][:, k - GT].rearrange("p k n -> p (k n)")
                    if not first:
                        act.wait_ge(gatep, MG * (2 * g - 1) + k - GT + 1)
                act.activation(dst, stage[:, k % 2, :], ACT.Copy).then_inc(hi_d, 1)

            def silu_gate(g, b, m):
                s = 2 * g + b
                act.wait_ge(gatep, MG * s + m + 1)
                if m == 0:
                    act.wait_ge(zf_d, CH * s)
                act.activation(sg[:, m, :], pp[:, m % 2, :], ACT.Silu).then_inc(sg_d, 1)

            high(0, X, True)
            for m in range(MC):
                high(0, X + m + 1, True)
                conv_start(0, 0, m)
                if m:
                    conv_silu(0, 0, m - 1, True)
            conv_silu(0, 0, MC - 1, True)
            silu_gate(0, 0, 0)
            for m in range(1, MG):
                high(0, GT + m, True)

            def step(g, b, nxt, last_group):
                s = 2 * g + b

                def high_z(j):
                    act.wait_ge(zf_d, CH * s + j + 1)
                    act.wait_ge(outp, CH * s + max(j - 1, 0))
                    act.activation(z[0][:, j % 2], zf[:], ACT.Copy).then_inc(zh_d, 1)

                def start(m):
                    if nxt is not None:
                        conv_start(*nxt, m)

                def finish(m):
                    if nxt is not None:
                        conv_silu(*nxt, m)

                def split(*pieces):
                    for k in pieces:
                        if k < X or not last_group:
                            high(g + (k >= X), k)

                if b == 0:
                    split(O, O + 1)
                silu_gate(g, b, 1)
                act.wait_ge(ld_d, 16 * (g + 1))
                act.wait_ge(y_d, CH * s)
                act.wait_ge(xc_d, MC * s + MG)
                for m in range(MG):
                    act.activation(xD[:, m, :], xc[:, m, :], ACT.Copy, scale=dpar[:, m:m + 1]).then_inc(xD_d, 1)
                silu_gate(g, b, 2)
                act.wait_ge(tr, (CH + 1) * (s + 1))
                act.wait_ge(ds, (CH - 1) * s)
                act.activation(Bt[:].rearrange("p c n -> p (c n)"), pt[:, 0, :], ACT.Copy).then_inc(bt_d, 1)
                if b == 0:
                    split(O + 2, O + 3)
                else:
                    split(X + 4, X + 5)
                silu_gate(g, b, 3)
                high_z(0)
                start(0)
                if b == 0:
                    split(X)
                else:
                    split(GT)
                start(1)
                finish(0)
                if b == 0:
                    split(X + 1)
                else:
                    split(GT + 1)
                finish(1)
                high_z(1)
                start(2)
                finish(2)
                if b == 0:
                    split(X + 2)
                else:
                    split(GT + 2)
                high_z(2)
                start(3)
                if b == 0:
                    split(X + 3)
                else:
                    split(GT + 3)
                start(4)
                finish(3)
                finish(4)
                high_z(3)
                start(5)
                finish(5)
                if nxt is not None:
                    silu_gate(*nxt, 0)

            steps(act, step)

        @block.vector
        def _(dve):
            dve.memset(ones[:], 1.0).then_inc(cst, 1)
            dve.memset(half[:], -0.5).then_inc(cst, 1)
            dve.memset(s_acc[:], 0.0).then_inc(cst, 1)
            for h in range(HG):
                dve.tensor_copy(id8[:, h, :], ident[:]).then_inc(cst, 1)

            def taps(g, b, m):
                s = 2 * g + b
                dve.wait_ge(acc, MC * s + m + 1)
                for i in range(1, KC):
                    if i > 1:
                        dve.wait_ge(tap, TAPS * (MC * s + m) + i - 1)
                    dve.scalar_tensor_tensor(cv[:, m % 2, i:], pp[:, m % 2, :L - i], cpar[:, m, KC - 1 - i:KC - i],
                                             cv[:, m % 2, i:], ALU.mult, ALU.add).then_inc(tap, 1)

            def x_dt(g, b, j):
                s = 2 * g + b
                dve.wait_ge(tr, (CH + 1) * s + j + 1)
                if j == 0:
                    dve.wait_ge(yp, CH * s)
                    dve.wait_ge(xw_d, (CH - 1) * s)
                dtb = dtT[:, CH * b + j, bass.ds(HG * g, HG)].unsqueeze(2).to_broadcast([P, HG, PH])
                dve.tensor_tensor(xdt[:, j, :].rearrange("p (h c) -> p h c", h=HG),
                                  pt[:, j % 2, :].rearrange("p (h c) -> p h c", h=HG), dtb, ALU.mult).then_inc(xdt_d, 1)

            def decays(g, b, j):
                s = 2 * g + b
                dve.wait_ge(ld_daz[j % 2], 16 * (2 * s + j // 2 + 1))
                dve.wait_ge(m_d, CH * s + max(j - 1, 0))
                dve.wait_ge(xw_d, (CH - 1) * s + max(j - 1, 0))
                dve.tensor_tensor_scan(Lm[:, j % 2, :], daz[:, j % 2, :], id8[:].rearrange("p h t -> p (h t)"), 0.0,
                                       ALU.mult, ALU.add).then_inc(scan, 1)

            for m in range(MC):
                taps(0, 0, m)
            dve.wait_ge(cst, 3 + HG)
            x_dt(0, 0, 0)
            decays(0, 0, 0)

            def step(g, b, nxt, last_group):
                s = 2 * g + b

                def mix(j):
                    dve.wait_ge(scan, CH * s + j + 1)
                    if j == 0:
                        dve.wait_ge(cb, s + 1)
                    if j >= 2:
                        dve.wait_ge(yp, CH * s + j - 1)
                    dve.tensor_tensor(M[:, j % 2], Lm[:, j % 2, :].rearrange("p (h t) -> p h t", h=HG),
                                      pc[:, j, :].unsqueeze(1).to_broadcast([P, HG, P]), ALU.mult).then_inc(m_d, 1)

                def low_out(m):
                    if b == 0:
                        dve.wait_ge(hi_d, order(g, m) + 1)
                        dve.scalar_tensor_tensor(wo[1][:, m, :], stage[:, m % 2, :], npar[:, m:m + 1],
                                                 wo[0][:, m, :].bitcast(F32), ALU.mult, ALU.subtract).then_inc(loo_d, 1)

                def state(j):
                    dve.wait_ge(ds, (CH - 1) * s + j + 1)
                    dve.wait_ge(st_d, 2 * s + j)
                    if j == 0:
                        dve.tensor_copy(S[:, 0, :], pss[:]).then_inc(s_d, 1)
                    else:
                        if j == 2:
                            dve.wait_ge(yp, CH * s + 2)
                        dve.tensor_tensor(S[:, j % 2, :], pss[:], St[:], ALU.add).then_inc(s_d, 1)

                def y_and_z(j):
                    dve.wait_ge(yp, CH * s + j + 1)
                    if j == 0:
                        dve.wait_ge(xD_d, MG * (s + 1))
                    dve.wait_ge(sq_d, 3 * (CH * s + max(j - 1, 0)))
                    dve.wait_ge(zf_d, CH * s + max(j - 1, 0))
                    t = slice(j * P, (j + 1) * P)
                    dve.tensor_tensor(y[:, j % 2], py[:, j % 2], xD[:, :, t], ALU.add).then_inc(y_d, 1)
                    dve.wait_ge(y_d, CH * s + j + 1)
                    if j == 0:
                        dve.wait_ge(sg_d, MG * (s + 1))
                    dve.wait_ge(zl_d, CH * s + j)
                    dve.tensor_tensor(zf[:], y[:, j % 2], sg[:, :, t], ALU.mult).then_inc(zf_d, 1)

                def low_z(j):
                    dve.wait_ge(zh_d, CH * s + j + 1)
                    dve.wait_ge(outp, CH * s + max(j - 1, 0))
                    dve.tensor_tensor(z[1][:, j % 2], zf[:], z[0][:, j % 2].bitcast(F32), ALU.subtract).then_inc(zl_d, 1)

                def variance(j):
                    dve.wait_ge(ssq, CH * s + j + 1)
                    dve.wait_ge(r_d, CH * s)
                    dve.tensor_scalar(var[:, j:j + 1], py[:, j % 2, 0, 0:1], 1.0 / CG, EPS, ALU.mult, ALU.add).then_inc(var_d, 1)

                def add_output(j):
                    dve.wait_ge(r_d, CH * s + j + 1)
                    dve.wait_ge(outp, CH * s + j + 1)
                    dve.wait_ge(o_d, CH * s)
                    i = CH * b + j
                    dve.scalar_tensor_tensor(s_acc[:, i, :], pt[:, j % 2, :], rstd[:, j:j + 1], s_acc[:, i, :],
                                             ALU.mult, ALU.add).then_inc(o_d, 1)

                def next_taps(m):
                    if nxt is not None:
                        taps(*nxt, m)

                x_dt(g, b, 1)
                x_dt(g, b, 2)
                low_out(0)
                low_out(1)
                x_dt(g, b, 3)
                mix(0)
                low_out(2)
                low_out(3)
                decays(g, b, 1)
                y_and_z(0)
                state(0)
                low_z(0)
                mix(1)
                next_taps(0)
                decays(g, b, 2)
                next_taps(1)
                y_and_z(1)
                state(1)
                low_z(1)
                mix(2)
                variance(0)
                add_output(0)
                next_taps(2)
                decays(g, b, 3)
                y_and_z(2)
                state(2)
                low_z(2)
                mix(3)
                variance(1)
                add_output(1)
                next_taps(3)
                next_taps(4)
                y_and_z(3)
                low_z(3)
                variance(2)
                add_output(2)
                next_taps(5)
                if nxt is not None:
                    x_dt(*nxt, 0)
                    decays(*nxt, 0)
                variance(3)
                add_output(3)

            steps(dve, step)

        @block.gpsimd
        def _(pool):
            def low(g, k):
                pool.wait_ge(hi_d, order(g, k) + 1)
                part = lambda i: (wx[i][:, k - X] if k < GT else wg[i][:, k - GT]).rearrange("p k n -> p (k n)")
                pool.tensor_tensor(part(1), stage[:, k % 2, :], part(0).bitcast(F32), ALU.subtract).then_inc(lo_d, 1)

            for k in range(X, NPI):
                low(0, k)
            pool.wait_ge(cst, 3)

            def step(g, b, nxt, last_group):
                s = 2 * g + b

                def weigh_x(j):
                    pool.wait_ge(scan, CH * s + j + 1)
                    pool.wait_ge(xdt_d, CH * s + j + 1)
                    pool.wait_ge(ds, (CH - 1) * s + (j == 2))
                    last = Lm[:, j % 2, :].rearrange("p (h t) -> p h t", h=HG)[:, :, P - 1:P].to_broadcast([P, HG, PH])
                    pool.tensor_tensor(Xw[:, (b + j) % 2, :].rearrange("p (h c) -> p h c", h=HG),
                                       xdt[:, j, :].rearrange("p (h c) -> p h c", h=HG), last, ALU.mult).then_inc(xw_d, 1)

                def scale_c(j):
                    q = (b + j - 1) % 2
                    pool.wait_ge(ld_din[q], 16 * (3 * g + (1, 1, 2, 2, 3, 3)[3 * b + j - 1]))
                    if j == 1:
                        pool.wait_ge(xc_d, MC * (s + 1))
                    pool.wait_ge(yp, CH * s + (2 if j == 3 else 0))
                    pool.tensor_tensor(CD[:, q], din[:, q], Cc[:, b, j * P:(j + 1) * P].unsqueeze(1).to_broadcast([P, HG, P]),
                                       ALU.mult).then_inc(cd_d, 1)

                def decay_state(j):
                    q = (b + j - 1) % 2
                    pool.wait_ge(s_d, (CH - 1) * s + j)
                    last = din[:, q, :, P - 1:P].to_broadcast([P, HG, PH])
                    pool.tensor_tensor(St[:].rearrange("p (h c) -> p h c", h=HG),
                                       S[:, (j - 1) % 2, :].rearrange("p (h c) -> p h c", h=HG), last, ALU.mult).then_inc(st_d, 1)

                def squares(j):
                    n = 3 * (CH * s + j)
                    pool.wait_ge(y_d, CH * s + j + 1)
                    pool.wait_ge(ssq, CH * s + j)
                    pool.tensor_tensor(ysq[:], y[:, j % 2], y[:, j % 2], ALU.mult).then_inc(sq_d, 1)
                    pool.wait_ge(sq_d, n + 1)
                    pool.tensor_tensor(ysq[:, 0:2, :], ysq[:, 0:2, :], ysq[:, 2:4, :], ALU.add).then_inc(sq_d, 1)
                    pool.wait_ge(sq_d, n + 2)
                    pool.tensor_tensor(ysq[:, 0, :], ysq[:, 0, :], ysq[:, 1, :], ALU.add).then_inc(sq_d, 1)

                def root(j):
                    pool.wait_ge(var_d, CH * s + j + 1)
                    pool.wait_ge(o_d, CH * s)
                    pool.tensor_tensor(rstd[:, j:j + 1], var[:, j:j + 1], half[:], ALU.pow).then_inc(r_d, 1)

                def split(*pieces):
                    if not last_group:
                        for k in pieces:
                            low(g + 1, k)

                weigh_x(0)
                scale_c(1)
                if b == 1:
                    split(X + 4, X + 5)
                weigh_x(1)
                squares(0)
                decay_state(1)
                scale_c(2)
                split(X if b == 0 else GT)
                weigh_x(2)
                root(0)
                squares(1)
                decay_state(2)
                scale_c(3)
                split(X + 1 if b == 0 else GT + 1)
                root(1)
                squares(2)
                split(X + 2 if b == 0 else GT + 2)
                split(X + 3 if b == 0 else GT + 3)
                root(2)
                squares(3)
                root(3)

            steps(pool, step)


def moe_phase(nc, w_gu, w_dn, comb_dram, xT, f_acc):
    with ExitStack() as ctx:
        sb = lambda n, s, d=F32: ctx.enter_context(nc.sbuf_tensor(f"mo_{n}", s, d))
        sem = phase_semaphores(nc, ctx, "mo")
        gu_in = sb("gu_in", [P, 2, KD * 2 * P])
        dn_in = sb("dn_in", [P, 2, DM])
        gu = [sb(f"gu{i}", [P, 2, KD, 2 * P], F32R) for i in range(2)]
        dn = [sb(f"dn{i}", [P, 2, EB, DM], F32R) for i in range(2)]
        comb = sb("comb", [P, 2, T])
        sgl = sb("sgl", [P, 2, L])
        sgc = sb("sgc", [P, 2, L])
        af = sb("af", [P, 2, L])
        a = [sb(f"a{i}", [P, EB, T], F32R) for i in range(2)]
        pg = ctx.enter_context(nc.psum_tensor("mo_pg", [P, 2, 512], F32))
        pu = ctx.enter_context(nc.psum_tensor("mo_pu", [P, 2, 512], F32))
        pd = ctx.enter_context(nc.psum_tensor("mo_pd", [P, 2, 512], F32))
        ld_gu, ld_dn, ld_cb = ([sem(f"{n}{i}") for i in range(2)] for n in ("ld_gu", "ld_dn", "ld_cb"))
        gp, up, dp, sl_d, sc_d, af_d, ah_d, al_d, f_d, cst, guh, gul, dnh, dnl = (sem(n) for n in (
            "gp", "up", "dp", "sl_d", "sc_d", "af_d", "ah_d", "al_d", "f_d", "cst", "guh", "gul", "dnh", "dnl"))
        block = ctx.enter_context(nc.Block())
        UN = EB * NB
        units = [(e, b) for e in range(EB) for b in range(NB)]

        def chunks(eng, one):
            one(0, 0)
            with eng.Fori(0, EC // 2) as i:
                one(2 * i + 1, 1)
                one(2 * i + 2, 0)

        def chunks_but_last(eng, one):
            one(0, 0)
            with eng.Fori(1, EC // 2) as i:
                one(2 * i - 1, 1)
                one(2 * i, 0)
            one(EC - 2, 1)
            one(EC - 1, 0)

        @block.sync
        def _(sp):
            for e in range(NE):
                q = e % 2
                if e >= 2:
                    sp.wait_ge(gul, e - 1)
                sp.dma_start(gu_in[:, q, :], w_gu[e]).then_inc(ld_gu[q], 16)
                if e >= 2:
                    sp.wait_ge(sc_d, NB * (e - 1))
                sp.dma_start(comb[:, q, :], comb_dram[e].partition_broadcast(P)).then_inc(ld_cb[q], 16)
                if e >= 2:
                    sp.wait_ge(dnl, e - 1)
                sp.dma_start(dn_in[:, q, :], w_dn[e]).then_inc(ld_dn[q], 16)

        @block.tensor
        def _(pe):
            def one(c, q):
                for u, (e, b) in enumerate(units):
                    x = lambda k: both(xT, slice(None), k, slice(b * L, (b + 1) * L))
                    if b == 0:
                        pe.wait_ge(gul, EB * c + e + 1)
                    pe.wait_ge(sl_d, UN * c + max(u - 1, 0))
                    for k in range(KD):
                        last = matmul3(pe, pg[:, b, :], both(gu, slice(None), e % 2, k, slice(0, P)), x(k), k == 0, k == KD - 1)
                    last.then_inc(gp, 1)
                    pe.wait_ge(af_d, UN * c + max(u - 1, 0))
                    for k in range(KD):
                        last = matmul3(pe, pu[:, b, :], both(gu, slice(None), e % 2, k, slice(P, 2 * P)), x(k), k == 0, k == KD - 1)
                    last.then_inc(up, 1)
                pe.wait_ge(dnl, EB * (c + 1))
                for i in range(TT):
                    if i == 0:
                        pe.wait_ge(al_d, UN * (c + 1) - 1)
                    if i == TT // NB:
                        pe.wait_ge(al_d, UN * (c + 1))
                    pe.wait_ge(f_d, TT * c + max(i - 1, 0))
                    for e in range(EB):
                        last = matmul3(pe, pd[:, i % 2, :], both(a, slice(None), e, slice(i * P, (i + 1) * P)),
                                       both(dn, slice(None), q, e), e == 0, e == EB - 1)
                    last.then_inc(dp, 1)
            chunks(pe, one)

        @block.scalar
        def _(act):
            def high(c, q, e):
                n = EB * c + e
                qe, qc = e % 2, (q + (e >= EB)) % 2
                act.wait_ge(ld_gu[qe], 8 * (n - qe) + 16)
                act.wait_ge(up, NB * (n - 1) if not isinstance(n, int) or n >= 2 else 0)
                act.activation(gu[0][:, qe].rearrange("p k n -> p (k n)"), gu_in[:, qe, :], ACT.Copy).then_inc(guh, 1)
                act.wait_ge(ld_dn[qe], 8 * (n - qe) + 16)
                act.wait_ge(dp, TT * (c - 1 + (e >= EB)) if not isinstance(c, int) or c + (e >= EB) >= 2 else 0)
                act.activation(dn[0][:, qc, e % EB, :], dn_in[:, qe, :], ACT.Copy).then_inc(dnh, 1)

            high(0, 0, 0)
            high(0, 0, 1)

            def one(c, q):
                for u, (e, b) in enumerate(units):
                    act.wait_ge(gp, UN * c + u + 1)
                    act.wait_ge(sc_d, UN * c + max(u - 1, 0))
                    act.activation(sgl[:, b, :], pg[:, b, :], ACT.Silu).then_inc(sl_d, 1)
                    act.wait_ge(af_d, UN * c + u + 1)
                    if u == 0:
                        act.wait_ge(dp, TT * c)
                    act.activation(a[0][:, e, b * L:(b + 1) * L], af[:, b, :], ACT.Copy).then_inc(ah_d, 1)
                    if b == 1 and not (isinstance(c, int) and c == EC - 1 and e >= EB - 2):
                        high(c, q, e + 2)
            chunks_but_last(act, one)

        @block.gpsimd
        def _(pool):
            def low(n, qe):
                pool.wait_ge(guh, n + 1)
                pool.tensor_tensor(gu[1][:, qe].rearrange("p k n -> p (k n)"), gu_in[:, qe, :],
                                   gu[0][:, qe].rearrange("p k n -> p (k n)").bitcast(F32), ALU.subtract).then_inc(gul, 1)

            low(0, 0)
            low(1, 1)

            def one(c, q):
                for u, (e, b) in enumerate(units):
                    if b == 0:
                        pool.wait_ge(ld_cb[e % 2], 8 * (EB * c + e - e % 2) + 16)
                    pool.wait_ge(sl_d, UN * c + u + 1)
                    pool.wait_ge(af_d, UN * c + max(u - 1, 0))
                    pool.tensor_tensor(sgc[:, b, :], sgl[:, b, :], comb[:, e % 2, b * L:(b + 1) * L], ALU.mult).then_inc(sc_d, 1)
                    if b == 1 and not (isinstance(c, int) and c == EC - 1 and e >= EB - 2):
                        low(EB * c + e + 2, e % 2)
            chunks_but_last(pool, one)

        @block.vector
        def _(dve):
            dve.memset(f_acc[:], 0.0).then_inc(cst, 1)

            def low_down(c, q, e):
                qe, qc = e % 2, (q + (e >= EB)) % 2
                dve.wait_ge(dnh, EB * c + e + 1)
                dve.tensor_tensor(dn[1][:, qc, e % EB, :], dn_in[:, qe, :], dn[0][:, qc, e % EB, :].bitcast(F32),
                                  ALU.subtract).then_inc(dnl, 1)

            low_down(0, 0, 0)
            low_down(0, 0, 1)

            def one(c, q):
                for u, (e, b) in enumerate(units):
                    dve.wait_ge(up, UN * c + u + 1)
                    dve.wait_ge(sc_d, UN * c + u + 1)
                    dve.wait_ge(al_d, UN * c + max(u - 1, 0))
                    dve.tensor_tensor(af[:, b, :], pu[:, b, :], sgc[:, b, :], ALU.mult).then_inc(af_d, 1)
                    dve.wait_ge(ah_d, UN * c + u + 1)
                    part = (slice(None), e, slice(b * L, (b + 1) * L))
                    dve.tensor_tensor(a[1][part], af[:, b, :], a[0][part].bitcast(F32), ALU.subtract).then_inc(al_d, 1)
                    if b == 1 and not (isinstance(c, int) and c == EC - 1 and e >= EB - 2):
                        low_down(c, q, e + 2)
                dve.wait_ge(cst, 1)
                dve.wait_ge(f_d, TT * c)
                for i in range(TT):
                    dve.wait_ge(dp, TT * c + i + 1)
                    dve.tensor_tensor(f_acc[:, i, :], pd[:, i % 2, :], f_acc[:, i, :], ALU.add).then_inc(f_d, 1)
            chunks_but_last(dve, one)


def qkv_phase(nc, w_q, w_k, w_v, rot_dram, cos_dram, sin_dram, xT, V1, q_parts, k_parts):
    with ExitStack() as ctx:
        sb = lambda n, s, d=F32: ctx.enter_context(nc.sbuf_tensor(f"qk_{n}", s, d))
        sem = phase_semaphores(nc, ctx, "qk")
        stage = [sb(n, [P, KD, DM]) for n in ("wq", "wk", "wv")]
        w = [[sb(f"{n}{i}", [P, KD, DM], F32R) for i in range(2)] for n in ("wq", "wk", "wv")]
        rot = sb("rot", [P, P])
        cos = sb("cos", [P, L])
        sin = sb("sin", [P, L])
        raw = sb("raw", [P, 2, L])
        t1 = sb("t1", [P, 2, L])
        t2 = sb("t2", [P, 2, L])
        qr = sb("qr", [P, 2, L])
        r1 = sb("r1", [P, 2, L])
        parts = sb("parts", [P, 2, 3, L], BF16)
        pq = ctx.enter_context(nc.psum_tensor("qk_pq", [P, 2, 512], F32))
        pr = ctx.enter_context(nc.psum_tensor("qk_pr", [P, 2, 512], F32))
        ld = [sem(f"ld{i}") for i in range(3)]
        ldc, proj, rotd, raw_d, t1_d, t2_d, qr_d, p1_d, r1_d, p2_d, p3_d, vp, v_d, vz, out_s = (sem(n) for n in (
            "ldc", "proj", "rotd", "raw_d", "t1_d", "t2_d", "qr_d", "p1_d", "r1_d", "p2_d", "p3_d", "vp", "v_d", "vz", "out_s"))
        st = [sem("st0"), sem("st1")]
        wh_d, wl_d = sem("wh_d"), [sem(f"wl_d{i}") for i in range(3)]
        block = ctx.enter_context(nc.Block())
        items = [(b, i, m) for b in range(NB) for i in range(2) for m in range(KD)]
        N = len(items)

        @block.sync
        def _(sp):
            for i, (dst, src) in enumerate(zip(stage, (w_q, w_k, w_v))):
                sp.dma_start(dst[:].rearrange("p k n -> p (k n)"), src).then_inc(ld[i], 16)
                if i == 0:
                    for dst, src in ((rot[:], rot_dram), (cos[:], cos_dram), (sin[:], sin_dram)):
                        sp.dma_start(dst, src).then_inc(ldc, 16)
            for n, (b, i, m) in enumerate(items):
                sp.wait_ge(p3_d, n + 1)
                sp.wait_ge(p1_d, n + 1)
                sp.wait_ge(p2_d, n + 1)
                dst = (q_parts, k_parts)[i][b, :, m * P:(m + 1) * P, :].rearrange("a p t -> p a t")
                sp.dma_start(dst, parts[:, n % 2]).then_inc(st[n % 2], 16)
            for i in range(2):
                sp.wait_ge(st[i], 16 * N // 2)

        @block.tensor
        def _(pe):
            def rotate(n):
                pe.wait_ge(raw_d, n + 1)
                if n >= 2:
                    pe.wait_ge(t1_d, n - 1)
                if n == 0:
                    pe.wait_ge(ldc, 48)
                pe.matmul(pr[:, n % 2, :], rot[:], raw[:, n % 2, :], start=True, stop=True).then_inc(rotd, 1)

            for n, (b, i, m) in enumerate(items):
                if b == 0:
                    pe.wait_ge(wl_d[i], 1)
                if n >= 2:
                    pe.wait_ge(raw_d, n - 1)
                for k in range(KD):
                    last = matmul3(pe, pq[:, n % 2, :], both(w[i], slice(None), k, slice(m * P, (m + 1) * P)),
                                   both(xT, slice(None), k, slice(b * L, (b + 1) * L)), k == 0, k == KD - 1)
                last.then_inc(proj, 1)
                if n:
                    rotate(n - 1)
            rotate(N - 1)
            pe.wait_ge(wl_d[2], 1)
            for i in range(TT):
                if i < 2:
                    pe.wait_ge(raw_d, N)
                else:
                    pe.wait_ge(v_d, i - 1)
                for k in range(KD):
                    last = matmul3(pe, pq[:, i % 2, :], both(xT, slice(None), k, slice(i * P, (i + 1) * P)),
                                   both(w[2], slice(None), k), k == 0, k == KD - 1)
                last.then_inc(vp, 1)

        @block.scalar
        def _(act):
            def split(n):
                act.wait_ge(qr_d, n + 1)
                if n >= 2:
                    act.wait_ge(st[n % 2], 16 * (n // 2))
                act.activation(parts[:, n % 2, 0, :], qr[:, n % 2, :], ACT.Copy).then_inc(p1_d, 1)
                act.wait_ge(r1_d, n + 1)
                act.activation(parts[:, n % 2, 1, :], r1[:, n % 2, :], ACT.Copy).then_inc(p2_d, 1)

            for i in range(3):
                act.wait_ge(ld[i], 16)
                act.activation(w[i][0][:], stage[i][:], ACT.Copy).then_inc(wh_d, 1)
            for n in range(N):
                act.wait_ge(proj, n + 1)
                if n >= 2:
                    act.wait_ge(rotd, n - 1)
                    act.wait_ge(t2_d, n - 1)
                act.activation(raw[:, n % 2, :], pq[:, n % 2, :], ACT.Copy).then_inc(raw_d, 1)
                if n:
                    split(n - 1)
            split(N - 1)
            act.wait_ge(vz, 1)
            for i in range(TT):
                act.wait_ge(vp, i + 1)
                act.activation(V1[:, i, :, 0:HD], pq[:, i % 2, :].rearrange("p (h d) -> p h d", d=HD), ACT.Copy).then_inc(v_d, 1)

        @block.gpsimd
        def _(pool):
            def low(i):
                pool.wait_ge(wh_d, i + 1)
                pool.tensor_tensor(w[i][1][:], stage[i][:], w[i][0][:].bitcast(F32), ALU.subtract).then_inc(wl_d[i], 1)

            low(1)
            pool.wait_ge(ldc, 48)
            for n in range(N):
                if n == KD:
                    low(2)
                if n == 2 * KD:
                    pool.memset(V1[:], 1.0).then_inc(vz, 1)
                pool.wait_ge(raw_d, n + 1)
                if n >= 2:
                    pool.wait_ge(qr_d, n - 1)
                pool.tensor_tensor(t2[:, n % 2, :], raw[:, n % 2, :], cos[:], ALU.mult).then_inc(t2_d, 1)

        @block.vector
        def _(dve):
            dve.wait_ge(wh_d, 1)
            dve.tensor_tensor(w[0][1][:], stage[0][:], w[0][0][:].bitcast(F32), ALU.subtract).then_inc(wl_d[0], 1)
            for n in range(N):
                dve.wait_ge(rotd, n + 1)
                if n == 0:
                    dve.wait_ge(ldc, 48)
                if n >= 2:
                    dve.wait_ge(qr_d, n - 1)
                dve.tensor_tensor(t1[:, n % 2, :], pr[:, n % 2, :], sin[:], ALU.mult).then_inc(t1_d, 1)
                dve.wait_ge(t1_d, n + 1)
                dve.wait_ge(t2_d, n + 1)
                if n >= 2:
                    dve.wait_ge(p1_d, n - 1)
                    dve.wait_ge(r1_d, n - 1)
                dve.tensor_tensor(qr[:, n % 2, :], t1[:, n % 2, :], t2[:, n % 2, :], ALU.add).then_inc(qr_d, 1)
                dve.wait_ge(p1_d, n + 1)
                if n >= 2:
                    dve.wait_ge(p3_d, n - 1)
                    dve.wait_ge(p2_d, n - 1)
                dve.tensor_tensor(r1[:, n % 2, :], qr[:, n % 2, :], parts[:, n % 2, 0, :], ALU.subtract).then_inc(r1_d, 1)
                dve.wait_ge(p2_d, n + 1)
                dve.tensor_tensor(parts[:, n % 2, 2, :], r1[:, n % 2, :], parts[:, n % 2, 1, :], ALU.subtract).then_inc(p3_d, 1)


def attention_phase(nc, q_parts, k_parts, V1, w_o, mask_dram, maskT_dram, ident, s_acc):
    with ExitStack() as ctx:
        sb = lambda n, s, d=F32: ctx.enter_context(nc.sbuf_tensor(f"at_{n}", s, d))
        sem = phase_semaphores(nc, ctx, "at")
        NU = NB * HN // HU
        UB = NU // NB
        NP = NU // 2
        SB, PR = 4, 6
        QS = [sb(f"QS{i}", [KR, HU, L], BF16) for i in range(SB)]
        KS = [sb(f"KS{i}", [KR, HU, L], BF16) for i in range(SB)]
        wo_in = sb("wo_in", [P, 2, DM])
        wo = [sb(f"wo{i}", [P, KD, DM], F32R) for i in range(2)]
        mask = sb("mask", [P, L])
        maskf = sb("maskf", [P, P])
        maskT = sb("maskT", [P, P], BF16)
        identb = sb("identb", [P, P], BF16)
        junk = sb("junk", [P, 2, L], BF16)
        mx = sb("mx", [P, 2, TH, HU])
        nm = sb("nm", [HU, L])
        nr = sb("nr", [HU, L])
        nparts = sb("nparts", [HU, 3, L], BF16)
        PT = sb("PT", [P, PR, PTW])
        oT = sb("oT", [P, 2, L])
        num = sb("num", [P, 2, L])
        den = sb("den", [P, 2, L])
        rden = sb("rden", [P, L])
        on = sb("on", [P, L])
        ons = [sb(f"on{i}", [P, KD, L], F32R) for i in range(2)]
        p1 = ctx.enter_context(nc.psum_tensor("at_p1", [P, 3, 512], F32))
        p2 = ctx.enter_context(nc.psum_tensor("at_p2", [P, 3, 512], F32))
        po = ctx.enter_context(nc.psum_tensor("at_po", [P, 512], F32))
        px = ctx.enter_context(nc.psum_tensor("at_px", [P, 512], F32))
        ldc, ld_wo, const_d, wh_d, wl_d = sem("ldc"), [sem("ld_wo0"), sem("ld_wo1")], sem("const_d"), sem("wh_d"), sem("wl_d")
        ldq = [sem(f"ldq{i}") for i in range(SB)]
        ldm = [sem(f"ldm{i}") for i in range(SB)]
        s1, mx_d, mt, nm_d, nr_d, np1_d, np2_d, np3_d, s2, ex_d, pv, oT_d, on_d, oh_d, ol_d, fo, f_d = (sem(n) for n in (
            "s1", "mx_d", "mt", "nm_d", "nr_d", "np1_d", "np2_d", "np3_d", "s2", "ex_d", "pv", "oT_d", "on_d", "oh_d",
            "ol_d", "fo", "f_d"))
        rden_d, rows_d = sem("rden_d"), sem("rows_d")
        packed = [sem("packed0"), sem("packed1")]
        block = ctx.enter_context(nc.Block())
        UT = HU * TH
        off = [sum(L - P * i for i in range(j)) for j in range(TH)]

        OUT0 = UB + 3
        px_order = [("m", 0)]
        for v in range(NU):
            if v + 1 < NU:
                px_order.append(("m", v + 1))
            if v == OUT0:
                px_order += [("o", i) for i in range(TH)]
        px_order.append(("o", TT - 1))
        last_bank = [p1[:, i, :] for i in range(3)] + [px[:]]
        out_bank = lambda i: px[:] if i < TH else last_bank[i - TH]

        def px_free(eng, use):
            at = px_order.index(use)
            if at:
                kind, i = px_order[at - 1]
                if kind == "m":
                    eng.wait_ge(nm_d, i + 1)
                    eng.wait_ge(np1_d, i + 1)
                else:
                    eng.wait_ge(f_d, i + 1)

        @block.sync
        def _(sp):
            def load(w):
                b, m, q = w // UB, w % UB, w % SB
                if w >= SB:
                    sp.wait_ge(s2, UT * (w - SB + 1))
                for n, (a, c) in enumerate(BLOCKS):
                    for dst, src, part in ((QS[q], q_parts, a), (KS[q], k_parts, c)):
                        sp.dma_start(dst[n * HD:(n + 1) * HD, :, :],
                                     src[b, part, m * HU * HD:(m + 1) * HU * HD, :].rearrange("(h d) t -> d h t", d=HD)
                                     ).then_inc(ldq[q], 16)

            def load_wo(k):
                if k >= 2:
                    sp.wait_ge(wl_d, k - 1)
                sp.dma_start(wo_in[:, k % 2, :], w_o[:, k * DM:(k + 1) * DM]).then_inc(ld_wo[k % 2], 16)

            def maxima_rows(w):
                sp.wait_ge(np1_d, w + 1)
                sp.wait_ge(np2_d, w + 1)
                sp.wait_ge(np3_d, w + 1)
                for i in range(3):
                    sp.dma_start(QS[w % SB][KB + i:KB + i + 1, :, :], nparts[:, i, :]).then_inc(ldm[w % SB], 16)

            def pack(w):
                sp.wait_ge(oT_d, w + 1)
                if w >= 4:
                    sp.wait_ge(on_d, w // 2 - 1)
                for c in range(HU):
                    lo = (w % 2) * HU * HD + c * HD
                    sp.dma_start(num[lo:lo + HD, w // 2 % 2, :], oT[32 * c:32 * c + HD, w % 2, :]).then_inc(packed[w % 2], 16)
                    sp.dma_start(den[lo:lo + HD, w // 2 % 2, :], oT[32 * c + HD:32 * c + 2 * HD, w % 2, :]).then_inc(packed[w % 2], 16)

            load(0)
            sp.dma_start(mask[:], mask_dram).then_inc(ldc, 16)
            sp.dma_start(maskf[:], maskT_dram).then_inc(ldc, 16)
            load(1)
            load(2)
            load_wo(0)
            load_wo(1)
            maxima_rows(0)
            for v in range(NU):
                if v + 3 < NU:
                    load(v + 3)
                if v + 1 < NU:
                    maxima_rows(v + 1)
                if v:
                    pack(v - 1)
                if v in (1, 2):
                    load_wo(v + 1)
            pack(NU - 1)

        @block.tensor
        def _(pe):
            def maxima(w, h, i):
                q = w % SB
                if h == 0 and i == 0:
                    pe.wait_ge(ldq[q], 16 * 12 * (w // SB + 1))
                n = (w * HU + h) * TH + i
                if n >= 3:
                    pe.wait_ge(mx_d, n - 2)
                pe.matmul(p1[:, n % 3, 0:(i + 1) * P], QS[q][0:KB, h, i * P:(i + 1) * P], KS[q][0:KB, h, 0:(i + 1) * P],
                          start=True, stop=True).then_inc(s1, 1)

            def turn_maxima(w):
                pe.wait_ge(mx_d, UT * (w + 1))
                px_free(pe, ("m", w))
                for i in range(TH):
                    last = pe.transpose(px[0:HU, i * P:(i + 1) * P], mx[:, w % 2, i, :], ident[:])
                last.then_inc(mt, 1)

            def scores(v, h, j):
                q = v % SB
                if h == 0 and j == 0:
                    pe.wait_ge(ldm[q], 48 * (v // SB + 1))
                n = (v * HU + h) * TH + j
                if n >= 3:
                    pe.wait_ge(ex_d, n - 2)
                pe.matmul(p2[:, n % 3, 0:L - j * P], KS[q][:, h, j * P:(j + 1) * P], QS[q][:, h, j * P:L], start=True, stop=False)
                pe.matmul(p2[:, n % 3, 0:P], identb[:], maskT[:], start=False, stop=True).then_inc(s2, 1)

            def values(v, j):
                if j == 0:
                    pe.wait_ge(ex_d, UT * (v + 1))
                    pe.wait_ge(oT_d, v)
                for c in range(HU):
                    last = pe.matmul(po[32 * c:32 * c + 32, j * P:L], V1[:, v // UB * TH + j, v % UB * HU + c, :],
                                     PT[:, (v * HU + c) % PR, off[j]:off[j] + L - j * P],
                                     start=(j == 0), stop=(j == TH - 1), skip_group_check=True)
                if j == TH - 1:
                    last.then_inc(pv, 1)

            def output(i, k):
                pe.wait_ge(ol_d, KD * (i // TH) + k + 1)
                if k == 0:
                    pe.wait_ge(wl_d, KD)
                    if ("o", i) in px_order:
                        px_free(pe, ("o", i))
                    else:
                        pe.wait_ge(mx_d, UT * NU)
                last = matmul3(pe, out_bank(i), both(ons, slice(None), k, slice(i % TH * P, (i % TH + 1) * P)), both(wo, slice(None), k),
                               k == 0, k == KD - 1)
                if k == KD - 1:
                    last.then_inc(fo, 1)

            for w in range(2):
                for h in range(HU):
                    for i in range(TH):
                        maxima(w, h, i)
                    if w == 1 and h == 0:
                        turn_maxima(0)
            pe.wait_ge(const_d, 2)
            pe.wait_ge(rows_d, SB)
            for v in range(NU):
                for h in range(HU):
                    for i in range(TH):
                        if v + 2 < NU:
                            maxima(v + 2, h, i)
                        if h == 0 and i == 0 and v + 1 < NU:
                            turn_maxima(v + 1)
                        scores(v, h, i)
                        if h == 1 and v:
                            values(v - 1, i)
                        if v == OUT0:
                            output(h, i)
                        if v == NU - 1 and i >= 2:
                            output(TH + h, i - 2)
            for i in range(TH):
                values(NU - 1, i)
            for k in range(2, KD):
                for i in range(TH, TT):
                    output(i, k)

        @block.scalar
        def _(act):
            def negate(w):
                act.wait_ge(mt, w + 1)
                if w:
                    act.wait_ge(np3_d, w)
                    act.wait_ge(ldm[(w - 1) % SB], 48 * ((w - 1) // SB + 1))
                act.activation(nm[:], px[0:HU, :], ACT.Copy, scale=-1.0).then_inc(nm_d, 1)
                act.activation(nparts[:, 0, :], px[0:HU, :], ACT.Copy, scale=-1.0).then_inc(np1_d, 1)

            def second_part(w):
                act.wait_ge(nr_d, w + 1)
                act.activation(nparts[:, 1, :], nr[:], ACT.Copy).then_inc(np2_d, 1)

            def weigh(v, h):
                for j in range(TH):
                    n = (v * HU + h) * TH + j
                    k = v * HU + h
                    act.wait_ge(s2, n + 1)
                    if k >= PR:
                        act.wait_ge(pv, (k - PR) // HU + 1)
                    w = L - j * P
                    act.activation(PT[:, k % PR, off[j]:off[j] + w], p2[:, n % 3, 0:w], ACT.Exp, scale=HD ** -0.5).then_inc(ex_d, 1)

            def copy_values(v):
                act.wait_ge(pv, v + 1)
                if v >= 2:
                    act.wait_ge(packed[v % 2], 16 * 2 * HU * (v // 2))
                act.activation(oT[:, v % 2, :], po[:], ACT.Copy).then_inc(oT_d, 1)

            def high(p):
                act.wait_ge(on_d, p + 1)
                if p % KD == 0 and p:
                    act.wait_ge(fo, TH * (p // KD))
                act.activation(ons[0][:, p % KD, :], on[:], ACT.Copy).then_inc(oh_d, 1)

            def copy_output(i):
                act.wait_ge(fo, i + 1)
                act.activation(s_acc[:, i, :], out_bank(i), ACT.Copy).then_inc(f_d, 1)

            negate(0)
            second_part(0)
            for v in range(NU):
                for h in range(HU):
                    if h == 0 and v + 1 < NU:
                        negate(v + 1)
                    weigh(v, h)
                    if h == 0 and v + 1 < NU:
                        second_part(v + 1)
                    if h == 1 and v:
                        copy_values(v - 1)
                    if h == HU - 1 and v >= 4 and v % 2 == 0:
                        high((v - 4) // 2)
                    if h == HU - 1 and v < KD:
                        act.wait_ge(ld_wo[v % 2], 16 * (v // 2 + 1))
                        act.activation(wo[0][:, v, :], wo_in[:, v % 2, :], ACT.Copy).then_inc(wh_d, 1)
                    if v == OUT0:
                        copy_output(h)
            high(NP - 2)
            copy_values(NU - 1)
            high(NP - 1)
            for i in range(TH, TT):
                copy_output(i)

        @block.gpsimd
        def _(pool):
            def divide(p):
                pool.wait_ge(rden_d, HU * (p + 1))
                for i in range(2):
                    pool.wait_ge(packed[i], 16 * 2 * HU * (p + 1))
                if p:
                    pool.wait_ge(ol_d, p)
                pool.tensor_tensor(on[:], num[:, p % 2, :], rden[:], ALU.mult).then_inc(on_d, 1)

            def low(p):
                pool.wait_ge(oh_d, p + 1)
                pool.tensor_tensor(ons[1][:, p % KD, :], on[:], ons[0][:, p % KD, :].bitcast(F32), ALU.subtract).then_inc(ol_d, 1)

            def maxima_parts(w):
                pool.wait_ge(np1_d, w + 1)
                if w:
                    pool.wait_ge(np2_d, w)
                pool.tensor_tensor(nr[:], nm[:], nparts[:, 0, :], ALU.subtract).then_inc(nr_d, 1)
                pool.wait_ge(np2_d, w + 1)
                pool.tensor_tensor(nparts[:, 2, :], nr[:], nparts[:, 1, :], ALU.subtract).then_inc(np3_d, 1)

            for i in range(SB):
                pool.memset(KS[i][KB:KR, :, :], 1.0).then_inc(rows_d, 1)
            maxima_parts(0)
            for v in range(NU):
                if v + 1 < NU:
                    maxima_parts(v + 1)
                if v < KD:
                    pool.wait_ge(wh_d, v + 1)
                    pool.tensor_tensor(wo[1][:, v, :], wo_in[:, v % 2, :], wo[0][:, v, :].bitcast(F32), ALU.subtract).then_inc(wl_d, 1)
                if v >= 4 and v % 2 == 0:
                    divide((v - 4) // 2)
                    low((v - 4) // 2)
            for p in (NP - 2, NP - 1):
                divide(p)
                low(p)

        @block.vector
        def _(dve):
            def maxima(w, h):
                for i in range(TH):
                    n = (w * HU + h) * TH + i
                    dve.wait_ge(s1, n + 1)
                    if n >= 2:
                        dve.wait_ge(mx_d, n - 1)
                    if h == 0 and w >= 2:
                        dve.wait_ge(mt, w - 1)
                    c = (i + 1) * P
                    dve.tensor_tensor_reduce(junk[:, n % 2, 0:c], p1[:, n % 3, 0:c], mask[:, L - c:L], 1.0, NEG,
                                             ALU.add, ALU.max, mx[:, w % 2, i, h:h + 1]).then_inc(mx_d, 1)

            def invert(p, i):
                if i == 0:
                    for u in range(2):
                        dve.wait_ge(packed[u], 16 * 2 * HU * (p + 1))
                    dve.wait_ge(on_d, p)
                c = slice(i * (L // HU), (i + 1) * (L // HU))
                dve.reciprocal(rden[:, c], den[:, p % 2, c]).then_inc(rden_d, 1)

            dve.wait_ge(ldc, 32)
            for h in range(HU):
                maxima(0, h)
            dve.tensor_copy(maskT[:], maskf[:]).then_inc(const_d, 1)
            dve.tensor_copy(identb[:], ident[:]).then_inc(const_d, 1)
            for h in range(HU):
                maxima(1, h)
            for v in range(NU):
                for h in range(HU):
                    if v + 2 < NU:
                        maxima(v + 2, h)
                    if v >= 3 and v % 2:
                        invert((v - 3) // 2, h)
            for h in range(HU):
                invert(NP - 1, h)


def adapter_phase(nc, w_r, w_ab, xT, ident, g_dram, s_acc, x_res, out):
    NA, RK = 64, 16
    with ExitStack() as ctx:
        sb = lambda n, s, d=F32: ctx.enter_context(nc.sbuf_tensor(f"ad_{n}", s, d))
        sem = phase_semaphores(nc, ctx, "ad")
        two = lambda n, s: [sb(f"{n}{i}", s, F32R) for i in range(2)]
        KT = NA * RK // P
        WPI = 2 * KT
        RING, HR = 4, 4
        wr_in = sb("wr_in", [P, KD, NA])
        wr = two("wr", [P, KD, NA])
        stage = sb("stage", [P, RING, DM])
        w = two("w", [P, WPI, DM])
        lgT = sb("lgT", [NA, T])
        lg = sb("lg", [P, TT, NA])
        v8 = sb("v8", [P, TT, 2, 8])
        rest = sb("rest", [P, TT, 2, NA])
        sh = sb("sh", [P, TT, NA])
        ex = sb("ex", [P, TT, NA])
        tk = sb("tk", [P, TT, NA])
        sm = sb("sm", [P, TT, 1])
        gT = sb("gT", [NA, T])
        gb = sb("gb", [P, 2, L])
        hf = sb("hf", [P, HR, L])
        hs = two("hs", [P, KT, L])
        ga = sb("ga", [P, 2, DM])
        pr = sb("pr", [P, 2, DM])
        res = sb("res", [P, 2, DM])
        pl = ctx.enter_context(nc.psum_tensor("ad_pl", [P, 2, 512], F32))
        ph = ctx.enter_context(nc.psum_tensor("ad_ph", [P, 2, 512], F32))
        pf = ctx.enter_context(nc.psum_tensor("ad_pf", [P, 2, 512], F32))
        ld_r, links = sem("ld_r"), sem("links")
        ld_w = [sem(f"ld_w{i}") for i in range(RING)]
        ld_g = [sem("ld_g0"), sem("ld_g1")]
        st = [sem("st0"), sem("st1")]
        g_st = [sem("g_st0"), sem("g_st1")]
        rh_d, rl_d, wh_d, wl_d, lp, lT_d, tr, lg_d, ch, ex_d, sh_d, gt, gT_d, hp, hf_d, hg_d, hh_d, hl_d, fp, ga_d, pr_d, re_d = (
            sem(n) for n in ("rh_d", "rl_d", "wh_d", "wl_d", "lp", "lT_d", "tr", "lg_d", "ch", "ex_d", "sh_d", "gt", "gT_d",
                             "hp", "hf_d", "hg_d", "hh_d", "hl_d", "fp", "ga_d", "pr_d", "re_d"))
        block = ctx.enter_context(nc.Block())
        N = NB * KT
        TB = TT // NB

        @block.sync
        def _(sp):
            sp.dma_start(wr_in[:].rearrange("p k n -> p (k n)"), w_r).then_inc(ld_r, 16)
            for i in range(WPI):
                if i >= RING:
                    sp.wait_ge(wl_d, i - RING + 1)
                sp.dma_start(stage[:, i % RING, :], w_ab[i]).then_inc(ld_w[i % RING], 16)
            for b in range(NB):
                sp.wait_ge(gT_d, TB * (b + 1))
                sp.dma_start(g_dram[:, b * L:(b + 1) * L], gT[:, b * L:(b + 1) * L]).then_inc(g_st[b], 16)

            def gates(n):
                b, i = n // KT, n % KT
                if i == 0:
                    sp.wait_ge(g_st[b], 16)
                if n >= 2:
                    sp.wait_ge(hg_d, n - 1)
                for a in range(NA // KT):
                    r = i * (NA // KT) + a
                    sp.dma_start(gb[a * RK:(a + 1) * RK, n % 2, :],
                                 g_dram[r, b * L:(b + 1) * L].partition_broadcast(RK)).then_inc(ld_g[n % 2], 16)

            def store(i):
                sp.wait_ge(re_d, i + 1)
                sp.dma_start(out[i * P:(i + 1) * P, :], res[:, i % 2, :]).then_inc(st[i % 2], 16)

            for n in range(KT + HR + 2):
                gates(n)
            for i in range(TB):
                store(i)
            for n in range(KT + HR + 2, N):
                gates(n)
            for i in range(TB, TT):
                store(i)
            for i in range(2):
                sp.wait_ge(st[i], 16 * TT // 2)

        @block.tensor
        def _(pe):
            def tokens(k, b):
                return both(xT, slice(None), k, slice(b * L, (b + 1) * L))

            def down(n):
                b, i = n // KT, n % KT
                if b == 0:
                    pe.wait_ge(wl_d, i + 1)
                if n >= 2:
                    pe.wait_ge(hf_d, n - 1)
                for k in range(KD):
                    last = matmul3(pe, ph[:, n % 2, :], both(w, slice(None), i, slice(k * P, (k + 1) * P)), tokens(k, b),
                                   k == 0, k == KD - 1)
                last.then_inc(hp, 1)

            def up(i):
                b = i // TB
                pe.wait_ge(hl_d, KT * (b + 1))
                pe.wait_ge(wl_d, WPI)
                if i >= 2:
                    pe.wait_ge(ga_d, i - 1)
                for k in range(KT):
                    last = matmul3(pe, pf[:, i % 2, :], both(hs, slice(None), k, slice(i % TB * P, (i % TB + 1) * P)),
                                   both(w, slice(None), KT + k), k == 0, k == KT - 1)
                last.then_inc(fp, 1)

            pe.wait_ge(rl_d, 1)
            for b in range(NB):
                for k in range(KD):
                    last = matmul3(pe, pl[0:NA, b, :], both(wr, slice(None), k), tokens(k, b), k == 0, k == KD - 1)
                last.then_inc(lp, 1)
            pe.wait_ge(lT_d, NB)
            for i in range(TT):
                if i >= 2:
                    pe.wait_ge(lg_d, i - 1)
                pe.transpose(pl[:, i % 2, 0:NA], lgT[:, i * P:(i + 1) * P], ident[0:NA, 0:NA]).then_inc(tr, 1)
            for n in range(HR):
                down(n)
            pe.wait_ge(ch, 1)
            for i in range(TT):
                if i < 2:
                    pe.wait_ge(lg_d, TT)
                else:
                    pe.wait_ge(gT_d, i - 1)
                pe.transpose(pl[0:NA, i % 2, 0:P], tk[:, i, :], ident[:]).then_inc(gt, 1)
            for n in range(HR, KT + HR):
                down(n)
            for i in range(TB):
                up(i)
            for n in range(KT + HR, N):
                down(n)
            for i in range(TB, TT):
                up(i)

        @block.scalar
        def _(act):
            def high(i):
                act.wait_ge(ld_w[i % RING], 16 * (i // RING + 1))
                act.activation(w[0][:, i, :], stage[:, i % RING, :], ACT.Copy).then_inc(wh_d, 1)

            def copy(n):
                act.wait_ge(hp, n + 1)
                if n >= HR:
                    act.wait_ge(hl_d, n - HR + 1)
                act.activation(hf[:, n % HR, :], ph[:, n % 2, :], ACT.Copy).then_inc(hf_d, 1)

            def high_h(n):
                act.wait_ge(hg_d, n + 1)
                if n == KT:
                    act.wait_ge(fp, TB)
                act.activation(hs[0][:, n % KT, :], hf[:, n % HR, :], ACT.Copy).then_inc(hh_d, 1)

            def gate(i):
                act.wait_ge(fp, i + 1)
                if i >= 2:
                    act.wait_ge(pr_d, i - 1)
                act.activation(ga[:, i % 2, :], pf[:, i % 2, :], ACT.Silu, scale=2.0).then_inc(ga_d, 1)

            act.wait_ge(ld_r, 16)
            act.activation(wr[0][:], wr_in[:], ACT.Copy).then_inc(rh_d, 1)
            for i in range(RING):
                high(i)
            for b in range(NB):
                act.wait_ge(lp, b + 1)
                act.activation(lgT[:, b * L:(b + 1) * L], pl[0:NA, b, :], ACT.Copy).then_inc(lT_d, 1)
            for i in range(HR):
                high(RING + i)
                copy(i)
            for i in range(RING + HR, WPI):
                high(i)
            act.wait_ge(sh_d, TT)
            act.activation(ex[:], sh[:], ACT.Exp).then_inc(ex_d, 1)
            for n in range(KT):
                high_h(n)
                copy(n + HR)
            for i in range(TB):
                gate(i)
            for n in range(KT, N):
                high_h(n)
                if n + HR < N:
                    copy(n + HR)
            for i in range(TB, TT):
                gate(i)

        @block.gpsimd
        def _(pool):
            pool.wait_ge(rh_d, 1)
            pool.tensor_tensor(wr[1][:], wr_in[:], wr[0][:].bitcast(F32), ALU.subtract).then_inc(rl_d, 1)
            for i in range(WPI):
                pool.wait_ge(wh_d, i + 1)
                pool.tensor_tensor(w[1][:, i, :], stage[:, i % RING, :], w[0][:, i, :].bitcast(F32), ALU.subtract).then_inc(wl_d, 1)
            for n in range(N):
                pool.wait_ge(hh_d, n + 1)
                if n == KT:
                    pool.wait_ge(fp, TB)
                pool.tensor_tensor(hs[1][:, n % KT, :], hf[:, n % HR, :], hs[0][:, n % KT, :].bitcast(F32),
                                   ALU.subtract).then_inc(hl_d, 1)

        @block.vector
        def _(dve):
            chain, count = links, [0]

            def link(ins):
                count[0] += 1
                ins.then_inc(chain, 1)
                dve.wait_ge(chain, count[0])

            def weigh(n):
                dve.wait_ge(ld_g[n % 2], 16 * (NA // KT) * (n // 2 + 1))
                dve.wait_ge(hf_d, n + 1)
                dve.tensor_tensor(hf[:, n % HR, :], hf[:, n % HR, :], gb[:, n % 2, :], ALU.mult).then_inc(hg_d, 1)

            def result(i):
                dve.wait_ge(ga_d, i + 1)
                if i >= 2:
                    dve.wait_ge(re_d, i - 1)
                dve.tensor_tensor(pr[:, i % 2, :], s_acc[:, i, :], ga[:, i % 2, :], ALU.mult).then_inc(pr_d, 1)
                dve.wait_ge(pr_d, i + 1)
                if i >= 2:
                    dve.wait_ge(st[i % 2], 16 * (i // 2))
                dve.tensor_tensor(res[:, i % 2, :], pr[:, i % 2, :], x_res[:, i, :], ALU.add).then_inc(re_d, 1)

            for i in range(TT):
                dve.wait_ge(tr, i + 1)
                dve.tensor_copy(lg[:, i, :], pl[:, i % 2, 0:NA]).then_inc(lg_d, 1)
            for i in range(TT):
                dve.wait_ge(lg_d, i + 1)
                link(dve.max(v8[:, i, 0, :], lg[:, i, :]))
                dve.tensor_scalar(sh[:, i, :], lg[:, i, :], v8[:, i, 0, 0:1], None, ALU.subtract).then_inc(sh_d, 1)
                link(dve.match_replace(rest[:, i, 0, :], v8[:, i, 0, :], lg[:, i, :], NEG))
                link(dve.max(v8[:, i, 1, :], rest[:, i, 0, :]))
                link(dve.match_replace(rest[:, i, 1, :], v8[:, i, 1, :], rest[:, i, 0, :], NEG))
            link(dve.tensor_tensor(tk[:], lg[:], rest[:, :, 1, :], ALU.not_equal))
            dve.wait_ge(ex_d, 1)
            link(dve.tensor_tensor(tk[:], tk[:], ex[:], ALU.mult))
            link(dve.tensor_reduce(sm[:], tk[:], AX.X, ALU.add))
            link(dve.reciprocal(sm[:], sm[:]))
            dve.tensor_tensor(tk[:], tk[:], sm[:].to_broadcast([P, TT, NA]), ALU.mult).then_inc(ch, 1)
            for i in range(TT):
                dve.wait_ge(gt, i + 1)
                dve.tensor_copy(gT[:, i * P:(i + 1) * P], pl[0:NA, i % 2, 0:P]).then_inc(gT_d, 1)
            for n in range(KT + HR):
                weigh(n)
            for i in range(TB):
                result(i)
            for n in range(KT + HR, N):
                weigh(n)
            for i in range(TB, TT):
                result(i)


def build_program(nc, x, w_small, small_bias, a_log, iota16, ident_dram, w_pieces,
                  conv_par, d_par, n_par, w_gu, w_dn, w_q, w_k, w_v, w_o, rot, cos, sin, mask, maskT,
                  w_r, w_ab, out):
    scratch = lambda n, s, d=F32: nc.dram_tensor(n, s, d, kind="Internal").ap()
    daz_dram = scratch("daz_dram", (TT, H, P))
    din_dram = scratch("din_dram", (TT, H, P))
    comb_dram = scratch("comb_dram", (NE, T))
    q_parts = scratch("q_parts", (NB, 3, DM, L), BF16)
    k_parts = scratch("k_parts", (NB, 3, DM, L), BF16)
    g_dram = scratch("g_dram", (64, T))
    with ExitStack() as ctx:
        sb = lambda n, s, d=F32: ctx.enter_context(nc.sbuf_tensor(n, s, d))
        ident = sb("ident", [P, P])
        xT = [sb(f"xT{i}", [P, KD, T], F32R) for i in range(2)]
        s_acc = sb("s_acc", [P, TT, DM])
        with nc.semaphore("ld0") as ld0, nc.Block() as block:
            @block.sync
            def _(sp):
                sp.dma_start(ident[:], ident_dram).then_inc(ld0, 16)
                sp.wait_ge(ld0, 16)
        layernorm_phase(nc, x, xT, ident, None, "n0")
        with nc.sbuf_tensor("dtT", [P, TT, H], F32) as dtT:
            small_phase(nc, w_small, small_bias, a_log, iota16, xT, ident, dtT, daz_dram, din_dram, comb_dram)
            ssm_phase(nc, w_pieces, conv_par, d_par, n_par, xT, ident, dtT, daz_dram, din_dram, s_acc)
        x1 = sb("x1", [P, TT, DM])
        with nc.sbuf_tensor("f_acc", [P, TT, DM], F32) as f_acc:
            moe_phase(nc, w_gu, w_dn, comb_dram, xT, f_acc)
            layernorm_phase(nc, x, xT, ident, x1, "n1", combine=(x, s_acc, f_acc, 1.0))
        with nc.sbuf_tensor("V1", [P, TT, HN, 2 * HD], F32) as V1:
            qkv_phase(nc, w_q, w_k, w_v, rot, cos, sin, xT, V1, q_parts, k_parts)
            attention_phase(nc, q_parts, k_parts, V1, w_o, mask, maskT, ident, s_acc)
        adapter_phase(nc, w_r, w_ab, xT, ident, g_dram, s_acc, x1, out)


def layouts(d):
    a = {k: np.asarray(v) for k, v in d.items()}
    W = a["L0_attn_in_proj_w"]
    I, GN = H * PH, G * NS

    def kmajor(rows):
        return rows.reshape(-1, KD, P).transpose(2, 1, 0)

    def per_group(lo, n):
        return W[lo:lo + G * n].reshape(G, n, KD, P).transpose(0, 3, 2, 1)

    def tiles(w):
        return w.reshape(G, P, KD, -1, P).transpose(0, 3, 1, 2, 4).reshape(G, -1, P, DM)

    out_w = a["L0_attn_out_proj_w"].reshape(DM, G, MG, P).transpose(1, 2, 3, 0)
    pieces = [out_w, tiles(per_group(I, CG)), tiles(per_group(2 * I, NS)), tiles(per_group(2 * I + GN, NS)), tiles(per_group(0, CG))]
    conv = np.concatenate([a["L0_attn_conv_weight"], a["L0_attn_conv_bias"][:, None]], 1)
    cx = conv[:I].reshape(G, MG, P, KC + 1)
    cB = conv[I:I + GN].reshape(G, 1, P, KC + 1)
    cC = conv[I + GN:].reshape(G, 1, P, KC + 1)
    shared = a["L0_ffn_shared_w_gate_up"].reshape(2, 4, P, DM).transpose(1, 0, 2, 3).reshape(4, 2 * P, DM)
    gu = np.concatenate([a["L0_ffn_w_gate_up"], shared], 0)
    shared_dn = a["L0_ffn_shared_w_down"].reshape(DM, 4, P).transpose(1, 2, 0)
    dn = np.concatenate([a["L0_ffn_w_down"].transpose(0, 2, 1), shared_dn], 0)
    theta = (1.0 / np.float32(10000.0) ** (np.arange(0, HD, 2, dtype=np.float32) / np.float32(HD))).astype(np.float32)
    angle = np.outer(np.arange(L, dtype=np.float32), theta).astype(np.float32)
    angle = np.tile(np.concatenate([angle, angle], 1).T, (P // HD, 1))
    R = np.zeros((P, P), np.float32)
    for p in range(P):
        base, i = p - p % HD, p % HD
        if i < HD // 2:
            R[base + i + HD // 2, p] = -1.0
        else:
            R[base + i - HD // 2, p] = 1.0
    mask = np.zeros((P, L), np.float32)
    mask[:, L - P:] = np.where(np.arange(P)[None, :] > np.arange(P)[:, None], np.float32(-1e30), np.float32(0))
    maskT = np.where(np.arange(P)[:, None] > np.arange(P)[None, :], np.float32(-1e30), np.float32(0))
    arr = {
        "x": a["L0_attn_hidden_states"].reshape(T, DM),
        "w_small": kmajor(np.concatenate([W[-H:], a["L0_ffn_gate_w"]], 0)),
        "small_bias": a["L0_attn_dt_bias"][:, None],
        "a_log": a["L0_attn_A_log"][:, None],
        "iota16": np.tile(np.arange(16, dtype=np.float32), (P, 1)),
        "ident_dram": np.eye(P, dtype=np.float32),
        "w_pieces": np.concatenate(pieces, 1).reshape(G * NPI, P, DM),
        "conv_par": np.concatenate([cx, cB, cC], 1).transpose(0, 2, 1, 3).reshape(G, P, -1),
        "d_par": np.repeat(a["L0_attn_D"], PH).reshape(G, MG, P).transpose(0, 2, 1),
        "n_par": a["L0_attn_norm_weight"].reshape(G, MG, P).transpose(0, 2, 1),
        "w_gu": gu.reshape(NE, 2 * P, KD, P).transpose(0, 3, 2, 1).reshape(NE, P, -1),
        "w_dn": dn,
        "w_q": kmajor(a["L1_attn_wq"]).reshape(P, -1),
        "w_k": kmajor(a["L1_attn_wk"]).reshape(P, -1),
        "w_v": kmajor(a["L1_attn_wv"]).reshape(P, -1),
        "w_o": kmajor(a["L1_attn_wo"]).reshape(P, -1),
        "rot": R,
        "cos": np.cos(angle).astype(np.float32),
        "sin": np.sin(angle).astype(np.float32),
        "mask": mask,
        "maskT": maskT,
        "w_r": kmajor(a["L1_ffn_Wr"]).reshape(P, -1),
        "w_ab": np.concatenate([kmajor(a["L1_ffn_A"].reshape(-1, DM)).reshape(P, KD, 8, P).transpose(2, 0, 1, 3).reshape(8, P, DM),
                                a["L1_ffn_B"].transpose(0, 2, 1).reshape(8, P, DM)], 0),
    }
    return {k: np.ascontiguousarray(v) for k, v in arr.items()}


def kernel(**inputs):
    import concourse.bacc as bacc
    from concourse.bass_utils import run_bass_kernel_spmd

    nc = bacc.Bacc("TRN2", target_bir_lowering=False, num_devices=1, dynamic_dma_scratch_size=1024)
    arrays = layouts(inputs)
    args = [nc.dram_tensor(k, v.shape, mybir.dt.from_np(v.dtype), kind="ExternalInput").ap() for k, v in arrays.items()]
    args.append(nc.dram_tensor("out", (T, DM), F32, kind="ExternalOutput").ap())
    build_program(nc, *args)
    r = run_bass_kernel_spmd(nc, [arrays], core_ids=[0])
    return r.results[0]["out"].reshape(NB, L, DM)
```

```python
from contextlib import ExitStack

import numpy as np

import concourse.bass as bass
from concourse import mybir
from concourse.alu_op_type import AluOpType as ALU

ACT = mybir.ActivationFunctionType
F32 = mybir.dt.float32
F32R = mybir.dt.float32r
BF16 = mybir.dt.bfloat16
U32 = mybir.dt.uint32
AX = mybir.AxisListType

P = 128
NB, L, DM = 2, 512, 512
T = NB * L
TT = T // P
KD = DM // P
EPS = 1e-5

G, H, PH, NS, KC = 8, 64, 64, 128, 4
HG = H // G
CG = HG * PH
MG = CG // P
MC = MG + 2
CH = L // P
HT = NB * H + 16

NPI = MG + MC + MG

NE, EB, EC = 20, 4, 5

HN, HD, HU = 32, 16, 4
TH = L // P
PTW = sum(L - P * j for j in range(TH))
RUNS = (3, 2, 1)
KB = HD * sum(RUNS)
KR = KB + 3
NEG = -3.0e38

NA, RK = 64, 16


def phase_semaphores(nc, ctx, tag):
    taken = []

    def sem(name):
        taken.append(nc.alloc_semaphore(f"{tag}_{name}"))
        return taken[-1]

    def end():
        nc.clear_and_free_semaphores(taken)
        nc.all_engine_barrier()

    ctx.callback(end)
    return sem


def matmul3(pe, out, lhs, rhs, start, stop):
    pe.matmul(out, lhs[0], rhs[0], start=start, stop=False)
    pe.matmul(out, lhs[0], rhs[1], start=False, stop=False)
    return pe.matmul(out, lhs[1], rhs[0], start=False, stop=stop)


def both(parts, *index):
    return tuple(p[index] for p in parts)


def layernorm_phase(nc, x_dram, xT, ident, x_res, tag, s_acc=None, ahead=None, ident_dram=None):
    with ExitStack() as ctx:
        sb = lambda n, s, d=F32: ctx.enter_context(nc.sbuf_tensor(f"{tag}_{n}", s, d))
        sem = phase_semaphores(nc, ctx, tag)
        x = sb("x", [P, TT, DM])
        xt = x if x_res is None else x_res
        xn = sb("xn", [P, 4, DM])
        gate = sb("gate", [P, 2, DM])
        prod = sb("prod", [P, 2, DM])
        stats = sb("stats", [P, TT, 6])
        mv = sb("mv", [P, TT, 2])
        ve = sb("ve", [P, TT])
        half = sb("half", [P, TT])
        rstd = sb("rstd", [P, TT])
        shift = sb("shift", [P, TT])
        ps = ctx.enter_context(nc.psum_tensor(f"{tag}_ps", [P, 4, 512], F32))
        if ahead is not None:
            stage = sb("stage", [P, KD, DM])
            ld_ahead, high_ahead, low_ahead = sem("ld_ahead"), sem("high_ahead"), sem("low_ahead")
        loaded = [sem(f"loaded{i}") for i in range(TT)]
        ident_loaded = sem("ident_loaded")
        half_set, gate_done, prod_done, x_done = sem("half_set"), sem("gate_done"), sem("prod_done"), sem("x_done")
        stats_done, mv_done, ve_done, rstd_done, shift_done = (sem(n) for n in (
            "stats_done", "mv_done", "ve_done", "rstd_done", "shift_done"))
        xn_done = [sem("xn_done0"), sem("xn_done1")]
        tr_done, hi_done, out_done = sem("tr_done"), sem("hi_done"), sem("out_done")
        block = ctx.enter_context(nc.Block())
        xv = x_dram.rearrange("(n p) d -> n p d", p=P)
        HT2 = TT // 2

        @block.sync
        def _(sp):
            for i in range(TT):
                sp.dma_start(x[:, i, :], xv[i]).then_inc(loaded[i], 16)
            if ident_dram is not None:
                sp.dma_start(ident[:], ident_dram).then_inc(ident_loaded, 16)
            if ahead is not None:
                sp.dma_start(stage[:].rearrange("p k n -> p (k n)"), ahead[0]).then_inc(ld_ahead, 16)

        @block.gpsimd
        def _(pool):
            def roots(g):
                pool.wait_ge(ve_done, HT2 * (g + 1))
                c = slice(HT2 * g, HT2 * (g + 1))
                pool.tensor_tensor(rstd[:, c], ve[:, c], half[:, c], ALU.pow).then_inc(rstd_done, 1)

            pool.wait_ge(half_set, 1)
            for i in range(TT):
                if x_res is not None:
                    pool.wait_ge(loaded[i], 16)
                    pool.wait_ge(prod_done, i + 1)
                    pool.tensor_tensor(xt[:, i, :], x[:, i, :], prod[:, i % 2, :], ALU.add).then_inc(x_done, 1)
                if i == HT2 + 1:
                    roots(0)
            roots(1)
            if ahead is not None:
                pool.wait_ge(ld_ahead, 16)
                for k in range(KD):
                    pool.wait_ge(high_ahead, k + 1)
                    pool.tensor_tensor(ahead[2][:, k, :], stage[:, k, :], ahead[1][:, k, :].bitcast(F32), ALU.subtract).then_inc(low_ahead, 1)

        @block.scalar
        def _(act):
            def weigh(i):
                if i >= 2:
                    act.wait_ge(prod_done, i - 1)
                act.activation(gate[:, i % 2, :], x_res[:, i, :], ACT.Silu).then_inc(gate_done, 1)

            def normalise(i):
                act.wait_ge(shift_done, i // HT2 + 1)
                if i >= 4:
                    act.wait_ge(tr_done, i - 3)
                act.activation(xn[:, i % 4, :], xt[:, i, :], ACT.Identity, scale=rstd[:, i:i + 1],
                               bias=shift[:, i:i + 1]).then_inc(xn_done[0], 1)

            def high(i):
                act.wait_ge(tr_done, i + 1)
                act.activation(xT[0][:, :, i * P:(i + 1) * P],
                               ps[:, i % 4, :].rearrange("p (k t) -> p k t", k=KD), ACT.Copy).then_inc(hi_done, 1)

            if x_res is not None:
                for i in range(TT):
                    weigh(i)
            if ahead is not None:
                act.wait_ge(ld_ahead, 16)
                for k in range(KD):
                    act.activation(ahead[1][:, k, :], stage[:, k, :], ACT.Copy).then_inc(high_ahead, 1)
            for i in range(0, TT, 2):
                normalise(i)
                if i:
                    high(i - 2)
                    high(i - 1)
            high(TT - 2)
            high(TT - 1)

        @block.vector
        def _(dve):
            def shifts(g):
                dve.wait_ge(rstd_done, g + 1)
                c = slice(HT2 * g, HT2 * (g + 1))
                dve.scalar_tensor_tensor(shift[:, c], mv[:, c, 0], -1.0, rstd[:, c], ALU.mult, ALU.mult).then_inc(shift_done, 1)

            def normalise(i):
                if i >= 4:
                    dve.wait_ge(tr_done, i - 3)
                dve.tensor_scalar(xn[:, i % 4, :], xt[:, i, :], mv[:, i, 0:1], rstd[:, i:i + 1],
                                  ALU.subtract, ALU.mult).then_inc(xn_done[1], 1)

            def low(i):
                dve.wait_ge(hi_done, i + 1)
                part = (slice(None), slice(None), slice(i * P, (i + 1) * P))
                dve.tensor_tensor(xT[1][part], ps[:, i % 4, :].rearrange("p (k t) -> p k t", k=KD),
                                  xT[0][part].bitcast(F32), ALU.subtract).then_inc(out_done, 1)

            def statistics(i):
                dve.wait_ge(loaded[i], 16)
                if x_res is not None:
                    dve.wait_ge(x_done, i + 1)
                dve.bn_stats(stats[:, i, :], xt[:, i, :]).then_inc(stats_done, 1)
                dve.wait_ge(stats_done, i + 1)
                dve.bn_aggr(mv[:, i, :], stats[:, i, :]).then_inc(mv_done, 1)
                dve.wait_ge(mv_done, i + 1)
                dve.tensor_scalar(ve[:, i:i + 1], mv[:, i, 1:2], EPS, None, ALU.add).then_inc(ve_done, 1)

            dve.memset(half[:], -0.5).then_inc(half_set, 1)
            for i in range(TT):
                if x_res is not None:
                    dve.wait_ge(gate_done, i + 1)
                    if i >= 2:
                        dve.wait_ge(x_done, i - 1)
                    dve.tensor_tensor(prod[:, i % 2, :], s_acc[:, i, :], gate[:, i % 2, :], ALU.mult).then_inc(prod_done, 1)
                    if i:
                        statistics(i - 1)
                else:
                    statistics(i)
                if i == TT - 2:
                    shifts(0)
            if x_res is not None:
                statistics(TT - 1)
            normalise(1)
            low(0)
            shifts(1)
            for i in range(3, TT, 2):
                normalise(i)
                low(i - 2)
                low(i - 1)
            low(TT - 1)

        @block.tensor
        def _(pe):
            if ident_dram is not None:
                pe.wait_ge(ident_loaded, 16)
            for i in range(TT):
                pe.wait_ge(xn_done[i % 2], i // 2 + 1)
                if i >= 4:
                    pe.wait_ge(out_done, i - 3)
                for k in range(KD):
                    last = pe.transpose(ps[:, i % 4, k * P:(k + 1) * P], xn[:, i % 4, k * P:(k + 1) * P], ident[:])
                last.then_inc(tr_done, 1)


def small_phase(nc, w_small, small_bias, a_log, iota16, w_pieces, xT, ident, wx, wg, dtT, daz_dram, din_dram, comb_dram):
    with ExitStack() as ctx:
        sb = lambda n, s, d=F32: ctx.enter_context(nc.sbuf_tensor(f"sm_{n}", s, d))
        sem = phase_semaphores(nc, ctx, "sm")
        pieces = [(wx, m) for m in range(MC)] + [(wg, m) for m in range(MG)]
        stage = sb("stage", [P, len(pieces), DM])
        w = sb("w", [P, KD, HT])
        w2 = [sb(f"w{i}", [P, KD, HT], F32R) for i in range(2)]
        bias = sb("bias", [P, 1])
        alog = sb("alog", [P, 1])
        ea = sb("ea", [P, 1])
        nea = sb("nea", [P, 1])
        io = sb("io", [P, 16])
        v, ab, e, u, lnu, d, r, mx, z, dA, first, din = (sb(n, [P, L]) for n in (
            "v", "ab", "e", "u", "lnu", "d", "r", "mx", "z", "dA", "first", "din"))
        lgT = sb("lgT", [16, T])
        lg = sb("lg", [P, TT, 16])
        top = sb("top", [P, TT, 8])
        idx = sb("idx", [P, TT, 8], U32)
        idf = sb("idf", [P, TT, 8])
        gap = sb("gap", [P, TT, 1])
        eg = sb("eg", [P, TT, 1])
        den = sb("den", [P, TT, 1])
        wt = sb("wt", [P, TT, 2])
        oh = sb("oh", [P, 2, TT, 16])
        comb = sb("comb", [P, TT, 16])
        combT = sb("combT", [16, T])
        ones = sb("ones", [4, T])
        ps = ctx.enter_context(nc.psum_tensor("sm_ps", [P, 2, 512], F32))
        pg = ctx.enter_context(nc.psum_tensor("sm_pg", [P, 2, 512], F32))
        pl = ctx.enter_context(nc.psum_tensor("sm_pl", [P, TT, 16], F32))
        pt = ctx.enter_context(nc.psum_tensor("sm_pt", [P, 512], F32))
        pc = ctx.enter_context(nc.psum_tensor("sm_pc", [P, 2, 512], F32))
        ld, stored, pe_z, pe_l, tr, ct, w2_done, v_done, links, dt_done, lg_done, max_done, idx_done, gap_done, comb_done = (
            sem(n) for n in ("ld", "stored", "pe_z", "pe_l", "tr", "ct", "w2_done", "v_done", "links", "dt_done", "lg_done",
                             "max_done", "idx_done", "gap_done", "comb_done"))
        lgT_done, lt = sem("lgT_done"), sem("lt")
        ld_w = [sem(f"ld_w{i}") for i in range(len(pieces))]
        hi_done, lo_done = sem("hi_done"), sem("lo_done")
        scan_done, ct_done, ones_set, dtT_done, u_done, first_set = (sem(n) for n in (
            "scan_done", "ct_done", "ones_set", "dtT_done", "u_done", "first_set"))
        ea_done, nea_done, e_done, ln_done, r_done, dA_done, eg_done, ab_done = (sem(n) for n in (
            "ea_done", "nea_done", "e_done", "ln_done", "r_done", "dA_done", "eg_done", "ab_done"))
        block = ctx.enter_context(nc.Block())

        @block.sync
        def _(sp):
            for dst, src in ((w[:], w_small), (bias[:], small_bias), (alog[:], a_log), (io[:], iota16)):
                sp.dma_start(dst, src).then_inc(ld, 16)
            for i in range(len(pieces)):
                sp.dma_start(stage[:, i, :], w_pieces[MG + i]).then_inc(ld_w[i], 16)
            sp.wait_ge(scan_done, 1)
            for b in range(NB):
                for dram, src in ((daz_dram, dA), (din_dram, din)):
                    sp.dma_start(dram[b * CH:(b + 1) * CH].rearrange("c h t -> h c t"),
                                 src[b * H:(b + 1) * H, :].rearrange("h (c t) -> h c t", t=P)).then_inc(stored, 16)
            sp.wait_ge(ones_set, 1)
            sp.dma_start(comb_dram[16:20, :], ones[:]).then_inc(stored, 16)
            sp.wait_ge(ct_done, NB)
            sp.dma_start(comb_dram[0:16, :], combT[:]).then_inc(stored, 16)
            sp.wait_ge(stored, 16 * 6)

        @block.tensor
        def _(pe):
            pe.wait_ge(w2_done, 2)
            for b in range(NB):
                for k in range(KD):
                    last = matmul3(pe, ps[:, b, :], both(w2, slice(None), k, slice(0, NB * H)),
                                   both(xT, slice(None), k, slice(b * L, (b + 1) * L)), k == 0, k == KD - 1)
                last.then_inc(pe_z, 1)
            for b in range(NB):
                for k in range(KD):
                    last = matmul3(pe, pg[0:16, b, :], both(w2, slice(None), k, slice(NB * H, HT)),
                                   both(xT, slice(None), k, slice(b * L, (b + 1) * L)), k == 0, k == KD - 1)
                last.then_inc(pe_l, 1)
            pe.wait_ge(lgT_done, NB)
            for i in range(TT):
                last = pe.transpose(pl[:, i, :], lgT[:, i * P:(i + 1) * P], ident[0:16, 0:16])
            last.then_inc(lt, 1)
            pe.wait_ge(dt_done, 1)
            for c in range(CH):
                last = pe.transpose(pt[:, c * P:(c + 1) * P], z[:, c * P:(c + 1) * P], ident[:])
            last.then_inc(tr, 1)
            pe.wait_ge(comb_done, 1)
            for b in range(NB):
                for c in range(CH):
                    last = pe.transpose(pc[0:16, b, c * P:(c + 1) * P], comb[:, b * CH + c, :], ident[:])
                last.then_inc(ct, 1)

        @block.scalar
        def _(act):
            act.wait_ge(ld, 64)
            act.activation(ea[:], alog[:], ACT.Exp).then_inc(ea_done, 1)
            act.wait_ge(ea_done, 1)
            act.activation(nea[:], ea[:], ACT.Copy, scale=-1.0).then_inc(nea_done, 1)
            for i, (parts, m) in enumerate(pieces):
                act.wait_ge(ld_w[i], 16)
                act.activation(parts[0][:, m].rearrange("p k n -> p (k n)"), stage[:, i, :], ACT.Copy).then_inc(hi_done, 1)
            act.wait_ge(v_done, NB)
            act.activation(ab[:], v[:], ACT.Abs).then_inc(ab_done, 1)
            act.wait_ge(ab_done, 1)
            act.activation(e[:], ab[:], ACT.Exp, scale=-1.0).then_inc(e_done, 1)
            act.wait_ge(u_done, 1)
            act.activation(lnu[:], u[:], ACT.Ln).then_inc(ln_done, 1)
            act.wait_ge(ln_done, 1)
            act.activation(r[:], lnu[:], ACT.Exp, scale=-1.0).then_inc(r_done, 1)
            for b in range(NB):
                act.wait_ge(pe_l, b + 1)
                act.activation(lgT[:, b * L:(b + 1) * L], pg[0:16, b, :], ACT.Copy).then_inc(lgT_done, 1)
            act.wait_ge(dt_done, 1)
            act.wait_ge(nea_done, 1)
            act.activation(dA[:], z[:], ACT.Exp, scale=nea[:]).then_inc(dA_done, 1)
            act.wait_ge(gap_done, 1)
            act.activation(eg[:], gap[:], ACT.Exp).then_inc(eg_done, 1)

        @block.gpsimd
        def _(pool):
            for i, (parts, m) in enumerate(pieces):
                flat = lambda a: a.rearrange("p k n -> p (k n)")
                pool.wait_ge(hi_done, i + 1)
                pool.tensor_tensor(flat(parts[1][:, m]), stage[:, i, :], flat(parts[0][:, m]).bitcast(F32),
                                   ALU.subtract).then_inc(lo_done, 1)

        @block.vector
        def _(dve):
            count = [0]

            def link(ins):
                count[0] += 1
                ins.then_inc(links, 1)
                dve.wait_ge(links, count[0])

            dve.wait_ge(ld, 64)
            dve.tensor_copy(w2[0][:], w[:]).then_inc(w2_done, 1)
            dve.wait_ge(w2_done, 1)
            dve.tensor_tensor(w2[1][:], w[:], w2[0][:].bitcast(F32), ALU.subtract).then_inc(w2_done, 1)
            dve.memset(ones[:], 1.0).then_inc(ones_set, 1)
            dve.memset(first[:], 0.0).then_inc(first_set, 1)
            for b in range(NB):
                dve.wait_ge(pe_z, b + 1)
                rows = slice(b * H, (b + 1) * H)
                dve.tensor_scalar(v[rows, :], ps[rows, b, :], bias[rows, :], None, ALU.add).then_inc(v_done, 1)
            dve.wait_ge(e_done, 1)
            dve.tensor_scalar(u[:], e[:], 1.0, None, ALU.add).then_inc(u_done, 1)
            dve.wait_ge(u_done, 1)
            link(dve.scalar_tensor_tensor(d[:], u[:], -1.0, e[:], ALU.add, ALU.subtract))
            dve.wait_ge(v_done, NB)
            dve.wait_ge(ln_done, 1)
            link(dve.scalar_tensor_tensor(mx[:], v[:], 0.0, lnu[:], ALU.max, ALU.add))
            dve.wait_ge(r_done, 1)
            link(dve.tensor_tensor(d[:], d[:], r[:], ALU.mult))
            dve.tensor_tensor(z[:], mx[:], d[:], ALU.subtract).then_inc(dt_done, 1)
            dve.wait_ge(lt, 1)
            dve.tensor_copy(lg[:], pl[:]).then_inc(lg_done, 1)
            dve.wait_ge(lg_done, 1)
            for i in range(TT):
                dve.max(top[:, i, :], lg[:, i, :]).then_inc(max_done, 1)
            for i in range(TT):
                dve.wait_ge(max_done, i + 1)
                dve.max_index(idx[:, i, :], top[:, i, :], lg[:, i, :]).then_inc(idx_done, 1)
            dve.tensor_tensor(gap[:], top[:, :, 1:2], top[:, :, 0:1], ALU.subtract).then_inc(gap_done, 1)
            dve.wait_ge(dA_done, 1)
            dve.wait_ge(first_set, 1)
            dAc = dA[:].rearrange("h (c t) -> h c t", t=P)
            fc = first[:].rearrange("h (c t) -> h c t", t=P)
            link(dve.tensor_copy(fc[:, :, 0:1], dAc[:, :, 0:1]))
            link(dve.memset(dAc[:, :, 0:1], 0.0))
            dve.tensor_tensor_scan(din[:], dA[:], first[:], 0.0, ALU.mult, ALU.add).then_inc(scan_done, 1)
            dve.wait_ge(tr, 1)
            dve.tensor_copy(dtT[:].rearrange("p (b c) h -> p c b h", b=NB),
                            pt[:].rearrange("p (c b h) -> p c b h", c=CH, b=NB)).then_inc(dtT_done, 1)
            dve.wait_ge(idx_done, TT)
            link(dve.tensor_copy(idf[:], idx[:]))
            dve.wait_ge(eg_done, 1)
            link(dve.tensor_scalar(den[:], eg[:], 1.0, None, ALU.add))
            link(dve.reciprocal(wt[:, :, 0:1], den[:]))
            link(dve.tensor_tensor(wt[:, :, 1:2], eg[:], wt[:, :, 0:1], ALU.mult))
            for j in range(2):
                link(dve.tensor_tensor(oh[:, j], io[:].unsqueeze(1).to_broadcast([P, TT, 16]),
                                       idf[:, :, j:j + 1].to_broadcast([P, TT, 16]), ALU.is_equal))
                link(dve.tensor_tensor(oh[:, j], oh[:, j], wt[:, :, j:j + 1].to_broadcast([P, TT, 16]), ALU.mult))
            dve.tensor_tensor(comb[:], oh[:, 0], oh[:, 1], ALU.add).then_inc(comb_done, 1)
            for b in range(NB):
                dve.wait_ge(ct, b + 1)
                dve.tensor_copy(combT[:, b * L:(b + 1) * L], pc[0:16, b, :]).then_inc(ct_done, 1)


def ssm_phase(nc, w_pieces, conv_par, d_par, n_par, xT, ident, wx, wg, dtT, daz_dram, din_dram, s_acc):
    with ExitStack() as ctx:
        sb = lambda n, s, d=F32: ctx.enter_context(nc.sbuf_tensor(f"ss_{n}", s, d))
        sem = phase_semaphores(nc, ctx, "ss")
        two = lambda n, s: [sb(f"{n}{i}", s, F32R) for i in range(2)]
        stage = sb("stage", [P, 2, DM])
        wo = two("wo", [P, MG, DM])
        cpar = sb("cpar", [P, MC, KC + 1])
        dpar = sb("dpar", [P, MG])
        npar = sb("npar", [P, MG])
        id8 = sb("id8", [P, HG, P], BF16)
        daz = sb("daz", [P, 2, HG * P])
        din = sb("din", [P, 2, HG, P])
        cv = sb("cv", [P, 2, L])
        xc = sb("xc", [P, MG, L])
        Bc = sb("Bc", [P, L])
        Cc = sb("Cc", [P, 2, L])
        xD = sb("xD", [P, MG, L])
        Bt = sb("Bt", [P, CH, NS])
        xdt = sb("xdt", [P, CH, CG])
        Lm = sb("Lm", [P, 2, HG * P])
        M = sb("M", [P, 2, HG, P])
        CD = sb("CD", [P, 2, HG, P])
        Xw = sb("Xw", [P, 2, CG])
        S = sb("S", [P, 2, CG])
        St = sb("St", [P, CG])
        y = sb("y", [P, 2, MG, P])
        ysq = sb("ysq", [P, MG, P])
        sg = sb("sg", [P, MG, L])
        zf = sb("zf", [P, MG, P])
        z = two("z", [P, 2, MG, P])
        ones = sb("ones", [P, 1])
        half = sb("half", [P, 1])
        var = sb("var", [P, CH])
        rstd = sb("rstd", [P, CH])
        pp = ctx.enter_context(nc.psum_tensor("ss_pp", [P, 2, 512], F32))
        pt = ctx.enter_context(nc.psum_tensor("ss_pt", [P, 2, 512], F32))
        pc = ctx.enter_context(nc.psum_tensor("ss_pc", [P, CH, P], F32))
        py = ctx.enter_context(nc.psum_tensor("ss_py", [P, 2, MG, P], F32))
        pss = ctx.enter_context(nc.psum_tensor("ss_ps", [P, 512], F32))

        ld_cp, ld_d, ld_n = (sem(n) for n in ("ld_cp", "ld_d", "ld_n"))
        ld_w = [sem("ld_w0"), sem("ld_w1")]
        ld_daz = [sem("ld_daz0"), sem("ld_daz1")]
        ld_din = [sem("ld_din0"), sem("ld_din1")]
        proj, gatep, tr, cb, ds, yp, ssq, outp = (sem(n) for n in (
            "proj", "gatep", "tr", "cb", "ds", "yp", "ssq", "outp"))
        acc, xc_d, xD_d, bt_d, sg_d, zh_d, hi_d = (sem(n) for n in (
            "acc", "xc_d", "xD_d", "bt_d", "sg_d", "zh_d", "hi_d"))
        tap, xdt_d, scan, m_d, s_d, y_d, zf_d, zl_d, o_d, var_d, cst, loo_d = (sem(n) for n in (
            "tap", "xdt_d", "scan", "m_d", "s_d", "y_d", "zf_d", "zl_d", "o_d", "var_d", "cst", "loo_d"))
        xw_d, cd_d, st_d, sq_d, r_d, lo_d, acc_set = (sem(n) for n in (
            "xw_d", "cd_d", "st_d", "sq_d", "r_d", "lo_d", "acc_set"))
        block = ctx.enter_context(nc.Block())
        TAPS = KC - 1
        row = lambda dram, i: dram[bass.ds(i, 1)].rearrange("a p n -> p (a n)")
        O, X, GT = 0, MG, MG + MC
        LOW = MC + MG

        def order(g, k):
            return NPI * (g - (k >= X)) + k

        def low_count(g, k):
            return LOW * (g - 1) + k - X + 1

        def groups(eng, pair):
            pair(0, False)
            with eng.Fori(1, G - 1) as g:
                pair(g, False)
            pair(G - 1, True)

        def steps(eng, step):
            def pair(g, last):
                step(g, 0, (g, 1), last)
                step(g, 1, None if last else (g + 1, 0), last)
            groups(eng, pair)

        @block.sync
        def _(sp):
            def load_piece(g, k):
                if k < 2:
                    if not (isinstance(g, int) and g == 0):
                        sp.wait_ge(lo_d, low_count(g, k + NPI - 2))
                elif k < X:
                    sp.wait_ge(loo_d, MG * g + k - 1)
                elif k < X + 2:
                    sp.wait_ge(loo_d, MG * (g - 1) + k - 1)
                else:
                    sp.wait_ge(lo_d, low_count(g, k - 2))
                sp.dma_start(stage[:, k % 2, :], row(w_pieces, NPI * g + k)).then_inc(ld_w[k % 2], 16)

            def load_conv(g):
                sp.wait_ge(tap, MC * TAPS * 2 * g)
                sp.dma_start(cpar[:].rearrange("p m k -> p (m k)"), row(conv_par, g)).then_inc(ld_cp, 16)

            def load_d(g):
                sp.wait_ge(xD_d, MG * 2 * g)
                sp.dma_start(dpar[:], row(d_par, g)).then_inc(ld_d, 16)

            def load_n(g):
                sp.wait_ge(loo_d, MG * g)
                sp.dma_start(npar[:], row(n_par, g)).then_inc(ld_n, 16)

            def load_daz(g, b, j):
                if not (isinstance(g, int) and g == 0 and b == 0 and j < 2):
                    sp.wait_ge(scan, CH * (2 * g + b) + j - 1)
                src = daz_dram[CH * b + j, bass.ds(HG * g, HG), :].rearrange("h t -> (h t)").partition_broadcast(P)
                sp.dma_start(daz[:, j % 2, :], src).then_inc(ld_daz[j % 2], 16)

            def load_din(g, b, j):
                s = 2 * g + b
                if j == 2:
                    sp.wait_ge(cd_d, (CH - 1) * s)
                else:
                    sp.wait_ge(st_d, 2 * s + (j == 3))
                src = din_dram[CH * b + j, bass.ds(HG * g, HG), :].rearrange("h t -> (h t)").partition_broadcast(P)
                sp.dma_start(din[:, (b + j - 1) % 2].rearrange("p h t -> p (h t)"), src).then_inc(ld_din[(b + j - 1) % 2], 16)

            load_conv(0)
            load_d(0)
            load_daz(0, 0, 0)
            load_daz(0, 0, 1)
            load_n(0)
            load_din(0, 0, 1)
            load_din(0, 0, 2)

            def pair(g, last, first=False):
                if not first:
                    load_d(g)
                    load_n(g)
                load_piece(g, O)
                load_piece(g, O + 1)
                load_daz(g, 0, 2)
                load_piece(g, O + 2)
                load_piece(g, O + 3)
                load_daz(g, 0, 3)
                if not last:
                    load_piece(g + 1, X)
                    load_piece(g + 1, X + 1)
                load_din(g, 0, 3)
                load_daz(g, 1, 0)
                if not last:
                    load_piece(g + 1, X + 2)
                    load_piece(g + 1, X + 3)
                load_daz(g, 1, 1)
                load_din(g, 1, 1)
                load_din(g, 1, 2)
                if not last:
                    load_piece(g + 1, X + 4)
                    load_piece(g + 1, X + 5)
                    load_conv(g + 1)
                load_daz(g, 1, 2)
                if not last:
                    load_piece(g + 1, GT)
                    load_piece(g + 1, GT + 1)
                load_daz(g, 1, 3)
                load_din(g, 1, 3)
                if not last:
                    load_daz(g + 1, 0, 0)
                    load_piece(g + 1, GT + 2)
                    load_piece(g + 1, GT + 3)
                    load_daz(g + 1, 0, 1)
                    load_din(g + 1, 0, 1)
                    load_din(g + 1, 0, 2)

            pair(0, False, first=True)
            with sp.Fori(1, G - 1) as g:
                pair(g, False)
            pair(G - 1, True)

        @block.tensor
        def _(pe):
            def project(g, b, m):
                if b == 0 and not (isinstance(g, int) and g == 0):
                    pe.wait_ge(lo_d, low_count(g, X + m))
                for k in range(KD):
                    last = matmul3(pe, pp[:, m % 2, :], both(wx, slice(None), m, k),
                                   both(xT, slice(None), k, slice(b * L, (b + 1) * L)), k == 0, k == KD - 1)
                last.then_inc(proj, 1)

            def gate(g, b, m):
                s = 2 * g + b
                if b == 0 and not (isinstance(g, int) and g == 0):
                    pe.wait_ge(lo_d, low_count(g, GT + m))
                if m < 2:
                    pe.wait_ge(tap, TAPS * (MC * s + m + MC - 1))
                else:
                    pe.wait_ge(sg_d, MG * s + m - 1)
                for k in range(KD):
                    last = matmul3(pe, pp[:, m % 2, :], both(wg, slice(None), m, k),
                                   both(xT, slice(None), k, slice(b * L, (b + 1) * L)), k == 0, k == KD - 1)
                last.then_inc(gatep, 1)

            def turn_x(g, b, j):
                s = 2 * g + b
                if j == 0:
                    pe.wait_ge(xc_d, MC * s + MG)
                if j < 2:
                    if not (isinstance(s, int) and s == 0):
                        pe.wait_ge(o_d, CH * s + j - 1)
                else:
                    pe.wait_ge(xdt_d, CH * s + j - 1)
                for m in range(MG):
                    last = pe.transpose(pt[:, j % 2, m * P:(m + 1) * P], xc[:, m, j * P:(j + 1) * P], ident[:])
                last.then_inc(tr, 1)

            for m in range(MC):
                if m >= 2:
                    pe.wait_ge(tap, TAPS * (m - 1))
                project(0, 0, m)
            turn_x(0, 0, 0)
            gate(0, 0, 0)

            def step(g, b, nxt, last_group):
                s = 2 * g + b

                def chunk(j):
                    if j < CH - 1:
                        pe.wait_ge(xw_d, (CH - 1) * s + j + 1)
                        if j == 0:
                            pe.wait_ge(bt_d, s + 1)
                        pe.wait_ge(s_d, (CH - 1) * s + j)
                        pe.matmul(pss[:], Bt[:, j, :], Xw[:, (b + j) % 2, :], start=True, stop=True).then_inc(ds, 1)
                    pe.wait_ge(m_d, CH * s + j + 1)
                    pe.wait_ge(var_d, CH * s + max(j - 1, 0))
                    if j:
                        pe.wait_ge(cd_d, (CH - 1) * s + j)
                        pe.wait_ge(s_d, (CH - 1) * s + j)
                    for m in range(MG):
                        for hh in range(2):
                            h = 2 * m + hh
                            dst = py[hh * PH:(hh + 1) * PH, j % 2, m, :]
                            last = pe.matmul(dst, xdt[:, j, h * PH:(h + 1) * PH], M[:, j % 2, h, :], start=True, stop=(j == 0))
                            if j:
                                last = pe.matmul(dst, S[:, (j - 1) % 2, h * PH:(h + 1) * PH], CD[:, (b + j - 1) % 2, h, :],
                                                 start=False, stop=True)
                    last.then_inc(yp, 1)

                def output(j):
                    pe.wait_ge(sq_d, 3 * (CH * s + j + 1))
                    pe.matmul(py[:, j % 2, 0, 0:1], ysq[:, 0, :], ones[:], start=True, stop=True).then_inc(ssq, 1)
                    if j == 0 and b == 0:
                        pe.wait_ge(loo_d, MG * (g + 1))
                    if j == 0:
                        pe.wait_ge(bt_d, s + 1)
                    elif j == 1:
                        pe.wait_ge(xdt_d, CH * (s + 1))
                    else:
                        pe.wait_ge(o_d, CH * s + j - 1)
                    pe.wait_ge(zl_d, CH * s + j + 1)
                    for m in range(MG):
                        last = matmul3(pe, pt[:, j % 2, :], both(z, slice(None), j % 2, m), both(wo, slice(None), m), m == 0, m == MG - 1)
                    last.then_inc(outp, 1)

                def next_tile(m):
                    if nxt is not None:
                        if m < 2:
                            pe.wait_ge(sg_d, MG * s + m + 3)
                        else:
                            pe.wait_ge(tap, TAPS * (MC * (s + 1) + m - 1))
                        project(*nxt, m)

                gate(g, b, 1)
                turn_x(g, b, 1)
                turn_x(g, b, 2)
                gate(g, b, 2)
                turn_x(g, b, 3)
                pe.wait_ge(xc_d, MC * (s + 1))
                pe.wait_ge(xdt_d, CH * s + 3)
                for j in range(CH):
                    last = pe.transpose(pt[:, 0, j * P:(j + 1) * P], Bc[:, j * P:(j + 1) * P], ident[:])
                last.then_inc(tr, 1)
                pe.wait_ge(m_d, CH * s)
                for j in range(CH):
                    last = pe.matmul(pc[:, j, :], Bc[:, j * P:(j + 1) * P], Cc[:, b, j * P:(j + 1) * P], start=True, stop=True)
                last.then_inc(cb, 1)
                gate(g, b, 3)
                chunk(0)
                next_tile(0)
                next_tile(1)
                chunk(1)
                output(0)
                next_tile(2)
                chunk(2)
                output(1)
                next_tile(3)
                next_tile(4)
                chunk(3)
                output(2)
                next_tile(5)
                if nxt is not None:
                    turn_x(*nxt, 0)
                    gate(*nxt, 0)
                output(3)

            steps(pe, step)

        @block.scalar
        def _(act):
            def conv_start(g, b, m):
                s = 2 * g + b
                act.wait_ge(proj, MC * s + m + 1)
                if m == 0:
                    act.wait_ge(ld_cp, 16 * (g + 1))
                act.wait_ge(xc_d, MC * s + max(m - 1, 0))
                act.activation(cv[:, m % 2, :], pp[:, m % 2, :], ACT.Identity, scale=cpar[:, m, KC - 1:KC],
                               bias=cpar[:, m, KC:KC + 1]).then_inc(acc, 1)

            def conv_silu(g, b, m, first=False):
                s = 2 * g + b
                act.wait_ge(tap, TAPS * (MC * s + m + 1))
                if m < MG:
                    dst = xc[:, m, :]
                    if not first:
                        act.wait_ge(tr, (CH + 1) * (s - 1) + CH)
                        act.wait_ge(xD_d, MG * s)
                elif m == MG:
                    dst = Bc[:]
                    if not first:
                        act.wait_ge(cb, s)
                else:
                    dst = Cc[:, b, :]
                    if not first:
                        act.wait_ge(cd_d, (CH - 1) * (s - 1))
                act.activation(dst, cv[:, m % 2, :], ACT.Silu).then_inc(xc_d, 1)

            def high(g, k):
                act.wait_ge(ld_w[k % 2], 16 * (NPI // 2 * (g - (k >= X)) + k // 2 + 1))
                if k < X:
                    if k == 0:
                        act.wait_ge(outp, CH * 2 * g)
                        act.wait_ge(ld_n, 16 * (g + 1))
                    act.activation(wo[0][:, k, :], stage[:, k % 2, :], ACT.Copy, scale=npar[:, k:k + 1]).then_inc(hi_d, 1)
                    return
                if k < GT:
                    dst = wx[0][:, k - X].rearrange("p k n -> p (k n)")
                    act.wait_ge(proj, MC * (2 * g - 1) + k - X + 1)
                else:
                    dst = wg[0][:, k - GT].rearrange("p k n -> p (k n)")
                    act.wait_ge(gatep, MG * (2 * g - 1) + k - GT + 1)
                act.activation(dst, stage[:, k % 2, :], ACT.Copy).then_inc(hi_d, 1)

            def silu_gate(g, b, m):
                s = 2 * g + b
                act.wait_ge(gatep, MG * s + m + 1)
                if m == 0:
                    act.wait_ge(zf_d, CH * s)
                act.activation(sg[:, m, :], pp[:, m % 2, :], ACT.Silu).then_inc(sg_d, 1)

            conv_start(0, 0, 0)
            for m in range(1, MC):
                conv_start(0, 0, m)
                conv_silu(0, 0, m - 1, True)
            conv_silu(0, 0, MC - 1, True)
            silu_gate(0, 0, 0)

            def step(g, b, nxt, last_group):
                s = 2 * g + b

                def high_z(j):
                    act.wait_ge(zf_d, CH * s + j + 1)
                    act.wait_ge(outp, CH * s + max(j - 1, 0))
                    act.activation(z[0][:, j % 2], zf[:], ACT.Copy).then_inc(zh_d, 1)

                def start(m):
                    if nxt is not None:
                        conv_start(*nxt, m)

                def finish(m):
                    if nxt is not None:
                        conv_silu(*nxt, m)

                def split(*pieces):
                    for k in pieces:
                        if k < X or not last_group:
                            high(g + (k >= X), k)

                if b == 0:
                    split(O, O + 1)
                silu_gate(g, b, 1)
                act.wait_ge(ld_d, 16 * (g + 1))
                act.wait_ge(y_d, CH * s)
                act.wait_ge(xc_d, MC * s + MG)
                for m in range(MG):
                    act.activation(xD[:, m, :], xc[:, m, :], ACT.Copy, scale=dpar[:, m:m + 1]).then_inc(xD_d, 1)
                silu_gate(g, b, 2)
                act.wait_ge(tr, (CH + 1) * (s + 1))
                act.wait_ge(ds, (CH - 1) * s)
                act.activation(Bt[:].rearrange("p c n -> p (c n)"), pt[:, 0, :], ACT.Copy).then_inc(bt_d, 1)
                if b == 0:
                    split(O + 2, O + 3)
                else:
                    split(X + 4, X + 5)
                silu_gate(g, b, 3)
                high_z(0)
                start(0)
                if b == 0:
                    split(X)
                else:
                    split(GT)
                start(1)
                finish(0)
                if b == 0:
                    split(X + 1)
                else:
                    split(GT + 1)
                finish(1)
                high_z(1)
                start(2)
                finish(2)
                if b == 0:
                    split(X + 2)
                else:
                    split(GT + 2)
                high_z(2)
                start(3)
                if b == 0:
                    split(X + 3)
                else:
                    split(GT + 3)
                start(4)
                finish(3)
                finish(4)
                high_z(3)
                start(5)
                finish(5)
                if nxt is not None:
                    silu_gate(*nxt, 0)

            steps(act, step)

        @block.vector
        def _(dve):
            dve.memset(ones[:], 1.0).then_inc(cst, 1)
            dve.memset(half[:], -0.5).then_inc(cst, 1)
            for h in range(HG):
                dve.tensor_copy(id8[:, h, :], ident[:]).then_inc(cst, 1)

            def taps(g, b, m):
                s = 2 * g + b
                dve.wait_ge(acc, MC * s + m + 1)
                for i in range(1, KC):
                    if i > 1:
                        dve.wait_ge(tap, TAPS * (MC * s + m) + i - 1)
                    dve.scalar_tensor_tensor(cv[:, m % 2, i:], pp[:, m % 2, :L - i], cpar[:, m, KC - 1 - i:KC - i],
                                             cv[:, m % 2, i:], ALU.mult, ALU.add).then_inc(tap, 1)

            def x_dt(g, b, j):
                s = 2 * g + b
                dve.wait_ge(tr, (CH + 1) * s + j + 1)
                if j == 0:
                    dve.wait_ge(yp, CH * s)
                    dve.wait_ge(xw_d, (CH - 1) * s)
                dtb = dtT[:, CH * b + j, bass.ds(HG * g, HG)].unsqueeze(2).to_broadcast([P, HG, PH])
                dve.tensor_tensor(xdt[:, j, :].rearrange("p (h c) -> p h c", h=HG),
                                  pt[:, j % 2, :].rearrange("p (h c) -> p h c", h=HG), dtb, ALU.mult).then_inc(xdt_d, 1)

            def decays(g, b, j):
                s = 2 * g + b
                dve.wait_ge(ld_daz[j % 2], 16 * (2 * s + j // 2 + 1))
                dve.wait_ge(m_d, CH * s + max(j - 1, 0))
                dve.wait_ge(xw_d, (CH - 1) * s + max(j - 1, 0))
                dve.tensor_tensor_scan(Lm[:, j % 2, :], daz[:, j % 2, :], id8[:].rearrange("p h t -> p (h t)"), 0.0,
                                       ALU.mult, ALU.add).then_inc(scan, 1)

            for m in range(MC):
                taps(0, 0, m)
            dve.wait_ge(cst, 2 + HG)
            dve.wait_ge(acc_set, 1)
            x_dt(0, 0, 0)
            decays(0, 0, 0)

            def step(g, b, nxt, last_group):
                s = 2 * g + b

                def mix(j):
                    dve.wait_ge(scan, CH * s + j + 1)
                    if j == 0:
                        dve.wait_ge(cb, s + 1)
                    if j >= 2:
                        dve.wait_ge(yp, CH * s + j - 1)
                    dve.tensor_tensor(M[:, j % 2], Lm[:, j % 2, :].rearrange("p (h t) -> p h t", h=HG),
                                      pc[:, j, :].unsqueeze(1).to_broadcast([P, HG, P]), ALU.mult).then_inc(m_d, 1)

                def low_out(m):
                    if b == 0:
                        dve.wait_ge(hi_d, order(g, m) + 1)
                        dve.scalar_tensor_tensor(wo[1][:, m, :], stage[:, m % 2, :], npar[:, m:m + 1],
                                                 wo[0][:, m, :].bitcast(F32), ALU.mult, ALU.subtract).then_inc(loo_d, 1)

                def state(j):
                    dve.wait_ge(ds, (CH - 1) * s + j + 1)
                    dve.wait_ge(st_d, 2 * s + j)
                    if j == 0:
                        dve.tensor_copy(S[:, 0, :], pss[:]).then_inc(s_d, 1)
                    else:
                        if j == 2:
                            dve.wait_ge(yp, CH * s + 2)
                        dve.tensor_tensor(S[:, j % 2, :], pss[:], St[:], ALU.add).then_inc(s_d, 1)

                def y_and_z(j):
                    dve.wait_ge(yp, CH * s + j + 1)
                    if j == 0:
                        dve.wait_ge(xD_d, MG * (s + 1))
                    dve.wait_ge(sq_d, 3 * (CH * s + max(j - 1, 0)))
                    dve.wait_ge(zf_d, CH * s + max(j - 1, 0))
                    t = slice(j * P, (j + 1) * P)
                    dve.tensor_tensor(y[:, j % 2], py[:, j % 2], xD[:, :, t], ALU.add).then_inc(y_d, 1)
                    dve.wait_ge(y_d, CH * s + j + 1)
                    if j == 0:
                        dve.wait_ge(sg_d, MG * (s + 1))
                    dve.wait_ge(zl_d, CH * s + j)
                    dve.tensor_tensor(zf[:], y[:, j % 2], sg[:, :, t], ALU.mult).then_inc(zf_d, 1)

                def low_z(j):
                    dve.wait_ge(zh_d, CH * s + j + 1)
                    dve.wait_ge(outp, CH * s + max(j - 1, 0))
                    dve.tensor_tensor(z[1][:, j % 2], zf[:], z[0][:, j % 2].bitcast(F32), ALU.subtract).then_inc(zl_d, 1)

                def variance(j):
                    dve.wait_ge(ssq, CH * s + j + 1)
                    dve.wait_ge(r_d, CH * s)
                    dve.tensor_scalar(var[:, j:j + 1], py[:, j % 2, 0, 0:1], 1.0 / CG, EPS, ALU.mult, ALU.add).then_inc(var_d, 1)

                def add_output(j):
                    dve.wait_ge(r_d, CH * s + j + 1)
                    dve.wait_ge(outp, CH * s + j + 1)
                    dve.wait_ge(o_d, CH * s)
                    i = CH * b + j
                    dve.scalar_tensor_tensor(s_acc[:, i, :], pt[:, j % 2, :], rstd[:, j:j + 1], s_acc[:, i, :],
                                             ALU.mult, ALU.add).then_inc(o_d, 1)

                def next_taps(m):
                    if nxt is not None:
                        taps(*nxt, m)

                x_dt(g, b, 1)
                x_dt(g, b, 2)
                low_out(0)
                low_out(1)
                x_dt(g, b, 3)
                mix(0)
                low_out(2)
                low_out(3)
                decays(g, b, 1)
                y_and_z(0)
                state(0)
                low_z(0)
                mix(1)
                next_taps(0)
                decays(g, b, 2)
                next_taps(1)
                y_and_z(1)
                state(1)
                low_z(1)
                mix(2)
                variance(0)
                add_output(0)
                next_taps(2)
                decays(g, b, 3)
                y_and_z(2)
                state(2)
                low_z(2)
                mix(3)
                variance(1)
                add_output(1)
                next_taps(3)
                next_taps(4)
                y_and_z(3)
                low_z(3)
                variance(2)
                add_output(2)
                next_taps(5)
                if nxt is not None:
                    x_dt(*nxt, 0)
                    decays(*nxt, 0)
                variance(3)
                add_output(3)

            steps(dve, step)

        @block.gpsimd
        def _(pool):
            def low(g, k):
                pool.wait_ge(hi_d, order(g, k) + 1)
                part = lambda i: (wx[i][:, k - X] if k < GT else wg[i][:, k - GT]).rearrange("p k n -> p (k n)")
                pool.tensor_tensor(part(1), stage[:, k % 2, :], part(0).bitcast(F32), ALU.subtract).then_inc(lo_d, 1)

            pool.memset(s_acc[:], 0.0).then_inc(acc_set, 1)
            pool.wait_ge(cst, 2)

            def step(g, b, nxt, last_group):
                s = 2 * g + b

                def weigh_x(j):
                    pool.wait_ge(scan, CH * s + j + 1)
                    pool.wait_ge(xdt_d, CH * s + j + 1)
                    pool.wait_ge(ds, (CH - 1) * s + (j == 2))
                    last = Lm[:, j % 2, :].rearrange("p (h t) -> p h t", h=HG)[:, :, P - 1:P].to_broadcast([P, HG, PH])
                    pool.tensor_tensor(Xw[:, (b + j) % 2, :].rearrange("p (h c) -> p h c", h=HG),
                                       xdt[:, j, :].rearrange("p (h c) -> p h c", h=HG), last, ALU.mult).then_inc(xw_d, 1)

                def scale_c(j):
                    q = (b + j - 1) % 2
                    pool.wait_ge(ld_din[q], 16 * (3 * g + (1, 1, 2, 2, 3, 3)[3 * b + j - 1]))
                    if j == 1:
                        pool.wait_ge(xc_d, MC * (s + 1))
                    pool.wait_ge(yp, CH * s + (2 if j == 3 else 0))
                    pool.tensor_tensor(CD[:, q], din[:, q], Cc[:, b, j * P:(j + 1) * P].unsqueeze(1).to_broadcast([P, HG, P]),
                                       ALU.mult).then_inc(cd_d, 1)

                def decay_state(j):
                    q = (b + j - 1) % 2
                    pool.wait_ge(s_d, (CH - 1) * s + j)
                    last = din[:, q, :, P - 1:P].to_broadcast([P, HG, PH])
                    pool.tensor_tensor(St[:].rearrange("p (h c) -> p h c", h=HG),
                                       S[:, (j - 1) % 2, :].rearrange("p (h c) -> p h c", h=HG), last, ALU.mult).then_inc(st_d, 1)

                def squares(j):
                    n = 3 * (CH * s + j)
                    pool.wait_ge(y_d, CH * s + j + 1)
                    pool.wait_ge(ssq, CH * s + j)
                    pool.tensor_tensor(ysq[:], y[:, j % 2], y[:, j % 2], ALU.mult).then_inc(sq_d, 1)
                    pool.wait_ge(sq_d, n + 1)
                    pool.tensor_tensor(ysq[:, 0:2, :], ysq[:, 0:2, :], ysq[:, 2:4, :], ALU.add).then_inc(sq_d, 1)
                    pool.wait_ge(sq_d, n + 2)
                    pool.tensor_tensor(ysq[:, 0, :], ysq[:, 0, :], ysq[:, 1, :], ALU.add).then_inc(sq_d, 1)

                def root(j):
                    pool.wait_ge(var_d, CH * s + j + 1)
                    pool.wait_ge(o_d, CH * s)
                    pool.tensor_tensor(rstd[:, j:j + 1], var[:, j:j + 1], half[:], ALU.pow).then_inc(r_d, 1)

                def split(*pieces):
                    if not last_group:
                        for k in pieces:
                            low(g + 1, k)

                weigh_x(0)
                scale_c(1)
                if b == 1:
                    split(X + 4, X + 5)
                weigh_x(1)
                squares(0)
                decay_state(1)
                scale_c(2)
                split(X if b == 0 else GT)
                weigh_x(2)
                root(0)
                squares(1)
                decay_state(2)
                scale_c(3)
                split(X + 1 if b == 0 else GT + 1)
                root(1)
                squares(2)
                split(X + 2 if b == 0 else GT + 2)
                split(X + 3 if b == 0 else GT + 3)
                root(2)
                squares(3)
                root(3)

            steps(pool, step)


def moe_phase(nc, w_gu, w_dn, comb_dram, xT, f_acc):
    with ExitStack() as ctx:
        sb = lambda n, s, d=F32: ctx.enter_context(nc.sbuf_tensor(f"mo_{n}", s, d))
        sem = phase_semaphores(nc, ctx, "mo")
        gu_in = sb("gu_in", [P, 2, KD * 2 * P])
        dn_in = sb("dn_in", [P, 2, DM])
        gu = [sb(f"gu{i}", [P, 2, KD, 2 * P], F32R) for i in range(2)]
        dn = [sb(f"dn{i}", [P, 2, EB, DM], F32R) for i in range(2)]
        comb = sb("comb", [P, 2, T])
        sgl = sb("sgl", [P, 2, L])
        sgc = sb("sgc", [P, 2, L])
        af = sb("af", [P, 2, L])
        a = [sb(f"a{i}", [P, EB, T], F32R) for i in range(2)]
        pg = ctx.enter_context(nc.psum_tensor("mo_pg", [P, 2, 512], F32))
        pu = ctx.enter_context(nc.psum_tensor("mo_pu", [P, 2, 512], F32))
        pd = ctx.enter_context(nc.psum_tensor("mo_pd", [P, 2, 512], F32))
        ld_gu, ld_dn, ld_cb = ([sem(f"{n}{i}") for i in range(2)] for n in ("ld_gu", "ld_dn", "ld_cb"))
        gp, up, dp, sl_d, sc_d, af_d, ah_d, al_d, f_d, cst, guh, gul, dnh, dnl = (sem(n) for n in (
            "gp", "up", "dp", "sl_d", "sc_d", "af_d", "ah_d", "al_d", "f_d", "cst", "guh", "gul", "dnh", "dnl"))
        block = ctx.enter_context(nc.Block())
        ld_first, first_high, first_low = [sem("ld_first0"), sem("ld_first1")], sem("first_high"), sem("first_low")
        HALF = KD * P
        UN = EB * NB
        units = [(e, b) for e in range(EB) for b in range(NB)]

        def chunks(eng, one):
            one(0, 0)
            with eng.Fori(0, EC // 2) as i:
                one(2 * i + 1, 1)
                one(2 * i + 2, 0)

        def chunks_but_last(eng, one):
            one(0, 0)
            with eng.Fori(1, EC // 2) as i:
                one(2 * i - 1, 1)
                one(2 * i, 0)
            one(EC - 2, 1)
            one(EC - 1, 0)

        @block.sync
        def _(sp):
            for e in range(NE):
                q = e % 2
                if e == 0:
                    for i in range(2):
                        sp.dma_start(gu_in[:, 0, i * HALF:(i + 1) * HALF], w_gu[0, :, i * HALF:(i + 1) * HALF]).then_inc(ld_first[i], 16)
                else:
                    if e == 2:
                        sp.wait_ge(first_low, 2)
                    elif e > 2:
                        sp.wait_ge(gul, e - 2)
                    sp.dma_start(gu_in[:, q, :], w_gu[e]).then_inc(ld_gu[q], 16)
                if e >= 2:
                    sp.wait_ge(sc_d, NB * (e - 1))
                sp.dma_start(comb[:, q, :], comb_dram[e].partition_broadcast(P)).then_inc(ld_cb[q], 16)
                if e >= 2:
                    sp.wait_ge(dnl, e - 1)
                sp.dma_start(dn_in[:, q, :], w_dn[e]).then_inc(ld_dn[q], 16)

        @block.tensor
        def _(pe):
            def one(c, q):
                for u, (e, b) in enumerate(units):
                    x = lambda k: both(xT, slice(None), k, slice(b * L, (b + 1) * L))
                    start = isinstance(c, int) and u == 0
                    if b == 0 and not start:
                        pe.wait_ge(gul, EB * c + e)
                    pe.wait_ge(sl_d, UN * c + max(u - 1, 0))
                    for k in range(KD):
                        if start and k % 2 == 0:
                            pe.wait_ge(first_low, k // 2 + 1)
                        last = matmul3(pe, pg[:, b, :], both(gu, slice(None), e % 2, k, slice(0, P)), x(k), k == 0, k == KD - 1)
                    last.then_inc(gp, 1)
                    pe.wait_ge(af_d, UN * c + max(u - 1, 0))
                    for k in range(KD):
                        last = matmul3(pe, pu[:, b, :], both(gu, slice(None), e % 2, k, slice(P, 2 * P)), x(k), k == 0, k == KD - 1)
                    last.then_inc(up, 1)
                pe.wait_ge(dnl, EB * (c + 1))
                for i in range(TT):
                    if i == 0:
                        pe.wait_ge(al_d, UN * (c + 1) - 1)
                    if i == TT // NB:
                        pe.wait_ge(al_d, UN * (c + 1))
                    pe.wait_ge(f_d, TT * c + max(i - 1, 0))
                    for e in range(EB):
                        last = matmul3(pe, pd[:, i % 2, :], both(a, slice(None), e, slice(i * P, (i + 1) * P)),
                                       both(dn, slice(None), q, e), e == 0, e == EB - 1)
                    last.then_inc(dp, 1)
            chunks(pe, one)

        @block.scalar
        def _(act):
            def high(c, q, e):
                n = EB * c + e
                qe, qc = e % 2, (q + (e >= EB)) % 2
                dst = gu[0][:, qe].rearrange("p k n -> p (k n)")
                if isinstance(n, int) and n == 0:
                    for i in range(2):
                        act.wait_ge(ld_first[i], 16)
                        act.activation(dst[:, i * HALF:(i + 1) * HALF], gu_in[:, 0, i * HALF:(i + 1) * HALF], ACT.Copy).then_inc(first_high, 1)
                else:
                    act.wait_ge(ld_gu[qe], 8 * (n + qe))
                    if not isinstance(n, int) or n >= 2:
                        act.wait_ge(up, NB * (n - 1))
                    act.activation(dst, gu_in[:, qe, :], ACT.Copy).then_inc(guh, 1)
                act.wait_ge(ld_dn[qe], 8 * (n - qe) + 16)
                act.wait_ge(dp, TT * (c - 1 + (e >= EB)) if not isinstance(c, int) or c + (e >= EB) >= 2 else 0)
                act.activation(dn[0][:, qc, e % EB, :], dn_in[:, qe, :], ACT.Copy).then_inc(dnh, 1)

            high(0, 0, 0)
            high(0, 0, 1)

            def one(c, q):
                for u, (e, b) in enumerate(units):
                    act.wait_ge(gp, UN * c + u + 1)
                    act.wait_ge(sc_d, UN * c + max(u - 1, 0))
                    act.activation(sgl[:, b, :], pg[:, b, :], ACT.Silu).then_inc(sl_d, 1)
                    act.wait_ge(af_d, UN * c + u + 1)
                    if u == 0:
                        act.wait_ge(dp, TT * c)
                    act.activation(a[0][:, e, b * L:(b + 1) * L], af[:, b, :], ACT.Copy).then_inc(ah_d, 1)
                    if b == 1 and not (isinstance(c, int) and c == EC - 1 and e >= EB - 2):
                        high(c, q, e + 2)
            chunks_but_last(act, one)

        @block.gpsimd
        def _(pool):
            def low(n, qe):
                pool.wait_ge(guh, n)
                pool.tensor_tensor(gu[1][:, qe].rearrange("p k n -> p (k n)"), gu_in[:, qe, :],
                                   gu[0][:, qe].rearrange("p k n -> p (k n)").bitcast(F32), ALU.subtract).then_inc(gul, 1)

            low(1, 1)

            def one(c, q):
                for u, (e, b) in enumerate(units):
                    if b == 0:
                        pool.wait_ge(ld_cb[e % 2], 8 * (EB * c + e - e % 2) + 16)
                    pool.wait_ge(sl_d, UN * c + u + 1)
                    pool.wait_ge(af_d, UN * c + max(u - 1, 0))
                    pool.tensor_tensor(sgc[:, b, :], sgl[:, b, :], comb[:, e % 2, b * L:(b + 1) * L], ALU.mult).then_inc(sc_d, 1)
                    if b == 1 and not (isinstance(c, int) and c == EC - 1 and e >= EB - 2):
                        low(EB * c + e + 2, e % 2)
            chunks_but_last(pool, one)

        @block.vector
        def _(dve):
            for i in range(2):
                dve.wait_ge(first_high, i + 1)
                flat = lambda a: a[:, 0].rearrange("p k n -> p (k n)")[:, i * HALF:(i + 1) * HALF]
                dve.tensor_tensor(flat(gu[1]), gu_in[:, 0, i * HALF:(i + 1) * HALF], flat(gu[0]).bitcast(F32), ALU.subtract).then_inc(first_low, 1)
            dve.memset(f_acc[:], 0.0).then_inc(cst, 1)

            def low_down(c, q, e):
                qe, qc = e % 2, (q + (e >= EB)) % 2
                dve.wait_ge(dnh, EB * c + e + 1)
                dve.tensor_tensor(dn[1][:, qc, e % EB, :], dn_in[:, qe, :], dn[0][:, qc, e % EB, :].bitcast(F32),
                                  ALU.subtract).then_inc(dnl, 1)

            low_down(0, 0, 0)
            low_down(0, 0, 1)

            def one(c, q):
                for u, (e, b) in enumerate(units):
                    dve.wait_ge(up, UN * c + u + 1)
                    dve.wait_ge(sc_d, UN * c + u + 1)
                    dve.wait_ge(al_d, UN * c + max(u - 1, 0))
                    dve.tensor_tensor(af[:, b, :], pu[:, b, :], sgc[:, b, :], ALU.mult).then_inc(af_d, 1)
                    dve.wait_ge(ah_d, UN * c + u + 1)
                    part = (slice(None), e, slice(b * L, (b + 1) * L))
                    dve.tensor_tensor(a[1][part], af[:, b, :], a[0][part].bitcast(F32), ALU.subtract).then_inc(al_d, 1)
                    if b == 1 and not (isinstance(c, int) and c == EC - 1 and e >= EB - 2):
                        low_down(c, q, e + 2)
                dve.wait_ge(cst, 1)
                dve.wait_ge(f_d, TT * c)
                for i in range(TT):
                    dve.wait_ge(dp, TT * c + i + 1)
                    dve.tensor_tensor(f_acc[:, i, :], pd[:, i % 2, :], f_acc[:, i, :], ALU.add).then_inc(f_d, 1)
            chunks_but_last(dve, one)


def qkv_phase(nc, wq, w_k, w_v, rot_dram, cos_dram, sin_dram, w_r, xT, ident, V1, q_stack, k_stack, g_dram):
    with ExitStack() as ctx:
        sb = lambda n, s, d=F32: ctx.enter_context(nc.sbuf_tensor(f"qk_{n}", s, d))
        sem = phase_semaphores(nc, ctx, "qk")
        stage = sb("stage", [P, 2, KD, DM])
        w = [wq] + [[sb(f"{n}{i}", [P, KD, DM], F32R) for i in range(2)] for n in ("wk", "wv")]
        rot = sb("rot", [P, P])
        cos = sb("cos", [P, L])
        sin = sb("sin", [P, L])
        raw = sb("raw", [P, 2, L])
        t1 = sb("t1", [P, 2, L])
        t2 = sb("t2", [P, 2, L])
        qr = sb("qr", [P, 2, L])
        r1 = sb("r1", [P, 2, L])
        parts = sb("parts", [P, 2, 3, L], BF16)
        wr_in = sb("wr_in", [P, KD, NA])
        wr = [sb(f"wr{i}", [P, KD, NA], F32R) for i in range(2)]
        lgT = sb("lgT", [NA, T])
        lg = sb("lg", [P, TT, NA])
        v8 = sb("v8", [P, TT, 2, 8])
        rest = sb("rest", [P, TT, 2, NA])
        sh = sb("sh", [P, TT, NA])
        ex = sb("ex", [P, TT, NA])
        tk = sb("tk", [P, TT, NA])
        sm = sb("sm", [P, TT, 1])
        gT = sb("gT", [NA, T])
        pq = ctx.enter_context(nc.psum_tensor("qk_pq", [P, 2, 512], F32))
        pr = ctx.enter_context(nc.psum_tensor("qk_pr", [P, 2, 512], F32))
        pl = ctx.enter_context(nc.psum_tensor("qk_pl", [P, 2, 512], F32))
        ld_r, chain, rh_d, rl_d, lp, lT_d, tr, lg_d, gates_d, ex_d, sh_d, gt, gT_d, g_st = (sem(n) for n in (
            "ld_r", "chain", "rh_d", "rl_d", "lp", "lT_d", "tr", "lg_d", "gates_d", "ex_d", "sh_d", "gt", "gT_d", "g_st"))
        ld = [sem(f"ld{i}") for i in range(2)]
        ldc, proj, rotd, raw_d, t1_d, t2_d, qr_d, p1_d, r1_d, p2_d, p3_d, vp, v_d, vz = (sem(n) for n in (
            "ldc", "proj", "rotd", "raw_d", "t1_d", "t2_d", "qr_d", "p1_d", "r1_d", "p2_d", "p3_d", "vp", "v_d", "vz"))
        st = [sem("st0"), sem("st1")]
        wh_d, wl_d = sem("wh_d"), [sem(f"wl_d{i}") for i in range(2)]
        block = ctx.enter_context(nc.Block())
        items = [(b, i, m) for b in range(NB) for i in range(2) for m in range(KD)]
        N = len(items)

        @block.sync
        def _(sp):
            for i, src in ((1, w_k), (2, w_v)):
                sp.dma_start(stage[:, i - 1].rearrange("p k n -> p (k n)"), src).then_inc(ld[i - 1], 16)
                if i == 1:
                    for dst, src in ((rot[:], rot_dram), (cos[:], cos_dram), (sin[:], sin_dram)):
                        sp.dma_start(dst, src).then_inc(ldc, 16)
            sp.dma_start(wr_in[:].rearrange("p k n -> p (k n)"), w_r).then_inc(ld_r, 16)
            for n, (b, i, m) in enumerate(items):
                sp.wait_ge(p3_d, n + 1)
                sp.wait_ge(p1_d, n + 1)
                sp.wait_ge(p2_d, n + 1)
                at = 0
                for r in RUNS:
                    src = parts[:, n % 2, 0:r] if i == 0 else parts[:, n % 2, 3 - r:4 - r].to_broadcast([P, r, L])
                    sp.dma_start((q_stack, k_stack)[i][b, m, at:at + r].rearrange("a p t -> p a t"), src).then_inc(st[n % 2], 16)
                    at += r
            sp.wait_ge(gT_d, TT)
            sp.dma_start(g_dram, gT[:]).then_inc(g_st, 16)
            sp.wait_ge(g_st, 16)
            for i in range(2):
                sp.wait_ge(st[i], 16 * len(RUNS) * N // 2)

        @block.tensor
        def _(pe):
            def rotate(n):
                pe.wait_ge(raw_d, n + 1)
                if n >= 2:
                    pe.wait_ge(t1_d, n - 1)
                if n == 0:
                    pe.wait_ge(ldc, 48)
                pe.matmul(pr[:, n % 2, :], rot[:], raw[:, n % 2, :], start=True, stop=True).then_inc(rotd, 1)

            for n, (b, i, m) in enumerate(items):
                if i == 1 and b == 0:
                    pe.wait_ge(wl_d[0], 1)
                if n >= 2:
                    pe.wait_ge(raw_d, n - 1)
                for k in range(KD):
                    last = matmul3(pe, pq[:, n % 2, :], both(w[i], slice(None), k, slice(m * P, (m + 1) * P)),
                                   both(xT, slice(None), k, slice(b * L, (b + 1) * L)), k == 0, k == KD - 1)
                last.then_inc(proj, 1)
                if n:
                    rotate(n - 1)
            rotate(N - 1)
            pe.wait_ge(rl_d, 1)
            for b in range(NB):
                for k in range(KD):
                    last = matmul3(pe, pl[0:NA, b, :], both(wr, slice(None), k), both(xT, slice(None), k, slice(b * L, (b + 1) * L)),
                                   k == 0, k == KD - 1)
                last.then_inc(lp, 1)
            pe.wait_ge(wl_d[1], 1)
            for i in range(TT):
                if i == 1:
                    pe.wait_ge(lT_d, NB)
                    for t in range(TT):
                        if t >= 2:
                            pe.wait_ge(lg_d, t - 1)
                        pe.transpose(pl[:, t % 2, 0:NA], lgT[:, t * P:(t + 1) * P], ident[0:NA, 0:NA]).then_inc(tr, 1)
                if i == TT - 1:
                    pe.wait_ge(gates_d, 1)
                    for t in range(TT):
                        if t < 2:
                            pe.wait_ge(lg_d, TT)
                        else:
                            pe.wait_ge(gT_d, t - 1)
                        pe.transpose(pl[0:NA, t % 2, 0:P], tk[:, t, :], ident[:]).then_inc(gt, 1)
                if i < 2:
                    pe.wait_ge(raw_d, N)
                else:
                    pe.wait_ge(v_d, i - 1)
                for k in range(KD):
                    last = matmul3(pe, pq[:, i % 2, :], both(xT, slice(None), k, slice(i * P, (i + 1) * P)),
                                   both(w[2], slice(None), k), k == 0, k == KD - 1)
                last.then_inc(vp, 1)
        @block.scalar
        def _(act):
            def first_part(n):
                act.wait_ge(qr_d, n + 1)
                if n >= 2:
                    act.wait_ge(st[n % 2], 16 * len(RUNS) * (n // 2))
                act.activation(parts[:, n % 2, 0, :], qr[:, n % 2, :], ACT.Copy).then_inc(p1_d, 1)

            def second_part(n):
                act.wait_ge(r1_d, n + 1)
                act.activation(parts[:, n % 2, 1, :], r1[:, n % 2, :], ACT.Copy).then_inc(p2_d, 1)

            def high(i):
                act.wait_ge(ld[i - 1], 16)
                act.activation(w[i][0][:], stage[:, i - 1], ACT.Copy).then_inc(wh_d, 1)

            high(1)
            for n in range(N):
                if n == KD:
                    high(2)
                    act.wait_ge(ld_r, 16)
                    act.activation(wr[0][:], wr_in[:], ACT.Copy).then_inc(rh_d, 1)
                act.wait_ge(proj, n + 1)
                if n >= 2:
                    act.wait_ge(rotd, n - 1)
                    act.wait_ge(t2_d, n - 1)
                act.activation(raw[:, n % 2, :], pq[:, n % 2, :], ACT.Copy).then_inc(raw_d, 1)
                if n >= 2:
                    second_part(n - 2)
                if n:
                    first_part(n - 1)
            second_part(N - 2)
            first_part(N - 1)
            second_part(N - 1)
            for b in range(NB):
                act.wait_ge(lp, b + 1)
                act.activation(lgT[:, b * L:(b + 1) * L], pl[0:NA, b, :], ACT.Copy).then_inc(lT_d, 1)
            act.wait_ge(vz, 1)
            for i in range(TT):
                if i == TT - 3:
                    act.wait_ge(sh_d, TT)
                    act.activation(ex[:], sh[:], ACT.Exp).then_inc(ex_d, 1)
                act.wait_ge(vp, i + 1)
                act.activation(V1[:, i, :, 0:HD], pq[:, i % 2, :].rearrange("p (h d) -> p h d", d=HD), ACT.Copy).then_inc(v_d, 1)

        @block.gpsimd
        def _(pool):
            def low(i):
                pool.wait_ge(wh_d, i)
                pool.tensor_tensor(w[i][1][:], stage[:, i - 1], w[i][0][:].bitcast(F32), ALU.subtract).then_inc(wl_d[i - 1], 1)

            pool.wait_ge(ldc, 48)
            for n in range(N):
                if n == 1:
                    low(1)
                if n == KD:
                    low(2)
                if n == KD + 2:
                    pool.wait_ge(rh_d, 1)
                    pool.tensor_tensor(wr[1][:], wr_in[:], wr[0][:].bitcast(F32), ALU.subtract).then_inc(rl_d, 1)
                if n == 2 * KD:
                    pool.memset(V1[:], 1.0).then_inc(vz, 1)
                pool.wait_ge(raw_d, n + 1)
                if n >= 2:
                    pool.wait_ge(qr_d, n - 1)
                pool.tensor_tensor(t2[:, n % 2, :], raw[:, n % 2, :], cos[:], ALU.mult).then_inc(t2_d, 1)

        @block.vector
        def _(dve):
            def rotary(n):
                dve.wait_ge(rotd, n + 1)
                if n == 0:
                    dve.wait_ge(ldc, 48)
                if n >= 2:
                    dve.wait_ge(qr_d, n - 1)
                dve.tensor_tensor(t1[:, n % 2, :], pr[:, n % 2, :], sin[:], ALU.mult).then_inc(t1_d, 1)

            def total(n):
                dve.wait_ge(t1_d, n + 1)
                dve.wait_ge(t2_d, n + 1)
                if n >= 2:
                    dve.wait_ge(p1_d, n - 1)
                    dve.wait_ge(r1_d, n - 1)
                dve.tensor_tensor(qr[:, n % 2, :], t1[:, n % 2, :], t2[:, n % 2, :], ALU.add).then_inc(qr_d, 1)

            def first_rest(n):
                dve.wait_ge(p1_d, n + 1)
                if n >= 2:
                    dve.wait_ge(p3_d, n - 1)
                    dve.wait_ge(p2_d, n - 1)
                dve.tensor_tensor(r1[:, n % 2, :], qr[:, n % 2, :], parts[:, n % 2, 0, :], ALU.subtract).then_inc(r1_d, 1)

            def third_part(n):
                dve.wait_ge(p2_d, n + 1)
                dve.tensor_tensor(parts[:, n % 2, 2, :], r1[:, n % 2, :], parts[:, n % 2, 1, :], ALU.subtract).then_inc(p3_d, 1)

            for n in range(N + 1):
                if n < N:
                    rotary(n)
                if n:
                    first_rest(n - 1)
                if n < N:
                    total(n)
                if n:
                    third_part(n - 1)

            links = [0]

            def link(ins):
                links[0] += 1
                ins.then_inc(chain, 1)
                dve.wait_ge(chain, links[0])

            for i in range(TT):
                dve.wait_ge(tr, i + 1)
                dve.tensor_copy(lg[:, i, :], pl[:, i % 2, 0:NA]).then_inc(lg_d, 1)
            for i in range(TT):
                dve.wait_ge(lg_d, i + 1)
                link(dve.max(v8[:, i, 0, :], lg[:, i, :]))
                dve.tensor_scalar(sh[:, i, :], lg[:, i, :], v8[:, i, 0, 0:1], None, ALU.subtract).then_inc(sh_d, 1)
                link(dve.match_replace(rest[:, i, 0, :], v8[:, i, 0, :], lg[:, i, :], NEG))
                link(dve.max(v8[:, i, 1, :], rest[:, i, 0, :]))
                link(dve.match_replace(rest[:, i, 1, :], v8[:, i, 1, :], rest[:, i, 0, :], NEG))
            link(dve.tensor_tensor(tk[:], lg[:], rest[:, :, 1, :], ALU.not_equal))
            dve.wait_ge(ex_d, 1)
            link(dve.tensor_tensor(tk[:], tk[:], ex[:], ALU.mult))
            link(dve.tensor_reduce(sm[:], tk[:], AX.X, ALU.add))
            link(dve.reciprocal(sm[:], sm[:]))
            dve.tensor_tensor(tk[:], tk[:], sm[:].to_broadcast([P, TT, NA]), ALU.mult).then_inc(gates_d, 1)
            for i in range(TT):
                dve.wait_ge(gt, i + 1)
                dve.tensor_copy(gT[:, i * P:(i + 1) * P], pl[0:NA, i % 2, 0:P]).then_inc(gT_d, 1)


def attention_phase(nc, q_stack, k_stack, V1, w_o, mask_dram, maskT_dram, ident, s_acc, g_dram, g_ranks, rows_dram):
    with ExitStack() as ctx:
        sb = lambda n, s, d=F32: ctx.enter_context(nc.sbuf_tensor(f"at_{n}", s, d))
        sem = phase_semaphores(nc, ctx, "at")
        NU = NB * HN // HU
        UB = NU // NB
        NP = NU // 2
        SB, PR = 4, 6
        QS = [sb(f"QS{i}", [KR, HU, L], BF16) for i in range(SB)]
        KS = [sb(f"KS{i}", [KR, HU, L], BF16) for i in range(SB)]
        wo_in = sb("wo_in", [P, 2, DM])
        wo = [sb(f"wo{i}", [P, KD, DM], F32R) for i in range(2)]
        mask = sb("mask", [P, L])
        maskf = sb("maskf", [P, P])
        maskT = sb("maskT", [P, P], BF16)
        identb = sb("identb", [P, P], BF16)
        junk = sb("junk", [P, 2, L], BF16)
        mx = sb("mx", [P, 2, TH, HU])
        nm = sb("nm", [HU, L])
        nr = sb("nr", [HU, L])
        nparts = sb("nparts", [HU, 3, L], BF16)
        PT = sb("PT", [P, PR, PTW])
        oT = sb("oT", [P, 2, L])
        num = sb("num", [P, 2, L])
        den = sb("den", [P, 2, L])
        rden = sb("rden", [P, L])
        on = sb("on", [P, L])
        ons = [sb(f"on{i}", [P, KD, L], F32R) for i in range(2)]
        p1 = ctx.enter_context(nc.psum_tensor("at_p1", [P, 3, 512], F32))
        p2 = ctx.enter_context(nc.psum_tensor("at_p2", [P, 3, 512], F32))
        po = ctx.enter_context(nc.psum_tensor("at_po", [P, 512], F32))
        px = ctx.enter_context(nc.psum_tensor("at_px", [P, 512], F32))
        ldc, ld_wo, const_d, wh_d, wl_d = sem("ldc"), [sem("ld_wo0"), sem("ld_wo1")], sem("const_d"), sem("wh_d"), sem("wl_d")
        ldq = [sem(f"ldq{i}") for i in range(SB)]
        ldm = [sem(f"ldm{i}") for i in range(SB)]
        s1, mx_d, mt, nm_d, nr_d, np1_d, np2_d, np3_d, s2, ex_d, pv, oT_d, on_d, oh_d, ol_d, fo, f_d = (sem(n) for n in (
            "s1", "mx_d", "mt", "nm_d", "nr_d", "np1_d", "np2_d", "np3_d", "s2", "ex_d", "pv", "oT_d", "on_d", "oh_d",
            "ol_d", "fo", "f_d"))
        spread = sem("spread")
        bounced = [sem("bounced0"), sem("bounced1")]
        GP = NU
        ont_d, oht_d, olt_d = sem("ont_d"), sem("oht_d"), sem("olt_d")
        tile = lambda t: slice(t * P, (t + 1) * P)
        rden_d, rows_d = sem("rden_d"), sem("rows_d")
        packed = [sem("packed0"), sem("packed1")]
        block = ctx.enter_context(nc.Block())
        UT = HU * TH
        off = [sum(L - P * i for i in range(j)) for j in range(TH)]

        OUT0 = UB + 3
        px_order = [("m", 0)]
        for v in range(NU):
            if v + 1 < NU:
                px_order.append(("m", v + 1))
            if v == OUT0:
                px_order += [("o", i) for i in range(TH)]
        px_order.append(("o", TT - 1))
        last_bank = [p1[:, i, :] for i in range(3)] + [px[:]]
        out_bank = lambda i: px[:] if i < TH else last_bank[i - TH]

        def px_free(eng, use):
            at = px_order.index(use)
            if at:
                kind, i = px_order[at - 1]
                if kind == "m":
                    eng.wait_ge(nm_d, i + 1)
                    eng.wait_ge(np1_d, i + 1)
                else:
                    eng.wait_ge(f_d, i + 1)

        @block.sync
        def _(sp):
            def load(w):
                b, m, q = w // UB, w % UB, w % SB
                if w >= SB:
                    sp.wait_ge(s2, UT * (w - SB + 1))
                for dst, src in ((QS[q], q_stack), (KS[q], k_stack)):
                    rows = src[b, m // 2].rearrange("a (d h) t -> (a d) h t", d=HD)
                    sp.dma_start(dst[0:KB, :, :], rows[:, m % 2 * HU:(m % 2 + 1) * HU, :]).then_inc(ldq[q], 16)

            def load_wo(k):
                if k >= 2:
                    sp.wait_ge(wl_d, k - 1)
                sp.dma_start(wo_in[:, k % 2, :], w_o[:, k * DM:(k + 1) * DM]).then_inc(ld_wo[k % 2], 16)

            def maxima_rows(w):
                sp.wait_ge(np1_d, w + 1)
                sp.wait_ge(np2_d, w + 1)
                sp.wait_ge(np3_d, w + 1)
                for i in range(3):
                    sp.dma_start(QS[w % SB][KB + i:KB + i + 1, :, :], nparts[:, i, :]).then_inc(ldm[w % SB], 16)

            def pack(w):
                sp.wait_ge(oT_d, w + 1)
                if w >= 4:
                    sp.wait_ge(on_d, w // 2 - 1)
                sp.dma_start(rows_dram[w % 2], oT[:, w % 2, :]).then_inc(bounced[w % 2], 16)
                sp.wait_ge(bounced[w % 2], 16 * (w // 2 + 1))
                heads = rows_dram[w % 2].rearrange("(c x r) t -> x c r t", x=2, r=HD)
                for x, dst in enumerate((num, den)):
                    sp.dma_start(dst[(w % 2) * HU * HD:(w % 2 + 1) * HU * HD, w // 2 % 2, :], heads[x]).then_inc(packed[w % 2], 16)

            load(0)
            sp.dma_start(mask[:], mask_dram).then_inc(ldc, 16)
            sp.dma_start(maskf[:], maskT_dram).then_inc(ldc, 16)
            load(1)
            load(2)
            load_wo(0)
            load_wo(1)
            maxima_rows(0)
            for v in range(NU):
                if v + 3 < NU:
                    load(v + 3)
                if v + 1 < NU:
                    maxima_rows(v + 1)
                if v:
                    pack(v - 1)
                if v in (1, 2):
                    load_wo(v + 1)
                a = slice(v * NA // GP, (v + 1) * NA // GP)
                sp.dma_start(g_ranks.rearrange("(a r) t -> a r t", r=RK)[a],
                             g_dram[a].unsqueeze(1).to_broadcast([NA // GP, RK, T])).then_inc(spread, 16)
            pack(NU - 1)
            sp.wait_ge(spread, 16 * GP)

        @block.tensor
        def _(pe):
            def maxima(w, h, i):
                q = w % SB
                if h == 0 and i == 0:
                    pe.wait_ge(ldq[q], 16 * 2 * (w // SB + 1))
                n = (w * HU + h) * TH + i
                if n >= 3:
                    pe.wait_ge(mx_d, n - 2)
                pe.matmul(p1[:, n % 3, 0:(i + 1) * P], QS[q][0:KB, h, i * P:(i + 1) * P], KS[q][0:KB, h, 0:(i + 1) * P],
                          start=True, stop=True).then_inc(s1, 1)

            def turn_maxima(w):
                pe.wait_ge(mx_d, UT * (w + 1))
                px_free(pe, ("m", w))
                for i in range(TH):
                    last = pe.transpose(px[0:HU, i * P:(i + 1) * P], mx[:, w % 2, i, :], ident[:])
                last.then_inc(mt, 1)

            def scores(v, h, j):
                q = v % SB
                if h == 0 and j == 0:
                    pe.wait_ge(ldm[q], 48 * (v // SB + 1))
                n = (v * HU + h) * TH + j
                if n >= 3:
                    pe.wait_ge(ex_d, n - 2)
                pe.matmul(p2[:, n % 3, 0:L - j * P], KS[q][:, h, j * P:(j + 1) * P], QS[q][:, h, j * P:L], start=True, stop=False)
                pe.matmul(p2[:, n % 3, 0:P], identb[:], maskT[:], start=False, stop=True).then_inc(s2, 1)

            def values(v, j):
                if j == 0:
                    pe.wait_ge(ex_d, UT * (v + 1))
                    pe.wait_ge(oT_d, v)
                for c in range(HU):
                    last = pe.matmul(po[32 * c:32 * c + 32, j * P:L], V1[:, v // UB * TH + j, v % UB * HU + c, :],
                                     PT[:, (v * HU + c) % PR, off[j]:off[j] + L - j * P],
                                     start=(j == 0), stop=(j == TH - 1), skip_group_check=True)
                if j == TH - 1:
                    last.then_inc(pv, 1)

            def output(i, k):
                if i // TH == NB - 1 and k == KD - 1:
                    pe.wait_ge(olt_d, i % TH + 1)
                else:
                    pe.wait_ge(ol_d, KD * (i // TH) + k + 1)
                if k == 0:
                    pe.wait_ge(wl_d, KD)
                    if ("o", i) in px_order:
                        px_free(pe, ("o", i))
                    else:
                        pe.wait_ge(mx_d, UT * NU)
                last = matmul3(pe, out_bank(i), both(ons, slice(None), k, slice(i % TH * P, (i % TH + 1) * P)), both(wo, slice(None), k),
                               k == 0, k == KD - 1)
                if k == KD - 1:
                    last.then_inc(fo, 1)

            for w in range(2):
                for h in range(HU):
                    for i in range(TH):
                        maxima(w, h, i)
                    if w == 1 and h == 0:
                        turn_maxima(0)
            pe.wait_ge(const_d, 2)
            pe.wait_ge(rows_d, SB)
            for v in range(NU):
                for h in range(HU):
                    for i in range(TH):
                        if v + 2 < NU:
                            maxima(v + 2, h, i)
                        if h == 0 and i == 1 and v + 1 < NU:
                            turn_maxima(v + 1)
                        scores(v, h, i)
                        if h == 1 and v:
                            values(v - 1, i)
                        if v == OUT0 and h:
                            output(h - 1, i)
                        if v == NU - 1 and i >= 2:
                            output(TH + h, i - 2)
                if v == OUT0:
                    for k in range(KD):
                        output(TH - 1, k)
            for i in range(TH):
                values(NU - 1, i)
            for k in range(2, KD):
                for i in range(TH, TT):
                    output(i, k)

        @block.scalar
        def _(act):
            def negate(w):
                act.wait_ge(mt, w + 1)
                if w:
                    act.wait_ge(np3_d, w)
                    act.wait_ge(ldm[(w - 1) % SB], 48 * ((w - 1) // SB + 1))
                act.activation(nm[:], px[0:HU, :], ACT.Copy, scale=-1.0).then_inc(nm_d, 1)
                act.activation(nparts[:, 0, :], px[0:HU, :], ACT.Copy, scale=-1.0).then_inc(np1_d, 1)

            def second_part(w):
                act.wait_ge(nr_d, w + 1)
                act.activation(nparts[:, 1, :], nr[:], ACT.Copy).then_inc(np2_d, 1)

            def weigh(v, h):
                for j in range(TH):
                    n = (v * HU + h) * TH + j
                    k = v * HU + h
                    act.wait_ge(s2, n + 1)
                    if k >= PR:
                        act.wait_ge(pv, (k - PR) // HU + 1)
                    if h == 0 and j == 2 and v + 1 < NU:
                        negate(v + 1)
                    if h == 1 and j == 1 and v + 1 < NU:
                        second_part(v + 1)
                    w = L - j * P
                    act.activation(PT[:, k % PR, off[j]:off[j] + w], p2[:, n % 3, 0:w], ACT.Exp, scale=HD ** -0.5).then_inc(ex_d, 1)

            def copy_values(v):
                act.wait_ge(pv, v + 1)
                if v >= 2:
                    act.wait_ge(packed[v % 2], 16 * 2 * (v // 2))
                act.activation(oT[:, v % 2, :], po[:], ACT.Copy).then_inc(oT_d, 1)

            def high(p):
                act.wait_ge(on_d, p + 1)
                if p % KD == 0 and p:
                    act.wait_ge(fo, TH * (p // KD))
                act.activation(ons[0][:, p % KD, :], on[:], ACT.Copy).then_inc(oh_d, 1)

            def copy_output(i):
                act.wait_ge(fo, i + 1)
                act.activation(s_acc[:, i, :], out_bank(i), ACT.Copy).then_inc(f_d, 1)

            negate(0)
            second_part(0)
            for v in range(NU):
                for h in range(HU):
                    weigh(v, h)
                    if h == 1 and v:
                        copy_values(v - 1)
                    if h == HU - 1 and v >= 4 and v % 2 == 0:
                        high((v - 4) // 2)
                    if h == HU - 1 and v < KD:
                        act.wait_ge(ld_wo[v % 2], 16 * (v // 2 + 1))
                        act.activation(wo[0][:, v, :], wo_in[:, v % 2, :], ACT.Copy).then_inc(wh_d, 1)
                    if v == OUT0 and h:
                        copy_output(h - 1)
                if v == OUT0:
                    copy_output(TH - 1)
            high(NP - 2)
            copy_values(NU - 1)
            for t in range(TH):
                act.wait_ge(ont_d, t + 1)
                act.activation(ons[0][:, KD - 1, tile(t)], on[:, tile(t)], ACT.Copy).then_inc(oht_d, 1)
            for i in range(TH, TT):
                copy_output(i)

        @block.gpsimd
        def _(pool):
            def divide(p):
                pool.wait_ge(rden_d, HU * (p + 1))
                for i in range(2):
                    pool.wait_ge(packed[i], 16 * 2 * (p + 1))
                if p:
                    pool.wait_ge(ol_d, p)
                pool.tensor_tensor(on[:], num[:, p % 2, :], rden[:], ALU.mult).then_inc(on_d, 1)

            def low(p):
                pool.wait_ge(oh_d, p + 1)
                pool.tensor_tensor(ons[1][:, p % KD, :], on[:], ons[0][:, p % KD, :].bitcast(F32), ALU.subtract).then_inc(ol_d, 1)

            def divide_tile(t):
                pool.wait_ge(rden_d, HU * (NP - 1) + t + 1)
                if t == 0:
                    pool.wait_ge(ol_d, NP - 1)
                pool.tensor_tensor(on[:, tile(t)], num[:, (NP - 1) % 2, tile(t)], rden[:, tile(t)], ALU.mult).then_inc(ont_d, 1)

            def low_tile(t):
                pool.wait_ge(oht_d, t + 1)
                pool.tensor_tensor(ons[1][:, KD - 1, tile(t)], on[:, tile(t)], ons[0][:, KD - 1, tile(t)].bitcast(F32),
                                   ALU.subtract).then_inc(olt_d, 1)

            def maxima_parts(w):
                pool.wait_ge(np1_d, w + 1)
                if w:
                    pool.wait_ge(np2_d, w)
                pool.tensor_tensor(nr[:], nm[:], nparts[:, 0, :], ALU.subtract).then_inc(nr_d, 1)
                pool.wait_ge(np2_d, w + 1)
                pool.tensor_tensor(nparts[:, 2, :], nr[:], nparts[:, 1, :], ALU.subtract).then_inc(np3_d, 1)

            for i in range(SB):
                pool.memset(KS[i][KB:KR, :, :], 1.0).then_inc(rows_d, 1)
            maxima_parts(0)
            for v in range(NU):
                if v + 1 < NU:
                    maxima_parts(v + 1)
                if v < KD:
                    pool.wait_ge(wh_d, v + 1)
                    pool.tensor_tensor(wo[1][:, v, :], wo_in[:, v % 2, :], wo[0][:, v, :].bitcast(F32), ALU.subtract).then_inc(wl_d, 1)
                if v >= 4 and v % 2 == 0:
                    divide((v - 4) // 2)
                    low((v - 4) // 2)
            divide(NP - 2)
            low(NP - 2)
            for t in range(TH):
                divide_tile(t)
                if t:
                    low_tile(t - 1)
            low_tile(TH - 1)

        @block.vector
        def _(dve):
            def maxima(w, h):
                for i in range(TH):
                    n = (w * HU + h) * TH + i
                    dve.wait_ge(s1, n + 1)
                    if n >= 2:
                        dve.wait_ge(mx_d, n - 1)
                    if h == 0 and w >= 2:
                        dve.wait_ge(mt, w - 1)
                    c = (i + 1) * P
                    dve.tensor_tensor_reduce(junk[:, n % 2, 0:c], p1[:, n % 3, 0:c], mask[:, L - c:L], 1.0, NEG,
                                             ALU.add, ALU.max, mx[:, w % 2, i, h:h + 1]).then_inc(mx_d, 1)

            def invert(p, i):
                if i == 0:
                    for u in range(2):
                        dve.wait_ge(packed[u], 16 * 2 * (p + 1))
                    dve.wait_ge(on_d, p)
                c = slice(i * (L // HU), (i + 1) * (L // HU))
                dve.reciprocal(rden[:, c], den[:, p % 2, c]).then_inc(rden_d, 1)

            dve.wait_ge(ldc, 32)
            for h in range(HU):
                maxima(0, h)
            dve.tensor_copy(maskT[:], maskf[:]).then_inc(const_d, 1)
            dve.tensor_copy(identb[:], ident[:]).then_inc(const_d, 1)
            for h in range(HU):
                maxima(1, h)
            for v in range(NU):
                for h in range(HU):
                    if v + 2 < NU:
                        maxima(v + 2, h)
                    if v >= 3 and v % 2 and h:
                        invert((v - 3) // 2, h - 1)
                    if v >= 4 and v % 2 == 0 and h == 0:
                        invert((v - 4) // 2, HU - 1)
            invert(NP - 2, HU - 1)
            for i in range(HU):
                invert(NP - 1, i)


def adapter_phase(nc, w_ab, xT, g_ranks, s_acc, x_res, out):
    with ExitStack() as ctx:
        sb = lambda n, s, d=F32: ctx.enter_context(nc.sbuf_tensor(f"ad_{n}", s, d))
        sem = phase_semaphores(nc, ctx, "ad")
        two = lambda n, s: [sb(f"{n}{i}", s, F32R) for i in range(2)]
        KT = NA * RK // P
        WPI = 2 * KT
        RING, HR = 4, 4
        stage = sb("stage", [P, RING, DM])
        w = two("w", [P, WPI, DM])
        gb = sb("gb", [P, 2, L])
        hf = sb("hf", [P, HR, L])
        hs = two("hs", [P, KT, L])
        ga = sb("ga", [P, 2, DM])
        pr = sb("pr", [P, 2, DM])
        res = sb("res", [P, 2, DM])
        ph = ctx.enter_context(nc.psum_tensor("ad_ph", [P, 4, 512], F32))
        pf = ctx.enter_context(nc.psum_tensor("ad_pf", [P, 4, 512], F32))
        ld_w = [sem(f"ld_w{i}") for i in range(RING)]
        ld_g = [sem("ld_g0"), sem("ld_g1")]
        st = [sem("st0"), sem("st1")]
        wh_d, al_d, bl_d, hp, hg_d, hh_d, hl_d, fp, ga_d, pr_d, re_d = (
            sem(n) for n in ("wh_d", "al_d", "bl_d", "hp", "hg_d", "hh_d", "hl_d", "fp", "ga_d", "pr_d", "re_d"))
        block = ctx.enter_context(nc.Block())
        N = NB * KT
        TB = TT // NB
        PAIRS = (WPI - RING) // 2

        def wait_split(eng, i):
            if i < KT:
                eng.wait_ge(al_d, i + 1)
            else:
                eng.wait_ge(bl_d, i - KT + 1)

        @block.sync
        def _(sp):
            def piece(i):
                if i >= RING:
                    wait_split(sp, i - RING)
                sp.dma_start(stage[:, i % RING, :], w_ab[i]).then_inc(ld_w[i % RING], 16)

            def gates(n):
                b, i = n // KT, n % KT
                if n >= 2:
                    sp.wait_ge(hg_d, n - 1)
                sp.dma_start(gb[:, n % 2, :], g_ranks[i * P:(i + 1) * P, b * L:(b + 1) * L]).then_inc(ld_g[n % 2], 16)

            def store(i):
                sp.wait_ge(re_d, i + 1)
                sp.dma_start(out[i * P:(i + 1) * P, :], res[:, i % 2, :]).then_inc(st[i % 2], 16)

            piece(0)
            piece(1)
            gates(0)
            piece(2)
            piece(3)
            gates(1)
            for n in range(PAIRS):
                piece(RING + 2 * n)
                piece(RING + 2 * n + 1)
                gates(n + 2)
            for n in range(PAIRS + 2, KT + HR + 2):
                gates(n)
            for i in range(TB):
                store(i)
            for n in range(KT + HR + 2, N):
                gates(n)
            for i in range(TB, TT):
                store(i)
            for i in range(2):
                sp.wait_ge(st[i], 16 * TT // 2)

        @block.tensor
        def _(pe):
            def down(n):
                b, i = n // KT, n % KT
                if b == 0:
                    wait_split(pe, i)
                if n >= 4:
                    pe.wait_ge(hg_d, n - 3)
                for k in range(KD):
                    last = matmul3(pe, ph[:, n % 4, :], both(w, slice(None), i, slice(k * P, (k + 1) * P)),
                                   both(xT, slice(None), k, slice(b * L, (b + 1) * L)), k == 0, k == KD - 1)
                last.then_inc(hp, 1)

            def up(i):
                b = i // TB
                if i >= 4:
                    pe.wait_ge(ga_d, i - 3)
                for k in range(KT):
                    if i % TB == 0:
                        pe.wait_ge(hl_d, KT * b + k + 1)
                    if i == 0:
                        wait_split(pe, KT + k)
                    last = matmul3(pe, pf[:, i % 4, :], both(hs, slice(None), k, slice(i % TB * P, (i % TB + 1) * P)),
                                   both(w, slice(None), KT + k), k == 0, k == KT - 1)
                last.then_inc(fp, 1)

            for n in range(KT + HR):
                down(n)
            for i in range(TB):
                up(i)
            for n in range(KT + HR, N):
                down(n)
            for i in range(TB, TT):
                up(i)

        @block.scalar
        def _(act):
            def high(i):
                act.wait_ge(ld_w[i % RING], 16 * (i // RING + 1))
                act.activation(w[0][:, i, :], stage[:, i % RING, :], ACT.Copy).then_inc(wh_d, 1)

            def high_h(n):
                act.wait_ge(hg_d, n + 1)
                if n == KT:
                    act.wait_ge(fp, TB)
                act.activation(hs[0][:, n % KT, :], hf[:, n % HR, :], ACT.Copy).then_inc(hh_d, 1)

            def gate(i):
                act.wait_ge(fp, i + 1)
                if i >= 2:
                    act.wait_ge(pr_d, i - 1)
                act.activation(ga[:, i % 2, :], pf[:, i % 4, :], ACT.Silu, scale=2.0).then_inc(ga_d, 1)

            for i in range(RING):
                high(i)
            for n in range(KT):
                if n < PAIRS:
                    high(RING + 2 * n)
                    high(RING + 2 * n + 1)
                high_h(n)
            for i in range(TB):
                gate(i)
            for n in range(KT, N):
                high_h(n)
            for i in range(TB, TT):
                gate(i)

        @block.gpsimd
        def _(pool):
            def low(i):
                pool.wait_ge(wh_d, i + 1)
                pool.tensor_tensor(w[1][:, i, :], stage[:, i % RING, :], w[0][:, i, :].bitcast(F32), ALU.subtract).then_inc(al_d, 1)

            for i in range(RING):
                low(i)
            for n in range(N):
                if RING + 2 * n < KT:
                    low(RING + 2 * n)
                    low(RING + 2 * n + 1)
                pool.wait_ge(hh_d, n + 1)
                if n == KT:
                    pool.wait_ge(fp, TB)
                pool.tensor_tensor(hs[1][:, n % KT, :], hf[:, n % HR, :], hs[0][:, n % KT, :].bitcast(F32),
                                   ALU.subtract).then_inc(hl_d, 1)

        @block.vector
        def _(dve):
            def low(i):
                dve.wait_ge(wh_d, i + 1)
                dve.tensor_tensor(w[1][:, i, :], stage[:, i % RING, :], w[0][:, i, :].bitcast(F32), ALU.subtract).then_inc(bl_d, 1)

            def weigh(n):
                dve.wait_ge(ld_g[n % 2], 16 * (n // 2 + 1))
                dve.wait_ge(hp, n + 1)
                if n >= HR:
                    dve.wait_ge(hl_d, n - HR + 1)
                dve.tensor_tensor(hf[:, n % HR, :], ph[:, n % 4, :], gb[:, n % 2, :], ALU.mult).then_inc(hg_d, 1)

            def result(i):
                dve.wait_ge(ga_d, i + 1)
                if i >= 2:
                    dve.wait_ge(re_d, i - 1)
                dve.tensor_tensor(pr[:, i % 2, :], s_acc[:, i, :], ga[:, i % 2, :], ALU.mult).then_inc(pr_d, 1)
                dve.wait_ge(pr_d, i + 1)
                if i >= 2:
                    dve.wait_ge(st[i % 2], 16 * (i // 2))
                dve.tensor_tensor(res[:, i % 2, :], pr[:, i % 2, :], x_res[:, i, :], ALU.add).then_inc(re_d, 1)

            for n in range(KT + HR):
                weigh(n)
                i = RING + 2 * n
                if KT <= i < WPI:
                    low(i)
                    low(i + 1)
            for i in range(TB):
                result(i)
            for n in range(KT + HR, N):
                weigh(n)
            for i in range(TB, TT):
                result(i)


def build_program(nc, x, w_small, small_bias, a_log, iota16, ident_dram, w_pieces,
                  conv_par, d_par, n_par, w_gu, w_dn, w_q, w_k, w_v, w_o, rot, cos, sin, mask, maskT,
                  w_r, w_ab, out):
    scratch = lambda n, s, d=F32: nc.dram_tensor(n, s, d, kind="Internal").ap()
    daz_dram = scratch("daz_dram", (TT, H, P))
    din_dram = scratch("din_dram", (TT, H, P))
    comb_dram = scratch("comb_dram", (NE, T))
    q_stack = scratch("q_stack", (NB, KD, sum(RUNS), P, L), BF16)
    k_stack = scratch("k_stack", (NB, KD, sum(RUNS), P, L), BF16)
    g_dram = scratch("g_dram", (NA, T))
    g_ranks = scratch("g_ranks", (NA * RK, T))
    rows_dram = scratch("rows_dram", (2, P, L))
    with ExitStack() as ctx:
        sb = lambda n, s, d=F32: ctx.enter_context(nc.sbuf_tensor(n, s, d))
        ident = sb("ident", [P, P])
        xT = [sb(f"xT{i}", [P, KD, T], F32R) for i in range(2)]
        s_acc = sb("s_acc", [P, TT, DM])
        layernorm_phase(nc, x, xT, ident, None, "n0", ident_dram=ident_dram)
        with ExitStack() as layer:
            lb = lambda n, s, d=F32: layer.enter_context(nc.sbuf_tensor(n, s, d))
            dtT = lb("dtT", [P, TT, H])
            wx = [lb(f"wx{i}", [P, MC, KD, P], F32R) for i in range(2)]
            wg = [lb(f"wg{i}", [P, MG, KD, P], F32R) for i in range(2)]
            small_phase(nc, w_small, small_bias, a_log, iota16, w_pieces, xT, ident, wx, wg, dtT, daz_dram, din_dram, comb_dram)
            ssm_phase(nc, w_pieces, conv_par, d_par, n_par, xT, ident, wx, wg, dtT, daz_dram, din_dram, s_acc)
        x1 = sb("x1", [P, TT, DM])
        moe_phase(nc, w_gu, w_dn, comb_dram, xT, x1)
        with nc.sbuf_tensor("V1", [P, TT, HN, 2 * HD], F32) as V1:
            with nc.sbuf_tensor("wq0", [P, KD, DM], F32R) as wq0, nc.sbuf_tensor("wq1", [P, KD, DM], F32R) as wq1:
                layernorm_phase(nc, x, xT, ident, x1, "n1", s_acc, (w_q, wq0, wq1))
                qkv_phase(nc, (wq0, wq1), w_k, w_v, rot, cos, sin, w_r, xT, ident, V1, q_stack, k_stack, g_dram)
            attention_phase(nc, q_stack, k_stack, V1, w_o, mask, maskT, ident, s_acc, g_dram, g_ranks, rows_dram)
        adapter_phase(nc, w_ab, xT, g_ranks, s_acc, x1, out)


def layouts(d):
    a = {k: np.asarray(v) for k, v in d.items()}
    W = a["L0_attn_in_proj_w"]
    I, GN = H * PH, G * NS

    def kmajor(rows):
        return rows.reshape(-1, KD, P).transpose(2, 1, 0)

    def per_group(lo, n):
        return W[lo:lo + G * n].reshape(G, n, KD, P).transpose(0, 3, 2, 1)

    def tiles(w):
        return w.reshape(G, P, KD, -1, P).transpose(0, 3, 1, 2, 4).reshape(G, -1, P, DM)

    out_w = a["L0_attn_out_proj_w"].reshape(DM, G, MG, P).transpose(1, 2, 3, 0)
    pieces = [out_w, tiles(per_group(I, CG)), tiles(per_group(2 * I, NS)), tiles(per_group(2 * I + GN, NS)), tiles(per_group(0, CG))]
    conv = np.concatenate([a["L0_attn_conv_weight"], a["L0_attn_conv_bias"][:, None]], 1)
    cx = conv[:I].reshape(G, MG, P, KC + 1)
    cB = conv[I:I + GN].reshape(G, 1, P, KC + 1)
    cC = conv[I + GN:].reshape(G, 1, P, KC + 1)
    shared = a["L0_ffn_shared_w_gate_up"].reshape(2, 4, P, DM).transpose(1, 0, 2, 3).reshape(4, 2 * P, DM)
    gu = np.concatenate([a["L0_ffn_w_gate_up"], shared], 0)
    shared_dn = a["L0_ffn_shared_w_down"].reshape(DM, 4, P).transpose(1, 2, 0)
    dn = np.concatenate([a["L0_ffn_w_down"].transpose(0, 2, 1), shared_dn], 0)
    theta = (1.0 / np.float32(10000.0) ** (np.arange(0, HD, 2, dtype=np.float32) / np.float32(HD))).astype(np.float32)
    angle = np.outer(np.arange(L, dtype=np.float32), theta).astype(np.float32)
    HPT = P // HD
    angle = np.repeat(np.concatenate([angle, angle], 1).T, HPT, 0)
    R = np.zeros((HD, HD), np.float32)
    for i in range(HD // 2):
        R[i + HD // 2, i] = -1.0
        R[i, i + HD // 2] = 1.0
    R = np.kron(R, np.eye(HPT, dtype=np.float32))

    def by_place(w):
        return w.reshape(KD, HPT, HD, DM).transpose(0, 2, 1, 3).reshape(DM, DM)

    mask = np.zeros((P, L), np.float32)
    mask[:, L - P:] = np.where(np.arange(P)[None, :] > np.arange(P)[:, None], np.float32(-1e30), np.float32(0))
    maskT = np.where(np.arange(P)[:, None] > np.arange(P)[None, :], np.float32(-1e30), np.float32(0))
    arr = {
        "x": a["L0_attn_hidden_states"].reshape(T, DM),
        "w_small": kmajor(np.concatenate([W[-H:], W[-H:], a["L0_ffn_gate_w"]], 0)),
        "small_bias": np.tile(a["L0_attn_dt_bias"][:, None], (NB, 1)),
        "a_log": np.tile(a["L0_attn_A_log"][:, None], (NB, 1)),
        "iota16": np.tile(np.arange(16, dtype=np.float32), (P, 1)),
        "ident_dram": np.eye(P, dtype=np.float32),
        "w_pieces": np.concatenate(pieces, 1).reshape(G * NPI, P, DM),
        "conv_par": np.concatenate([cx, cB, cC], 1).transpose(0, 2, 1, 3).reshape(G, P, -1),
        "d_par": np.repeat(a["L0_attn_D"], PH).reshape(G, MG, P).transpose(0, 2, 1),
        "n_par": a["L0_attn_norm_weight"].reshape(G, MG, P).transpose(0, 2, 1),
        "w_gu": gu.reshape(NE, 2 * P, KD, P).transpose(0, 3, 2, 1).reshape(NE, P, -1),
        "w_dn": dn,
        "w_q": kmajor(by_place(a["L1_attn_wq"])).reshape(P, -1),
        "w_k": kmajor(by_place(a["L1_attn_wk"])).reshape(P, -1),
        "w_v": kmajor(a["L1_attn_wv"]).reshape(P, -1),
        "w_o": kmajor(a["L1_attn_wo"]).reshape(P, -1),
        "rot": R,
        "cos": np.cos(angle).astype(np.float32),
        "sin": np.sin(angle).astype(np.float32),
        "mask": mask,
        "maskT": maskT,
        "w_r": kmajor(a["L1_ffn_Wr"]).reshape(P, -1),
        "w_ab": np.concatenate([kmajor(a["L1_ffn_A"].reshape(-1, DM)).reshape(P, KD, 8, P).transpose(2, 0, 1, 3).reshape(8, P, DM),
                                a["L1_ffn_B"].transpose(0, 2, 1).reshape(8, P, DM)], 0),
    }
    return {k: np.ascontiguousarray(v) for k, v in arr.items()}


def kernel(**inputs):
    import concourse.bacc as bacc
    from concourse.bass_utils import run_bass_kernel_spmd

    nc = bacc.Bacc("TRN2", target_bir_lowering=False, num_devices=1, dynamic_dma_scratch_size=1024)
    arrays = layouts(inputs)
    args = [nc.dram_tensor(k, v.shape, mybir.dt.from_np(v.dtype), kind="ExternalInput").ap() for k, v in arrays.items()]
    args.append(nc.dram_tensor("out", (T, DM), F32, kind="ExternalOutput").ap())
    build_program(nc, *args)
    r = run_bass_kernel_spmd(nc, [arrays], core_ids=[0])
    return r.results[0]["out"].reshape(NB, L, DM)
```
